# Optimizing a Trainium2 kernel written in Bass

```python
import numpy as np
import jax
import jax.numpy as jnp

def _softmax(x, axis=-1):
    return jax.nn.softmax(x, axis=axis)

def _gelu(x):
    return jax.nn.gelu(x, approximate=True)

def _silu(x):
    return jax.nn.silu(x)

def _sigmoid(x):
    return jax.nn.sigmoid(x)

def _layernorm(x, axis=-1, eps=1e-05):
    m = jnp.mean(x, axis=axis, keepdims=True)
    v = jnp.var(x, axis=axis, keepdims=True)
    return (x - m) / jnp.sqrt(v + eps)

def _scatter_add(tgt, idx, src, axis=0):
    return tgt.at[idx].add(src)

def _segment_sum(src, seg, n):
    return jax.ops.segment_sum(src, seg, n)
kernel_name = 'mk_gnn_resnorm_d4_gnn_r64_2c7f60'

def setup_inputs(seed: int=0):
    np.random.seed(seed)
    _w = jnp.asarray

    def _rec_inputs():
        import jax
        import jax.numpy as jnp
        _gk = jax.random.key(seed)
        x = -0.000202 + 1 * jax.random.normal(jax.random.fold_in(_gk, 1), (100000, 64), jnp.float32)
        src = jax.random.randint(jax.random.fold_in(_gk, 2), (50000,), 0, 100000, jnp.int32)
        dst = jax.random.randint(jax.random.fold_in(_gk, 3), (50000,), 0, 100000, jnp.int32)
        _o = jnp.argsort(dst, stable=True)
        src = src[_o]
        dst = dst[_o]
        edge_attr_48 = 5.93493e-05 + 1.00006 * jax.random.normal(jax.random.fold_in(_gk, 13), (50000, 48), jnp.float32)
        edge_weight = jax.random.uniform(jax.random.fold_in(_gk, 15), (50000,), jnp.float32, 0.0, 1)
        return (x, src, dst, edge_attr_48, edge_weight)
    x, src, dst, edge_attr_48, edge_weight = _rec_inputs()

    def _L0_gnn_setup():
        import jax, jax.numpy as jnp
        import numpy as np
        N = 100000
        E = 50000
        D = 64
        K = 10
        ALPHA = 0.1
        key = jax.random.key(seed)
        k1, k2, k3, k4 = jax.random.split(key, 4)
        feat = jax.random.normal(k1, (N, D), dtype=jnp.float32)
        src = jax.random.randint(k2, (E,), 0, N, dtype=jnp.int32)
        dst = jax.random.randint(k3, (E,), 0, N, dtype=jnp.int32)
        edge_weight = jax.random.uniform(k4, (E,), dtype=jnp.float32)
        return {'feat': feat, 'edge_weight': edge_weight, 'src': src, 'dst': dst}
    _L0_gnn_all = _L0_gnn_setup()
    _L0_gnn_in = {k: v for k, v in _L0_gnn_all.items() if k in ()}
    del _L0_gnn_all

    def _L1_gnn_setup():
        import jax, jax.numpy as jnp
        import numpy as np
        from functools import partial
        N_NODES = 50000
        N_EDGES = 12500
        IN_F = 64
        OUT_F = 64
        key = jax.random.key(seed)
        k1, k2, k3, k4, k5 = jax.random.split(key, 5)
        stdv = 1.0 / np.sqrt(OUT_F)
        x = jax.random.normal(k1, (N_NODES, IN_F), dtype=jnp.float32)
        edge_index = jax.random.randint(k2, (2, N_EDGES), 0, N_NODES, dtype=jnp.int64)
        edge_weight = jax.random.uniform(k3, (N_EDGES,), dtype=jnp.float32)
        weight = jax.random.uniform(k4, (IN_F, OUT_F), minval=-stdv, maxval=stdv, dtype=jnp.float32)
        bias = jax.random.uniform(k5, (OUT_F,), minval=-stdv, maxval=stdv, dtype=jnp.float32)
        return {'x': x, 'edge_index': edge_index, 'edge_weight': edge_weight, 'weight': weight, 'bias': bias}
    _L1_gnn_all = _L1_gnn_setup()
    _L1_gnn_in = {k: v for k, v in _L1_gnn_all.items() if k in ('weight', 'bias')}
    del _L1_gnn_all

    def _L2_gnn_setup():
        import jax, jax.numpy as jnp
        import numpy as np
        N_NODES = 100000
        N_EDGES = 25000
        EMBED = 64
        HEADS = 8
        HEAD_DIM = EMBED // HEADS
        FFN = 4 * EMBED
        EPS = 1e-05

        def _layer_norm(x, g, b):
            m = jnp.mean(x, axis=-1, keepdims=True)
            v = jnp.mean(jnp.square(x - m), axis=-1, keepdims=True)
            return (x - m) * jax.lax.rsqrt(v + EPS) * g + b

        def _self_attention(x, edge_indices, attn_w, attn_b):
            n = x.shape[0]
            row, col = (edge_indices[0], edge_indices[1])
            scale = EMBED ** (-0.5)
            qkv = (x @ attn_w + attn_b).reshape(n, HEADS, 3 * HEAD_DIM)
            q, k, v = jnp.split(qkv, 3, axis=2)
            alpha = jnp.sum(q[row] * k[col], axis=2) * scale
            m = jax.ops.segment_max(alpha, row, num_segments=n)
            e = jnp.exp(alpha - m[row])
            denom = jax.ops.segment_sum(e, row, num_segments=n)
            weights = e / denom[row]
            vals = v[col] * weights[:, :, None]
            out = jax.ops.segment_sum(vals, row, num_segments=n)
            return out.reshape(n, EMBED)
        key = jax.random.key(seed)
        ks = jax.random.split(key, 10)
        s = lambda fan_in: 1.0 / np.sqrt(fan_in)
        x = jax.random.normal(ks[0], (N_NODES, EMBED), dtype=jnp.float32)
        edge_indices = jax.random.randint(ks[1], (2, N_EDGES), 0, N_NODES, dtype=jnp.int64)
        attn_w = jax.random.uniform(ks[2], (EMBED, 3 * EMBED), jnp.float32, -s(EMBED), s(EMBED))
        attn_b = jnp.zeros((3 * EMBED,), jnp.float32)
        w1 = jax.random.uniform(ks[3], (EMBED, FFN), jnp.float32, -s(EMBED), s(EMBED))
        b1 = jnp.zeros((FFN,), jnp.float32)
        w2 = jax.random.uniform(ks[4], (FFN, EMBED), jnp.float32, -s(FFN), s(FFN))
        b2 = jnp.zeros((EMBED,), jnp.float32)
        ln1_g = jnp.ones((EMBED,), jnp.float32)
        ln1_b = jnp.zeros((EMBED,), jnp.float32)
        ln2_g = jnp.ones((EMBED,), jnp.float32)
        ln2_b = jnp.zeros((EMBED,), jnp.float32)
        return {'x': x, 'edge_indices': edge_indices, 'attn_w': attn_w, 'attn_b': attn_b, 'w1': w1, 'b1': b1, 'w2': w2, 'b2': b2, 'ln1_g': ln1_g, 'ln1_b': ln1_b, 'ln2_g': ln2_g, 'ln2_b': ln2_b}
    _L2_gnn_all = _L2_gnn_setup()
    _L2_gnn_in = {k: v for k, v in _L2_gnn_all.items() if k in ('attn_w', 'attn_b', 'w1', 'b1', 'w2', 'b2', 'ln1_g', 'ln1_b', 'ln2_g', 'ln2_b')}
    del _L2_gnn_all

    def _L3_gnn_setup():
        import jax, jax.numpy as jnp
        import numpy as np
        N_NODES = 100000
        N_EDGES = 25000
        NODE_D = 64
        EDGE_D = 48
        U_D = 32
        N_GRAPHS = 64
        HIDDEN = 128
        OUT_D = 64
        IN_D = NODE_D + EDGE_D + U_D
        key = jax.random.key(seed)
        ks = jax.random.split(key, 10)
        x = jax.random.normal(ks[0], (N_NODES, NODE_D), dtype=jnp.float32)
        edge_index = jax.random.randint(ks[1], (2, N_EDGES), 0, N_NODES, dtype=jnp.int64)
        edge_attr = jax.random.normal(ks[2], (N_EDGES, EDGE_D), dtype=jnp.float32)
        u = jax.random.normal(ks[3], (N_GRAPHS, U_D), dtype=jnp.float32)
        batch = jnp.sort(jax.random.randint(ks[4], (N_NODES,), 0, N_GRAPHS, dtype=jnp.int64))
        W1 = jax.random.normal(ks[5], (IN_D, HIDDEN), dtype=jnp.float32) / np.sqrt(IN_D)
        b1 = jnp.zeros((HIDDEN,), dtype=jnp.float32)
        W2 = jax.random.normal(ks[6], (HIDDEN, HIDDEN), dtype=jnp.float32) / np.sqrt(HIDDEN)
        b2 = jnp.zeros((HIDDEN,), dtype=jnp.float32)
        W3 = jax.random.normal(ks[7], (HIDDEN, OUT_D), dtype=jnp.float32) / np.sqrt(HIDDEN)
        b3 = jnp.zeros((OUT_D,), dtype=jnp.float32)
        return {'x': x, 'edge_index': edge_index, 'edge_attr': edge_attr, 'u': u, 'batch': batch, 'W1': W1, 'b1': b1, 'W2': W2, 'b2': b2, 'W3': W3, 'b3': b3}
    _L3_gnn_all = _L3_gnn_setup()
    _L3_gnn_in = {k: v for k, v in _L3_gnn_all.items() if k in ('u', 'W1', 'b1', 'W2', 'b2', 'W3', 'b3')}
    del _L3_gnn_all
    return {'x': x, 'src': src, 'dst': dst, 'edge_attr_48': edge_attr_48, 'edge_weight': edge_weight, 'L1_gnn_weight': _L1_gnn_in['weight'], 'L1_gnn_bias': _L1_gnn_in['bias'], 'L2_gnn_attn_w': _L2_gnn_in['attn_w'], 'L2_gnn_attn_b': _L2_gnn_in['attn_b'], 'L2_gnn_w1': _L2_gnn_in['w1'], 'L2_gnn_b1': _L2_gnn_in['b1'], 'L2_gnn_w2': _L2_gnn_in['w2'], 'L2_gnn_b2': _L2_gnn_in['b2'], 'L2_gnn_ln1_g': _L2_gnn_in['ln1_g'], 'L2_gnn_ln1_b': _L2_gnn_in['ln1_b'], 'L2_gnn_ln2_g': _L2_gnn_in['ln2_g'], 'L2_gnn_ln2_b': _L2_gnn_in['ln2_b'], 'L3_gnn_u': _L3_gnn_in['u'], 'L3_gnn_W1': _L3_gnn_in['W1'], 'L3_gnn_b1': _L3_gnn_in['b1'], 'L3_gnn_W2': _L3_gnn_in['W2'], 'L3_gnn_b2': _L3_gnn_in['b2'], 'L3_gnn_W3': _L3_gnn_in['W3'], 'L3_gnn_b3': _L3_gnn_in['b3']}

def reference(x, src, dst, edge_attr_48, edge_weight, L1_gnn_weight, L1_gnn_bias, L2_gnn_attn_w, L2_gnn_attn_b, L2_gnn_w1, L2_gnn_b1, L2_gnn_w2, L2_gnn_b2, L2_gnn_ln1_g, L2_gnn_ln1_b, L2_gnn_ln2_g, L2_gnn_ln2_b, L3_gnn_u, L3_gnn_W1, L3_gnn_b1, L3_gnn_W2, L3_gnn_b2, L3_gnn_W3, L3_gnn_b3):
    import jax
    import jax.numpy as jnp

    def _L0_gnn_ref(feat, edge_weight, src, dst):
        import jax, jax.numpy as jnp
        import numpy as np
        N = 100000
        E = 50000
        D = 64
        K = 10
        ALPHA = 0.1
        n = feat.shape[0]
        loop = jnp.arange(n, dtype=src.dtype)
        s = jnp.concatenate([src, loop])
        d = jnp.concatenate([dst, loop])
        w = jnp.concatenate([edge_weight, jnp.ones((n,), feat.dtype)])
        deg_out = jax.ops.segment_sum(w, s, num_segments=n)
        deg_in = jax.ops.segment_sum(w, d, num_segments=n)
        inv_sqrt_out = jnp.where(deg_out > 0, jax.lax.rsqrt(deg_out), 0.0)
        inv_sqrt_in = jnp.where(deg_in > 0, jax.lax.rsqrt(deg_in), 0.0)
        wn = w * inv_sqrt_out[s] * inv_sqrt_in[d]
        feat_0 = feat

        def step(h, _):
            agg = jax.ops.segment_sum(h[s] * wn[:, None], d, num_segments=n)
            return ((1.0 - ALPHA) * agg + ALPHA * feat_0, None)
        h, _ = jax.lax.scan(step, feat, None, length=K)
        return h

    def _L1_gnn_ref(x, edge_index, edge_weight, weight, bias):
        import jax, jax.numpy as jnp
        import numpy as np
        from functools import partial
        N_NODES = 50000
        N_EDGES = 12500
        IN_F = 64
        OUT_F = 64
        num_nodes = x.shape[0]
        support = x @ weight
        row, col = (edge_index[0], edge_index[1])
        deg = jax.ops.segment_sum(jnp.ones_like(row, dtype=jnp.float32), row, num_segments=num_nodes)
        deg_inv_sqrt = jnp.where(deg > 0, jax.lax.rsqrt(jnp.maximum(deg, 1.0)), 0.0)
        norm = deg_inv_sqrt[row] * edge_weight * deg_inv_sqrt[col]
        msgs = norm[:, None] * support[col]
        output = jax.ops.segment_sum(msgs, row, num_segments=num_nodes)
        return output + bias

    def _L2_gnn_ref(x, edge_indices, attn_w, attn_b, w1, b1, w2, b2, ln1_g, ln1_b, ln2_g, ln2_b):
        import jax, jax.numpy as jnp
        import numpy as np
        N_NODES = 100000
        N_EDGES = 25000
        EMBED = 64
        HEADS = 8
        HEAD_DIM = EMBED // HEADS
        FFN = 4 * EMBED
        EPS = 1e-05

        def _layer_norm(x, g, b):
            m = jnp.mean(x, axis=-1, keepdims=True)
            v = jnp.mean(jnp.square(x - m), axis=-1, keepdims=True)
            return (x - m) * jax.lax.rsqrt(v + EPS) * g + b

        def _self_attention(x, edge_indices, attn_w, attn_b):
            n = x.shape[0]
            row, col = (edge_indices[0], edge_indices[1])
            scale = EMBED ** (-0.5)
            qkv = (x @ attn_w + attn_b).reshape(n, HEADS, 3 * HEAD_DIM)
            q, k, v = jnp.split(qkv, 3, axis=2)
            alpha = jnp.sum(q[row] * k[col], axis=2) * scale
            m = jax.ops.segment_max(alpha, row, num_segments=n)
            e = jnp.exp(alpha - m[row])
            denom = jax.ops.segment_sum(e, row, num_segments=n)
            weights = e / denom[row]
            vals = v[col] * weights[:, :, None]
            out = jax.ops.segment_sum(vals, row, num_segments=n)
            return out.reshape(n, EMBED)
        x = _layer_norm(x + _self_attention(x, edge_indices, attn_w, attn_b), ln1_g, ln1_b)
        ffn = jax.nn.relu(x @ w1 + b1) @ w2 + b2
        x = _layer_norm(x + ffn, ln2_g, ln2_b)
        return x

    def _L3_gnn_ref(x, edge_index, edge_attr, u, batch, W1, b1, W2, b2, W3, b3):
        import jax, jax.numpy as jnp
        import numpy as np
        N_NODES = 100000
        N_EDGES = 25000
        NODE_D = 64
        EDGE_D = 48
        U_D = 32
        N_GRAPHS = 64
        HIDDEN = 128
        OUT_D = 64
        IN_D = NODE_D + EDGE_D + U_D
        n = x.shape[0]
        seg = edge_index[0]
        sums = jax.ops.segment_sum(edge_attr, seg, num_segments=n)
        cnt = jax.ops.segment_sum(jnp.ones((edge_attr.shape[0],), edge_attr.dtype), seg, num_segments=n)
        v_e = sums / jnp.maximum(cnt, 1.0)[:, None]
        comb = jnp.concatenate([x, v_e, u[batch]], axis=1)
        h = jax.nn.relu(comb @ W1 + b1)
        h = jax.nn.relu(h @ W2 + b2)
        return h @ W3 + b3
    edge_index = jnp.stack([src, dst])
    batch0 = jnp.zeros((100000,), jnp.int32)
    x = _layernorm(x + _L0_gnn_ref(x, edge_weight, src, dst), axis=-1)
    x = _layernorm(x + _L1_gnn_ref(x, edge_index, edge_weight, L1_gnn_weight, L1_gnn_bias), axis=-1)
    x = _layernorm(x + _L2_gnn_ref(x, edge_index, L2_gnn_attn_w, L2_gnn_attn_b, L2_gnn_w1, L2_gnn_b1, L2_gnn_w2, L2_gnn_b2, L2_gnn_ln1_g, L2_gnn_ln1_b, L2_gnn_ln2_g, L2_gnn_ln2_b), axis=-1)
    x = _layernorm(x + _L3_gnn_ref(x, edge_index, edge_attr_48, L3_gnn_u, batch0, L3_gnn_W1, L3_gnn_b1, L3_gnn_W2, L3_gnn_b2, L3_gnn_W3, L3_gnn_b3), axis=-1)
    return x

_drawn_inputs = setup_inputs


def setup_inputs(seed=0):
    import zlib

    import numpy as np

    out = dict(_drawn_inputs(seed))
    spreads = {'L2_gnn_attn_b': (0.0, 0.268),
     'L2_gnn_b1': (0.0, 0.477),
     'L2_gnn_b2': (0.0, 0.1),
     'L2_gnn_ln1_g': (1.0, 0.2),
     'L2_gnn_ln1_b': (0.0, 0.1),
     'L2_gnn_ln2_g': (1.0, 0.2),
     'L2_gnn_ln2_b': (0.0, 0.1),
     'L3_gnn_b1': (0.0, 0.1),
     'L3_gnn_b2': (0.0, 0.1),
     'L3_gnn_b3': (0.0, 0.1)}
    factors = {}
    for name, (base, spread) in spreads.items():
        noise = np.random.default_rng([zlib.crc32(name.encode()), seed]).standard_normal(out[name].shape)
        drawn = base * np.exp(spread * noise) if base else spread * noise
        out[name] = jnp.asarray(drawn.astype(out[name].dtype))
    for name, factor in factors.items():
        out[name] = (out[name] * factor).astype(out[name].dtype)
    return out
```

```python
import concourse.bass as bass
from concourse import mybir
from concourse.alu_op_type import AluOpType as ALU
from contextlib import ExitStack, contextmanager

F32, I32, F16, BF16 = mybir.dt.float32, mybir.dt.int32, mybir.dt.float16, mybir.dt.bfloat16
ACT = mybir.ActivationFunctionType
AX = mybir.AxisListType

P = 128
D = 64
ED = 48
N, E = 100000, 50000
HEADS, HD = 8, 8
FFN, HID, UD = 256, 128, 32
K_STEPS = 10
EPS = 1e-5
CH = 28
T = -(-E // (P * 2 * CH)) * 2 * CH
NPAIR = T // (2 * CH)
EP = P * T
G = 8
NPP = -(-N // (P * 2 * G)) * 2 * G
NR = P * NPP
NLAST = N - (P - 1) * NPP
PAIRS_FULL = NLAST // (2 * G)
PAIRS = NPP // (2 * G)
SKIP = 1 << 20
ZROW = EP
TR = EP + P
LOBITS = 9
NB_LO, NB_HI = 1 << LOBITS, (N >> LOBITS) + 1
XW = D + 4
AW = D + ED
QW = D + HEADS
RING = 7
DH, DL = 16, 32
DC = P // DH
ZW = NPP * 8


class Steps:

    def __init__(self, eng, sem):
        self.eng, self.sem, self.base, self.n = eng, sem, 0, 0

    def enter(self, i, per):
        self.outer, self.start, self.per, self.n = (self.base, self.n), self.n, per, 0
        self.base = self.base + self.start + i * per

    def leave(self, turns):
        assert self.n == self.per, f"{self.n} steps in a turn, not {self.per}"
        self.base, self.n = self.outer[0], self.outer[1] + turns * self.per

    def mark(self, ins):
        ins.then_inc(self.sem, 1)
        self.n += 1

    def did(self, ins):
        self.mark(ins)
        self.wait()

    def wait(self):
        self.eng.wait_ge(self.sem, self.base + self.n)


def spread(ap, axis, count):
    v = ap.unsqueeze(axis)
    shape = list(v.shape)
    shape[axis] = count
    return v.to_broadcast(shape)


def halves(eng, sem, tile_of, dram_of, store):
    for a, b in ((0, P - P // 8), (P - P // 8, P - 1)):
        if store:
            eng.dma_start(dram_of(a, b), tile_of(a, b)).then_inc(sem, 16)
        else:
            eng.dma_start(tile_of(a, b), dram_of(a, b)).then_inc(sem, 16)


class Net:

    def __init__(self, nc, ctx):
        self.nc, self.ctx = nc, ctx

    own = None

    def sem(self, name):
        if self.own is None:
            return self.ctx.enter_context(self.nc.semaphore(name))
        self.own.append(self.nc.alloc_semaphore(name=name))
        return self.own[-1]

    @contextmanager
    def phase(self):
        self.own = []
        with ExitStack() as c:
            yield c
        self.nc.clear_and_free_semaphores(self.own)
        self.nc.all_engine_barrier()
        self.own = None

    def dram(self, name, shape, dt=F32):
        return self.nc.dram_tensor(name, shape, dt, kind=self.kinds.get(name, "Internal")).ap()

    kinds = {}


def tile(nc, ctx, name, shape, dt=F32):
    return ctx.enter_context(nc.sbuf_tensor(name, shape, dt))


def bank(nc, ctx, name, shape, dt=F32):
    return ctx.enter_context(nc.psum_tensor(name, shape, dt))



def constants(net, c):
    nc = net.nc
    net.ident = tile(nc, c, "ident", [P, P])
    net.upper = tile(nc, c, "upper", [P, P])
    net.ones = tile(nc, c, "ones", [P, P])
    net.part = tile(nc, c, "part", [P, 1])
    net.minus = tile(nc, c, "minus", [1, 4], I32)
    net.iota16 = tile(nc, c, "iota16", [P, NB_LO], F16)
    net.zero16, net.ones16, net.upper16, net.lower16 = (
        tile(nc, c, n, [P, P], F16) for n in ("zero16", "ones16", "upper16", "lower16"))
    net.zero_tile, net.zeroed = net.sem("zero_tile"), net.sem("zeroed")


def setup_phase(net, src, dst, edge_weight):
    nc = net.nc
    with net.phase() as c:
        s_in = tile(nc, c, "su_src", [P, T], I32)
        d_in = tile(nc, c, "su_dst", [P, T], I32)
        w_in = tile(nc, c, "su_w", [P, T])
        e_no = tile(nc, c, "su_no", [P, T], I32)
        rec = tile(nc, c, "su_rec", [P, T, 4], I32)
        iota_lo = tile(nc, c, "su_iota", [P, NB_LO])
        padded, loaded, made, const, stored, drawn = (
            net.sem("su_" + n) for n in ("padded", "loaded", "made", "const", "stored", "drawn"))
        block = c.enter_context(nc.Block())

        @block.gpsimd
        def _(pool):
            pool.iota(e_no[:], pattern=[[1, T]], base=0, channel_multiplier=T).then_inc(const, 1)
            pool.iota(iota_lo[:], pattern=[[1, NB_LO]], base=0, channel_multiplier=0,
                      allow_small_or_imprecise_dtypes=True).then_inc(const, 1)
            pool.iota(net.part[:], pattern=[[0, 1]], base=0, channel_multiplier=1,
                      allow_small_or_imprecise_dtypes=True).then_inc(const, 1)
            pool.memset(net.ones[:], 1.0).then_inc(const, 1)
            pool.wait_ge(const, 4)
            pool.affine_select(out=net.ident[:], in_=net.ones[:], compare_op=ALU.is_equal, fill=0.0,
                               base=0, pattern=[[-1, P]], channel_multiplier=1).then_inc(const, 1)
            pool.affine_select(out=net.upper[:], in_=net.ones[:], compare_op=ALU.is_gt, fill=0.0,
                               base=0, pattern=[[1, P]], channel_multiplier=-1).then_inc(const, 1)

        @block.vector
        def _(dve):
            dve.memset(s_in[:], N)
            dve.memset(d_in[:], N)
            dve.memset(w_in[:], 0.0).then_inc(padded, 1)
            dve.memset(net.minus[:], -1)
            dve.memset(net.zeros[:], 0.0).then_inc(net.zero_tile, 1)
            dve.memset(net.zero16[:], 0.0)
            dve.memset(net.ones16[:], 1.0)
            dve.wait_ge(const, 6)
            dve.tensor_copy(net.iota16[:], iota_lo[:])
            dve.tensor_copy(net.upper16[:], net.upper[:])
            dve.tensor_scalar(net.lower16[:], net.upper[:], -1.0, 1.0, ALU.mult, ALU.add)
            dve.tensor_copy(rec[:, :, 3], e_no[:])
            dve.wait_ge(loaded, 9 * 16)
            dve.tensor_copy(rec[:, :, 0], s_in[:])
            dve.tensor_copy(rec[:, :, 1], d_in[:])
            dve.tensor_copy(rec[:, :, 2].bitcast(F32), w_in[:]).then_inc(made, 1)

        @block.sync
        def _(sp):
            sp.wait_ge(padded, 1)
            whole = (P - 1) * T
            for ap, to in ((src, s_in), (dst, d_in), (edge_weight, w_in)):
                rows = ap[0:whole].rearrange("(p t) -> p t", t=T)
                halves(sp, loaded, lambda a, b: to[a:b, :], lambda a, b: rows[a:b, :], False)
                sp.dma_start(to[P - 1:P, 0:E - whole],
                             ap[whole:E].rearrange("(p t) -> p t", p=1)).then_inc(loaded, 16)
            sp.wait_ge(made, 1)
            sp.dma_start(net.records[:, :].rearrange("(p t) c -> p t c", p=P), rec[:]).then_inc(stored, 16)
            sp.wait_ge(stored, 16)

        @block.scalar
        def _(act):
            act.wait_ge(net.zero_tile, 1)
            for table in net.orders:
                for row in (0, EP + 1):
                    act.dma_start(table[row:row + 1, :], net.minus[0:1, :]).then_inc(drawn, 16)
            act.wait_ge(drawn, 4 * 16)



def zero_parts(net):
    parts = []
    for table, w in ((net.by_dst, 2), (net.by_src, 2), (net.node_r, D), (net.agg, AW), (net.att, QW)):
        flat = table[:, :].rearrange("(p g) c -> p (g c)", p=P)
        for a in range(0, NPP * w, ZW):
            b = min(a + ZW, NPP * w)
            parts.append((flat[:, a:b], b - a))
    for k in range(2):
        parts.append((net.slots[k][EP:TR, :].rearrange("(p z) c -> p (z c)", p=P), D))
    net.zeroed_all = 16 * len(parts)
    return parts


def sort_pass(net, name, source, dest, key, high, zero):
    nc = net.nc
    nb = NB_HI if high else NB_LO
    with net.phase() as c:
        rec = tile(nc, c, name + "rec", [P, T, 4], I32)
        digit = tile(nc, c, name + "digit", [P, T], I32)
        digitf = tile(nc, c, name + "digitf", [P, T + 2])
        part = [tile(nc, c, name + f"part{k}", [P, T], I32) for k in range(2)]
        partf = [tile(nc, c, name + f"partf{k}", [P, T], F16) for k in range(2)]
        hot_up, hot_low = tile(nc, c, name + "hot_up", [P, T, DH], F16), tile(nc, c, name + "hot_low", [P, T, DL], F16)
        upto, before = tile(nc, c, name + "upto", [DH, DL]), tile(nc, c, name + "before", [DH, DL])
        rows_before = tile(nc, c, name + "rows_before", [DH, DH])
        base, base2 = tile(nc, c, name + "base", [DH, DH, DL]), tile(nc, c, name + "base2", [DH, DH, DL])
        same, fold = tile(nc, c, name + "same", [P, DC]), tile(nc, c, name + "fold", [P, DH])
        own_part, by_row = tile(nc, c, name + "own_part", [P, DC, DL]), tile(nc, c, name + "by_row", [P, DL])
        cross = bank(nc, c, name + "cross", [P, DC, DL])
        counts = bank(nc, c, name + "counts", [DH, DL])
        hot = [tile(nc, c, name + f"hot{r}", [P, nb], F16) for r in range(RING)]
        junk = [tile(nc, c, name + f"junk{r}", [P, nb]) for r in range(2)]
        rank = [tile(nc, c, name + f"rank{j}", [P, CH]) for j in range(2)]
        ranki = [tile(nc, c, name + f"ranki{j}", [P, CH], I32) for j in range(2)]
        low = [tile(nc, c, name + f"low{j}", [P, CH], I32) for j in range(2)]
        row = [tile(nc, c, name + f"row{j}", [P, CH], I32) for j in range(2)]
        stage = [tile(nc, c, name + f"stage{j}", [P, CH, 4], I32) for j in range(2)]
        acc = [bank(nc, c, name + f"acc{b}", [P, 512]) for b in range(2)]
        loaded, own, parts_ready, crossed, folding, counted, base_ready, hot_ready, ranked, read, started = (
            net.sem(name + n) for n in ("loaded", "own", "parts_ready", "crossed", "folding", "counted",
                                        "base_ready", "hot_ready", "ranked", "read", "started"))
        rows_ready = [net.sem(name + f"rows{j}") for j in range(2)]
        staged = [net.sem(name + f"staged{j}") for j in range(2)]
        sent = [net.sem(name + f"sent{j}") for j in range(2)]
        block = c.enter_context(nc.Block())
        records = source.rearrange("(p t) c -> p t c", p=P)
        COUNTED = 7

        @block.scalar
        def _(act):
            act.wait_ge(loaded, 16)
            for table, width in zero:
                act.dma_start(table, net.zeros[:, 0:width]).then_inc(net.zeroed, 16)

        @block.sync
        def _(sp):
            sp.dma_start(rec[:], records).then_inc(loaded, 16)
            with sp.Fori(0, NPAIR) as i:
                for j in range(2):
                    sp.wait_ge(sent[j], i * (16 * CH))
                    sp.dma_start(stage[j][:], records[:, bass.ds(i * (2 * CH) + j * CH, CH), :]).then_inc(staged[j], 16)

        @block.vector
        def _(dve):
            st = Steps(dve, own)
            for t in (RING - 2, RING - 1):
                dve.memset(hot[t][:], 0.0)
            dve.memset(digitf[:, T:T + 2], 0.0)
            dve.wait_ge(loaded, 16)
            op, n = (ALU.arith_shift_right, LOBITS) if high else (ALU.bitwise_and, NB_LO - 1)
            st.did(dve.tensor_scalar(digit[:], rec[:, :, key], n, None, op))
            st.did(dve.tensor_copy(digitf[:, 0:T], digit[:]))
            dve.tensor_scalar(part[0][:], digit[:], 5, None, ALU.arith_shift_right)
            st.did(dve.tensor_scalar(part[1][:], digit[:], DL - 1, None, ALU.bitwise_and))
            for k in range(2):
                st.did(dve.tensor_copy(partf[k][:], part[k][:]))
            for k, (hots, width) in enumerate(((hot_up, DH), (hot_low, DL))):
                dve.tensor_tensor(hots[:], spread(partf[k][:], 2, width), spread(net.iota16[:, 0:width], 1, T),
                                  ALU.is_equal).then_inc(parts_ready, 1)
            blocks = net.ident[:].rearrange("p (c h) -> p c h", h=DH)
            dve.tensor_reduce(same[:], blocks, AX.X, ALU.add)
            st.did(dve.tensor_reduce(fold[:], blocks.rearrange("p c h -> p h c"), AX.X, ALU.add))
            dve.wait_ge(crossed, T // DC)
            st.did(dve.tensor_tensor(own_part[:], cross[:], spread(same[:], 2, DL), ALU.mult))
            dve.tensor_reduce(by_row[:], own_part[:].rearrange("p c l -> p l c"), AX.X, ALU.add).then_inc(folding, 1)
            dve.wait_ge(counted, 1)
            st.did(dve.tensor_tensor_scan(out=upto[:], data0=net.ones[0:DH, 0:DL], data1=counts[:], initial=0.0,
                                          op0=ALU.mult, op1=ALU.add))
            st.did(dve.tensor_tensor(before[:], upto[:], counts[:], ALU.subtract))
            st.did(dve.tensor_scalar(rows_before[:], net.upper[0:DH, 0:DH], upto[:, DL - 1:DL], None, ALU.mult))
            st.did(dve.tensor_tensor(base[:], spread(before[:], 1, DH), spread(net.ident[0:DH, 0:DH], 2, DL), ALU.mult))
            st.did(dve.tensor_tensor(base2[:], base[:], spread(rows_before[:], 2, DL), ALU.add))
            dve.sem_inc(base_ready, 1)

            def one_hot(r, t):
                dve.tensor_scalar(hot[r][:], net.iota16[:, 0:nb], digitf[:, bass.ds(t, 1)], None,
                                  ALU.is_equal).then_inc(hot_ready, 1)

            one_hot(0, 0)
            one_hot(1, 1)
            with dve.Fori(0, NPAIR) as i:
                st.enter(i, 2 * (1 if high else 3))
                for j in range(2):
                    dve.wait_ge(sent[j], i * (16 * CH))
                    for u in range(j * CH, (j + 1) * CH):
                        one_hot((u + 2) % RING, i * (2 * CH) + (u + 2))
                        dve.wait_ge(ranked, i * (2 * CH) + (u + 1))
                        dve.scalar_tensor_tensor(out=junk[u % 2][:], in0=hot[u % RING][:], scalar=1.0,
                                                 in1=acc[u % 2][:, 0:nb], op0=ALU.mult, op1=ALU.mult,
                                                 accum_out=rank[j][:, u % CH:u % CH + 1]).then_inc(read, 1)
                    dve.wait_ge(read, i * (2 * CH) + (j + 1) * CH + 2)
                    if high:
                        st.did(dve.tensor_scalar(rank[j][:], rank[j][:], 1.0, None, ALU.add))
                        dve.tensor_copy(row[j][:], rank[j][:]).then_inc(rows_ready[j], 1)
                    else:
                        st.did(dve.tensor_copy(ranki[j][:], rank[j][:]))
                        st.did(dve.tensor_scalar(low[j][:], ranki[j][:], P - 1, None, ALU.bitwise_and))
                        st.did(dve.tensor_scalar(ranki[j][:], ranki[j][:], 7, None, ALU.arith_shift_right))
                        dve.scalar_tensor_tensor(out=row[j][:], in0=low[j][:], scalar=float(T), in1=ranki[j][:],
                                                 op0=ALU.mult, op1=ALU.add).then_inc(rows_ready[j], 1)
                st.leave(NPAIR)

        @block.tensor
        def _(pe):
            pe.wait_ge(parts_ready, 2)

            def cross_product(n, first):
                cols = bass.ds(n * DC, DC)
                pe.matmul(cross[:], hot_up[:, cols, :].rearrange("p c h -> p (c h)"), hot_low[:, cols, :],
                          start=first, stop=False, skip_group_check=True).then_inc(crossed, 1)

            for n in range(COUNTED):
                cross_product(n, n == 0)
            with pe.Fori(1, T // (DC * COUNTED)) as i:
                for n in range(COUNTED):
                    cross_product(i * COUNTED + n, False)
            pe.wait_ge(folding, 1)
            pe.matmul(counts[:], fold[:], by_row[:], start=True, stop=True).then_inc(counted, 1)
            pe.wait_ge(base_ready, 1)
            for b in range(2):
                pe.matmul(acc[b][:, 0:nb], net.ones[0:DH, :], base2[:].rearrange("p h l -> p (h l)")[:, 0:nb], start=True, stop=False, skip_group_check=True)
            pe.sem_inc(read, 2)
            with pe.Fori(0, NPAIR) as i:
                for u in range(2 * CH):
                    a = acc[u % 2][:, 0:nb]
                    pe.wait_ge(hot_ready, i * (2 * CH) + u + 1)
                    pe.wait_ge(read, i * (2 * CH) + u + 1)
                    pe.matmul(a, net.lower16[:], hot[(u - 2) % RING][:], start=False, stop=False, skip_group_check=True)
                    pe.matmul(a, net.ones16[:], hot[(u - 1) % RING][:], start=False, stop=False, skip_group_check=True)
                    pe.matmul(a, net.upper16[:], hot[u % RING][:], start=False, stop=True, skip_group_check=True).then_inc(ranked, 1)

        @block.gpsimd
        def _(pool):
            with pool.Fori(0, NPAIR) as i:
                for j in range(2):
                    pool.wait_ge(rows_ready[j], i + 1)
                    pool.wait_ge(staged[j], i * 16 + 16)
                    pool.sem_inc(started, 1)
                    for r in range(CH):
                        pool.indirect_dma_start(
                            out=dest, out_offset=bass.IndirectOffsetOnAxis(ap=row[j][:, r:r + 1], axis=0),
                            in_=stage[j][:, r, :], in_offset=None).then_inc(sent[j], 16)
            for j in range(2):
                pool.wait_ge(sent[j], NPAIR * CH * 16)



class Order:

    def __init__(self, net, c, name, records, key):
        nc = net.nc
        self.name, self.records, self.key_col = name, records, key
        self.cont = tile(nc, c, name + "_cont", [P, T])
        self.key = tile(nc, c, name + "_key", [P, T])
        self.scan = tile(nc, c, name + "_scan", [P, T])
        self.to_node = tile(nc, c, name + "_to_node", [P, T], I32)
        self.carry = tile(nc, c, name + "_carry", [P, P])
        self.fix_node = tile(nc, c, name + "_fix_node", [P, 1], I32)
        self.fix_slot = tile(nc, c, name + "_fix_slot", [P, 1], I32)


def order_phase(net, o, table, second):
    nc = net.nc
    name = o.name
    with net.phase() as c:
        rec, prev, nxt = (tile(nc, c, name + n, [P, T, 4], I32) for n in ("rec", "prev", "nxt"))
        key = o.key
        pkey, nkey, t1, last, lead, deg, num = (
            tile(nc, c, name + n, [P, T]) for n in ("pkey", "nkey", "t1", "last", "lead", "deg", "num"))
        diag = tile(nc, c, name + "diag", [P, P])
        fixf, ends, cnt, s1 = (tile(nc, c, name + n, [P, 1]) for n in ("fixf", "ends", "cnt", "s1"))
        tail = tile(nc, c, name + "tail", [P, 2])
        carried = tile(nc, c, name + "carried", [P, 2])
        slot = tile(nc, c, name + "slot", [P, T])
        stage = [tile(nc, c, name + f"stage{j}", [P, CH, 2]) for j in range(2)]
        row = [tile(nc, c, name + f"row{j}", [P, CH], I32) for j in range(2)]
        kb = bank(nc, c, name + "kb", [P, P])
        cb = bank(nc, c, name + "cb", [P, 2])
        loaded, own, diag_ready, key_rows, tail_ready, carry_ready, iotas, started = (
            net.sem(name + n) for n in ("loaded", "own", "diag_ready", "key_rows", "tail_ready",
                                        "carry_ready", "iotas", "started"))
        staged = [net.sem(name + f"staged{j}") for j in range(2)]
        sent = [net.sem(name + f"sent{j}") for j in range(2)]
        block = c.enter_context(nc.Block())

        @block.sync
        def _(sp):
            for k, to in enumerate((prev, rec, nxt)):
                sp.dma_start(to[:], o.records[k:k + EP, :].rearrange("(p t) c -> p t c", p=P)).then_inc(loaded, 16)

        @block.vector
        def _(dve):
            st = Steps(dve, own)
            dve.wait_ge(loaded, 3 * 16)
            dve.tensor_copy(pkey[:], prev[:, :, o.key_col])
            dve.tensor_copy(nkey[:], nxt[:, :, o.key_col])
            st.did(dve.tensor_copy(key[:], rec[:, :, o.key_col]))
            dve.tensor_tensor(o.cont[:], key[:], pkey[:], ALU.is_equal)
            dve.tensor_tensor(last[:], key[:], nkey[:], ALU.not_equal)
            st.did(dve.tensor_scalar(lead[:], key[:], key[:, 0:1], None, ALU.is_equal))
            st.did(dve.tensor_copy(o.scan[:], o.cont[:]))
            st.did(dve.memset(o.scan[:].rearrange("p (c t) -> p c t", t=CH)[:, :, 0:1], 0.0))
            st.did(dve.tensor_scalar(t1[:], key[:], float(SKIP), None, ALU.subtract))
            st.did(dve.tensor_tensor(t1[:], t1[:], last[:], ALU.mult))
            st.did(dve.tensor_scalar(o.to_node[:], t1[:], float(SKIP), None, ALU.add))
            st.did(dve.tensor_scalar(diag[:], net.ident[:], key[:, 0:1], None, ALU.mult))
            dve.sem_inc(diag_ready, 1)
            dve.wait_ge(key_rows, 1)
            st.did(dve.tensor_scalar(diag[:], kb[:], key[:, T - 1:T], None, ALU.is_equal))
            st.did(dve.tensor_tensor(o.carry[:], diag[:], net.upper[:], ALU.mult))
            st.did(dve.tensor_reduce(cnt[:], lead[:], AX.X, ALU.add))
            st.did(dve.tensor_tensor(ends[:], key[:, 0:1], nkey[:, T - 1:T], ALU.not_equal))
            st.did(dve.tensor_tensor(ends[:], ends[:], o.cont[:, 0:1], ALU.mult))
            st.did(dve.tensor_scalar(fixf[:], key[:, 0:1], float(SKIP), None, ALU.subtract))
            st.did(dve.tensor_tensor(fixf[:], fixf[:], ends[:], ALU.mult))
            dve.tensor_scalar(o.fix_node[:], fixf[:], float(SKIP), None, ALU.add)
            st.did(dve.tensor_scalar(s1[:], net.part[:], float(T), float(-1 - SKIP), ALU.mult, ALU.add))
            st.did(dve.tensor_tensor(s1[:], s1[:], cnt[:], ALU.add))
            st.did(dve.tensor_tensor(s1[:], s1[:], ends[:], ALU.mult))
            st.did(dve.tensor_scalar(o.fix_slot[:], s1[:], float(SKIP), None, ALU.add))
            weight = rec[:, :, 2].bitcast(F32)
            st.did(dve.tensor_tensor_scan(out=deg[:], data0=o.cont[:], data1=weight, initial=0.0,
                                          op0=ALU.mult, op1=ALU.add))
            if second == "count":
                st.did(dve.memset(t1[:], 1.0))
                st.did(dve.tensor_tensor_scan(out=num[:], data0=o.cont[:], data1=t1[:], initial=0.0,
                                              op0=ALU.mult, op1=ALU.add))
                st.did(dve.tensor_copy(tail[:, 1:2], num[:, T - 1:T]))
            else:
                st.did(dve.memset(tail[:, 1:2], 0.0))
                dve.wait_ge(iotas, 1)
            st.did(dve.tensor_copy(tail[:, 0:1], deg[:, T - 1:T]))
            dve.sem_inc(tail_ready, 1)
            st.did(dve.tensor_scalar(lead[:], lead[:], o.cont[:, 0:1], None, ALU.mult))
            dve.wait_ge(carry_ready, 1)
            st.did(dve.tensor_copy(carried[:], cb[:]))
            st.did(dve.tensor_scalar(t1[:], lead[:], carried[:, 0:1], None, ALU.mult))
            st.did(dve.tensor_tensor(deg[:], deg[:], t1[:], ALU.add))
            if second == "count":
                st.did(dve.tensor_scalar(t1[:], lead[:], carried[:, 1:2], None, ALU.mult))
                st.did(dve.tensor_tensor(num[:], num[:], t1[:], ALU.add))
            both = (deg, num if second == "count" else slot)
            with dve.Fori(0, NPAIR) as i:
                for j in range(2):
                    at = bass.ds(i * (2 * CH) + j * CH, CH)
                    dve.wait_ge(sent[j], i * (16 * CH))
                    dve.tensor_copy(stage[j][:, :, 0], both[0][:, at])
                    dve.tensor_copy(stage[j][:, :, 1], both[1][:, at])
                    dve.tensor_copy(row[j][:], o.to_node[:, at]).then_inc(staged[j], 1)

        @block.tensor
        def _(pe):
            pe.wait_ge(diag_ready, 1)
            pe.matmul(kb[:], net.ones[:], diag[:], start=True, stop=True).then_inc(key_rows, 1)
            pe.wait_ge(tail_ready, 1)
            pe.matmul(cb[:], o.carry[:], tail[:], start=True, stop=True).then_inc(carry_ready, 1)

        @block.gpsimd
        def _(pool):
            pool.iota(slot[:], pattern=[[1, T]], base=1, channel_multiplier=T,
                      allow_small_or_imprecise_dtypes=True).then_inc(iotas, 1)
            pool.wait_ge(net.zeroed, net.zeroed_all)
            with pool.Fori(0, NPAIR) as i:
                for j in range(2):
                    pool.wait_ge(staged[j], i + 1)
                    pool.sem_inc(started, 1)
                    for r in range(CH):
                        pool.indirect_dma_start(
                            out=table, out_offset=bass.IndirectOffsetOnAxis(ap=row[j][:, r:r + 1], axis=0),
                            in_=stage[j][:, r, :], in_offset=None,
                            bounds_check=NR - 1, oob_is_err=False).then_inc(sent[j], 16)
            for j in range(2):
                pool.wait_ge(sent[j], NPAIR * CH * 16)



def node_scalars_phase(net):
    nc = net.nc
    with net.phase() as c:
        bd = tile(nc, c, "ns_bd", [P, NPP, 2])
        bs = tile(nc, c, "ns_bs", [P, NPP, 2])
        deg = [tile(nc, c, f"ns_deg{n}", [P, NPP]) for n in range(3)]
        pos = [tile(nc, c, f"ns_pos{n}", [P, NPP]) for n in range(3)]
        root = [tile(nc, c, f"ns_root{n}", [P, NPP]) for n in range(3)]
        pair = tile(nc, c, "ns_pair", [P, NPP, 2])
        half = tile(nc, c, "ns_half", [P, NPP])
        loaded, own, degrees, rooted, paired, written = (
            net.sem("ns_" + n) for n in ("loaded", "own", "degrees", "rooted", "paired", "written"))
        block = c.enter_context(nc.Block())

        @block.sync
        def _(sp):
            sp.dma_start(bd[:], net.by_dst[:, :].rearrange("(p g) c -> p g c", p=P)).then_inc(loaded, 16)
            sp.dma_start(bs[:], net.by_src[:, :].rearrange("(p g) c -> p g c", p=P)).then_inc(loaded, 16)
            sp.wait_ge(paired, 1)
            sp.dma_start(net.pairs[:, :].rearrange("(p g) c -> p g c", p=P), pair[:]).then_inc(written, 16)
            sp.wait_ge(written, 16)

        @block.scalar
        def _(act):
            act.wait_ge(degrees, 1)
            for n in range(3):
                act.activation(root[n][:], deg[n][:], ACT.Sqrt).then_inc(rooted, 1)

        @block.vector
        def _(dve):
            st = Steps(dve, own)
            dve.wait_ge(loaded, 2 * 16)
            dve.tensor_scalar(deg[0][:], bs[:, :, 0], 1.0, None, ALU.add)
            dve.tensor_scalar(deg[1][:], bd[:, :, 0], 1.0, None, ALU.add)
            st.did(dve.tensor_copy(deg[2][:], bs[:, :, 1]))
            dve.tensor_copy(net.slot1[:], bd[:, :, 1])
            for n in range(3):
                st.did(dve.tensor_scalar(pos[n][:], deg[n][:], 0.0, None, ALU.is_gt))
            st.did(dve.tensor_scalar(deg[0][:], deg[0][:], 1e-30, None, ALU.max))
            st.did(dve.tensor_scalar(deg[1][:], deg[1][:], 1e-30, None, ALU.max))
            dve.tensor_scalar(deg[2][:], deg[2][:], 1.0, None, ALU.max).then_inc(degrees, 1)
            dve.wait_ge(rooted, 3)
            dve.reciprocal(net.inv_count[:], deg[2][:])
            for n, to in enumerate((net.inv_out, net.inv_in, net.inv_deg)):
                st.did(dve.reciprocal(root[n][:], root[n][:]))
                st.did(dve.tensor_tensor(half[:], root[n][:], root[n][:], ALU.mult))
                st.did(dve.tensor_tensor(half[:], half[:], deg[n][:], ALU.mult))
                st.did(dve.tensor_scalar(half[:], half[:], -0.5, 1.5, ALU.mult, ALU.add))
                st.did(dve.tensor_tensor(root[n][:], root[n][:], half[:], ALU.mult))
                st.did(dve.tensor_tensor(to[:], root[n][:], pos[n][:], ALU.mult))
            st.did(dve.scalar_tensor_tensor(out=net.own_part[:], in0=net.inv_out[:], scalar=0.9, in1=net.inv_in[:],
                                            op0=ALU.mult, op1=ALU.mult))
            dve.tensor_copy(pair[:, :, 0], net.inv_in[:])
            dve.tensor_copy(pair[:, :, 1], net.own_part[:]).then_inc(paired, 1)
            st.did(dve.memset(net.own_k[:], 1.0))
            for _ in range(K_STEPS):
                st.did(dve.tensor_tensor(net.own_k[:], net.own_k[:], net.own_part[:], ALU.mult))
                st.did(dve.tensor_scalar(net.own_k[:], net.own_k[:], 0.1, None, ALU.add))
            st.did(dve.tensor_scalar(net.own_k[:], net.own_k[:], 1.0, None, ALU.add))


def node_view(table, width):
    return table[:, :].rearrange("(p g) c -> p g c", p=P)


class RealRows:

    def __init__(self, ap):
        whole = (P - 1) * NPP
        self.first = ap[0:whole, :].rearrange("(p g) c -> p g c", g=NPP)
        self.last = ap[whole:N, :].rearrange("(p g) c -> p g c", p=1)

    def move(self, eng, sem, tile_ap, at, full, store):
        halves(eng, sem, lambda a, b: tile_ap[a:b], lambda a, b: self.first[a:b, at, :], store)
        if full:
            if store:
                eng.dma_start(self.last[:, at, :], tile_ap[P - 1:P]).then_inc(sem, 16)
            else:
                eng.dma_start(tile_ap[P - 1:P], self.last[:, at, :]).then_inc(sem, 16)


PARTS = ((0, PAIRS_FULL, True), (PAIRS_FULL, PAIRS, False))


def moved(i, full, turns=1):
    return (i + turns) * 48 if full else (i + turns) * 32 + PAIRS_FULL * 16


def x_rows_phase(net, x):
    nc = net.nc
    with net.phase() as c:
        row = [tile(nc, c, f"xr_row{j}", [P, G, XW]) for j in range(2)]
        blank = net.sem("xr_blank")
        loaded = [net.sem(f"xr_loaded{j}") for j in range(2)]
        made = [net.sem(f"xr_made{j}") for j in range(2)]
        stored = [net.sem(f"xr_stored{j}") for j in range(2)]
        rows, to = RealRows(x), node_view(net.x_rows, XW)
        block = c.enter_context(nc.Block())

        @block.sync
        def _(sp):
            sp.wait_ge(blank, 2)
            for a, b, full in PARTS:
                with sp.Fori(a, b) as i:
                    for j in range(2):
                        sp.wait_ge(stored[j], i * 16)
                        rows.move(sp, loaded[j], row[j][:, :, 0:D], bass.ds(i * (2 * G) + j * G, G), full, False)

        @block.vector
        def _(dve):
            for j in range(2):
                dve.memset(row[j][:], 0.0).then_inc(blank, 1)
            dve.wait_ge(blank, 2)
            for a, b, full in PARTS:
                with dve.Fori(a, b) as i:
                    for j in range(2):
                        at = bass.ds(i * (2 * G) + j * G, G)
                        dve.wait_ge(stored[j], i * 16)
                        dve.tensor_copy(row[j][:, :, D], net.inv_out[:, at])
                        dve.tensor_copy(row[j][:, :, D + 1], net.own_part[:, at])
                        dve.tensor_copy(row[j][:, :, D + 2], net.slot1[:, at]).then_inc(made[j], 1)

        @block.scalar
        def _(act):
            for a, b, full in PARTS:
                with act.Fori(a, b) as i:
                    for j in range(2):
                        act.wait_ge(loaded[j], moved(i, full))
                        act.wait_ge(made[j], i + 1)
                        act.dma_start(to[:, bass.ds(i * (2 * G) + j * G, G), :], row[j][:]).then_inc(stored[j], 16)
            for j in range(2):
                act.wait_ge(stored[j], PAIRS * 16)



def edge_view(table):
    return table.rearrange("(p t) c -> p t c", p=P)


def chunk(i, j):
    return i * (2 * CH) + j * CH


MW = 32


def mask_phase(net, o, mask):
    nc = net.nc
    with net.phase() as c:
        block = c.enter_context(nc.Block())

        @block.vector
        def _(dve):
            with dve.Fori(0, NPAIR) as i:
                for j in range(2):
                    dve.tensor_copy(mask[:, bass.ds(i * 2 + j, 1), :].rearrange("p o (f t) -> p (o f) t", t=CH),
                                    spread(o.scan[:, bass.ds(chunk(i, j), CH)], 1, MW))


class Fix:

    def __init__(self, net, c, name, width):
        self.row = tile(net.nc, c, name + "_fixrow", [P, width])
        self.bank = bank(net.nc, c, name + "_fixbank", [P, width])
        self.product, self.got, self.added, self.put, self.turns, self.blanked = (
            net.sem(f"{name}_fix_{n}") for n in ("product", "got", "added", "put", "turns", "blanked"))

    def tensor(self, pe, n, o, tail):
        pe.wait_ge(self.added, n)
        pe.matmul(self.bank[:], o.carry[:], tail, start=True, stop=True).then_inc(self.product, 1)

    def blank(self, dve):
        dve.memset(self.row[:], 0.0).then_inc(self.blanked, 1)

    def gpsimd(self, pool, n, table, index, last_row):
        pool.wait_ge(self.blanked, 1)
        pool.sem_inc(self.turns, 1)
        pool.indirect_dma_start(out=self.row[:], out_offset=None, in_=table,
                                in_offset=bass.IndirectOffsetOnAxis(ap=index, axis=0),
                                bounds_check=last_row, oob_is_err=False).then_inc(self.got, 16)
        pool.wait_ge(self.added, n + 1)
        pool.sem_inc(self.turns, 1)
        pool.indirect_dma_start(out=table, out_offset=bass.IndirectOffsetOnAxis(ap=index, axis=0),
                                in_=self.row[:], in_offset=None,
                                bounds_check=last_row, oob_is_err=False).then_inc(self.put, 16)
        pool.wait_ge(self.put, n * 16 + 16)

    def vector(self, dve, n):
        dve.wait_ge(self.product, n + 1)
        dve.wait_ge(self.got, n * 16 + 16)
        dve.tensor_tensor(self.row[:], self.row[:], self.bank[:], ALU.add).then_inc(self.added, 1)


def scan_chunk(dve, st, o, mask, msg, sums, prev, i, j):
    w, flat = msg.shape[1], "p f t -> p (f t)"
    st.did(dve.scalar_tensor_tensor(out=msg[:, :, 0], in0=prev[:, :, CH - 1], scalar=o.cont[:, bass.ds(chunk(i, j), 1)],
                                    in1=msg[:, :, 0], op0=ALU.mult, op1=ALU.add))
    for a in range(0, w, MW):
        b = min(a + MW, w)
        ins = dve.tensor_tensor_scan(out=sums[:, a:b, :].rearrange(flat), data1=msg[:, a:b, :].rearrange(flat),
                                     data0=mask[:, bass.ds(i * 2 + j, 1), 0:(b - a) * CH].rearrange("p o n -> p (o n)"),
                                     initial=0.0, op0=ALU.mult, op1=ALU.add)
        (st.did if b == w else st.mark)(ins)


def scan_steps(w):
    return 1 + -(-w // MW)



def appnp_first_phase(net, o, co):
    nc = net.nc
    with net.phase() as c:
        rec = [tile(nc, c, f"a0_rec{j}", [P, CH, 4], I32) for j in range(2)]
        xg = [tile(nc, c, f"a0_xg{j}", [P, CH, XW]) for j in range(2)]
        pg = [tile(nc, c, f"a0_pg{j}", [P, CH, 2]) for j in range(2)]
        msg = [tile(nc, c, f"a0_msg{j}", [P, D, CH]) for j in range(2)]
        sums = [tile(nc, c, f"a0_sums{j}", [P, D, CH]) for j in range(2)]
        rows = [tile(nc, c, f"a0_rows{j}", [P, CH, D]) for j in range(2)]
        slot = tile(nc, c, "a0_slot", [P, T])
        has = tile(nc, c, "a0_has", [P, T])
        zrow = tile(nc, c, "a0_zrow", [P, 1])
        index = tile(nc, c, "a0_index", [P, T], I32)
        own, started, indexed, kept = (net.sem("a0_" + n) for n in ("own", "started", "indexed", "kept"))
        sem2 = lambda n: [net.sem(f"a0_{n}{j}") for j in range(2)]
        staged, gathered, used, summed, rowed, x_out, r_out = (
            sem2(n) for n in ("staged", "gathered", "used", "summed", "rowed", "x_out", "r_out"))
        fix = Fix(net, c, "a0", D)
        block = c.enter_context(nc.Block())
        records = edge_view(o.records[1:EP + 1, :])

        @block.sync
        def _(sp):
            with sp.Fori(0, NPAIR) as i:
                for j in range(2):
                    sp.wait_ge(used[j], i)
                    sp.dma_start(rec[j][:], records[:, bass.ds(chunk(i, j), CH), :]).then_inc(staged[j], 16)
            sp.wait_ge(indexed, 1)
            sp.dma_start(net.slot_index[:, :], index[:]).then_inc(kept, 16)
            sp.wait_ge(kept, 16)

        @block.gpsimd
        def _(pool):
            with pool.Fori(0, NPAIR) as i:
                for j in range(2):
                    pool.wait_ge(staged[j], i * 16 + 16)
                    pool.wait_ge(x_out[j], i * 16)
                    pool.sem_inc(started, 1)
                    for r in range(CH):
                        pool.indirect_dma_start(
                            out=xg[j][:, r, :], out_offset=None, in_=net.x_rows[:, :],
                            in_offset=bass.IndirectOffsetOnAxis(ap=rec[j][:, r, 0:1], axis=0)).then_inc(gathered[j], 16)
                        pool.indirect_dma_start(
                            out=pg[j][:, r, :], out_offset=None, in_=net.pairs[:, :],
                            in_offset=bass.IndirectOffsetOnAxis(ap=rec[j][:, r, 1:2], axis=0)).then_inc(gathered[j], 16)
            for j in range(2):
                pool.wait_ge(r_out[j], NPAIR * 16)
            fix.gpsimd(pool, 0, net.slots[1][:, :], o.fix_slot[:], TR - 1)

        @block.vector
        def _(dve):
            st = Steps(dve, own)
            fix.blank(dve)
            st.did(dve.memset(sums[1][:, :, CH - 1:CH], 0.0))
            st.did(dve.tensor_scalar(zrow[:], net.part[:], float(ZROW), None, ALU.add))
            with dve.Fori(0, NPAIR) as i:
                st.enter(i, 2 * (6 + scan_steps(D)))
                for j in range(2):
                    at = bass.ds(chunk(i, j), CH)
                    dve.wait_ge(gathered[j], i * (2 * CH * 16) + 2 * CH * 16)
                    st.did(dve.scalar_tensor_tensor(out=co.weight[:, at], in0=rec[j][:, :, 2].bitcast(F32), scalar=0.9,
                                                    in1=xg[j][:, :, D], op0=ALU.mult, op1=ALU.mult))
                    st.did(dve.tensor_tensor(co.weight[:, at], co.weight[:, at], pg[j][:, :, 0], ALU.mult))
                    st.did(dve.tensor_copy(co.src_part[:, at], xg[j][:, :, D + 1]))
                    st.did(dve.tensor_copy(co.dst_part[:, at], pg[j][:, :, 1]))
                    st.did(dve.tensor_copy(slot[:, at], xg[j][:, :, D + 2]))
                    st.did(dve.tensor_tensor(msg[j][:].rearrange("p f t -> p t f"), xg[j][:, :, 0:D],
                                             spread(co.weight[:, at], 2, D), ALU.mult))
                    dve.sem_inc(used[j], 1)
                    dve.wait_ge(rowed[j], i)
                    scan_chunk(dve, st, o, co.mask, msg[j], sums[j], sums[1 - j], i, j)
                    dve.sem_inc(summed[j], 1)
                st.leave(NPAIR)
            st.did(dve.tensor_scalar(has[:], slot[:], 0.0, None, ALU.is_gt))
            st.did(dve.tensor_scalar(slot[:], slot[:], zrow[:, 0:1], -1.0, ALU.subtract, ALU.add))
            st.did(dve.tensor_tensor(slot[:], slot[:], has[:], ALU.mult))
            dve.tensor_scalar(index[:], slot[:], zrow[:, 0:1], None, ALU.add).then_inc(indexed, 1)
            st.did(dve.tensor_scalar(co.alpha[:], co.src_part[:], 0.1, None, ALU.add))
            fix.vector(dve, 0)

        @block.scalar
        def _(act):
            with act.Fori(0, NPAIR) as i:
                for j in range(2):
                    at = bass.ds(chunk(i, j), CH)
                    act.wait_ge(gathered[j], i * (2 * CH * 16) + 2 * CH * 16)
                    act.dma_start(edge_view(net.x_edges)[:, at, :], xg[j][:, :, 0:D]).then_inc(x_out[j], 16)
                    act.wait_ge(summed[j], i + 1)
                    act.wait_ge(r_out[j], i * 16)
                    act.activation(rows[j][:], sums[j][:].rearrange("p f t -> p t f"), ACT.Copy).then_inc(rowed[j], 1)
                    act.wait_ge(rowed[j], i + 1)
                    act.dma_start(edge_view(net.slots[1][0:EP, :])[:, at, :], rows[j][:]).then_inc(r_out[j], 16)
            for j in range(2):
                act.wait_ge(x_out[j], NPAIR * 16)

        @block.tensor
        def _(pe):
            pe.wait_ge(summed[1], NPAIR)
            fix.tensor(pe, 0, o, sums[1][:, :, CH - 1])


def appnp_steps_phase(net, o, co):
    nc = net.nc
    with net.phase() as c:
        index = [tile(nc, c, f"as_index{j}", [P, CH], I32) for j in range(2)]
        rg = [tile(nc, c, f"as_rg{j}", [P, CH, D]) for j in range(2)]
        xe = [tile(nc, c, f"as_xe{j}", [P, CH, D]) for j in range(2)]
        rr = [tile(nc, c, f"as_rr{j}", [P, CH, D]) for j in range(2)]
        msg = [tile(nc, c, f"as_msg{j}", [P, D, CH]) for j in range(2)]
        sums = [tile(nc, c, f"as_sums{j}", [P, D, CH]) for j in range(2)]
        of_x = tile(nc, c, "as_of_x", [P, T])
        own, started, stepped, turns, begun = (
            net.sem("as_" + n) for n in ("own", "started", "stepped", "turns", "begun"))
        sem2 = lambda n: [net.sem(f"as_{n}{j}") for j in range(2)]
        staged, gathered, streamed, used, summed, r_out = (
            sem2(n) for n in ("staged", "gathered", "streamed", "used", "summed", "r_out"))
        fix = Fix(net, c, "as", D)
        block = c.enter_context(nc.Block())
        STEPS = K_STEPS - 1
        PER = NPAIR * 2 * (5 + scan_steps(D)) + 5

        def steps(eng, step):
            with eng.Fori(0, STEPS // 2) as m:
                for odd in range(2):
                    step(m * 2 + odd, 1 - odd)
            step(STEPS - 1, 1)

        @block.sync
        def _(sp):
            def step(s, rt):
                sp.wait_ge(stepped, s)
                sp.sem_inc(turns, 1)
                with sp.Fori(0, NPAIR) as i:
                    n = s * NPAIR + i
                    for j in range(2):
                        at = bass.ds(chunk(i, j), CH)
                        sp.wait_ge(gathered[j], n * (CH * 16))
                        sp.dma_start(index[j][:], net.slot_index[:, at]).then_inc(staged[j], 16)
                        sp.wait_ge(used[j], n)
                        sp.sem_inc(turns, 1)
                        sp.wait_ge(r_out[j], n * 16)
                        sp.dma_start(xe[j][:], edge_view(net.x_edges)[:, at, :]).then_inc(streamed[j], 16)
                        sp.dma_start(rr[j][:], edge_view(net.slots[rt][0:EP, :])[:, at, :]).then_inc(streamed[j], 16)
            steps(sp, step)

        @block.gpsimd
        def _(pool):
            def step(s, rt):
                with pool.Fori(0, NPAIR) as i:
                    n = s * NPAIR + i
                    for j in range(2):
                        pool.wait_ge(staged[j], n * 16 + 16)
                        pool.wait_ge(used[j], n)
                        pool.sem_inc(started, 1)
                        for r in range(CH):
                            pool.indirect_dma_start(
                                out=rg[j][:, r, :], out_offset=None, in_=net.slots[rt][:, :],
                                in_offset=bass.IndirectOffsetOnAxis(ap=index[j][:, r:r + 1], axis=0)).then_inc(gathered[j], 16)
                for j in range(2):
                    pool.wait_ge(r_out[j], (s + 1) * (NPAIR * 16))
                fix.gpsimd(pool, s, net.slots[1 - rt][:, :], o.fix_slot[:], TR - 1)
                pool.sem_inc(stepped, 1)
            steps(pool, step)

        @block.vector
        def _(dve):
            st = Steps(dve, own)
            fix.blank(dve)

            def step(s, rt):
                own_before = st.base
                st.base = own_before + s * PER
                st.n = 0
                dve.wait_ge(fix.product, s)
                st.did(dve.memset(sums[1][:, :, CH - 1:CH], 0.0))
                st.did(dve.tensor_tensor(of_x[:], co.alpha[:], co.weight[:], ALU.mult))
                dve.sem_inc(begun, 1)
                with dve.Fori(0, NPAIR) as i:
                    n = s * NPAIR + i
                    st.enter(i, 2 * (5 + scan_steps(D)))
                    for j in range(2):
                        at = bass.ds(chunk(i, j), CH)
                        dve.wait_ge(streamed[j], n * 32 + 32)
                        st.did(dve.tensor_tensor(xe[j][:], xe[j][:], spread(of_x[:, at], 2, D), ALU.mult))
                        dve.wait_ge(gathered[j], n * (CH * 16) + CH * 16)
                        st.did(dve.tensor_tensor(rg[j][:], rg[j][:], spread(co.weight[:, at], 2, D), ALU.mult))
                        st.did(dve.tensor_tensor(msg[j][:].rearrange("p f t -> p t f"), rg[j][:], xe[j][:], ALU.add))
                        dve.sem_inc(used[j], 1)
                        scan_chunk(dve, st, o, co.mask, msg[j], sums[j], sums[1 - j], i, j)
                        st.did(dve.tensor_tensor(rr[j][:], rr[j][:], spread(co.dst_part[:, at], 2, D), ALU.mult))
                        st.did(dve.tensor_tensor(rr[j][:], rr[j][:], sums[j][:].rearrange("p f t -> p t f"), ALU.add))
                        dve.sem_inc(summed[j], 1)
                    st.leave(NPAIR)
                st.did(dve.tensor_tensor(co.alpha[:], co.alpha[:], co.src_part[:], ALU.mult))
                st.did(dve.tensor_scalar(co.alpha[:], co.alpha[:], 0.1, None, ALU.add))
                fix.vector(dve, s)
                st.did(dve.nop())
                assert st.n == PER, st.n
                st.base = own_before
            steps(dve, step)

        @block.scalar
        def _(act):
            def step(s, rt):
                with act.Fori(0, NPAIR) as i:
                    n = s * NPAIR + i
                    for j in range(2):
                        act.wait_ge(summed[j], n + 1)
                        act.dma_start(edge_view(net.slots[1 - rt][0:EP, :])[:, bass.ds(chunk(i, j), CH), :],
                                      rr[j][:]).then_inc(r_out[j], 16)
            steps(act, step)

        @block.tensor
        def _(pe):
            def step(s, rt):
                pe.wait_ge(summed[1], (s + 1) * NPAIR)
                fix.tensor(pe, s, o, sums[1][:, :, CH - 1])
            steps(pe, step)


def to_nodes_phase(net, o):
    nc = net.nc
    with net.phase() as c:
        rows = [tile(nc, c, f"tn_rows{j}", [P, CH, D]) for j in range(2)]
        node = [tile(nc, c, f"tn_node{j}", [P, CH], I32) for j in range(2)]
        started = net.sem("tn_started")
        sem2 = lambda n: [net.sem(f"tn_{n}{j}") for j in range(2)]
        loaded, named, sent = (sem2(n) for n in ("loaded", "named", "sent"))
        block = c.enter_context(nc.Block())

        @block.sync
        def _(sp):
            with sp.Fori(0, NPAIR) as i:
                for j in range(2):
                    sp.wait_ge(sent[j], i * (CH * 16))
                    sp.dma_start(rows[j][:], edge_view(net.slots[0][0:EP, :])[:, bass.ds(chunk(i, j), CH), :]).then_inc(loaded[j], 16)

        @block.vector
        def _(dve):
            with dve.Fori(0, NPAIR) as i:
                for j in range(2):
                    dve.wait_ge(sent[j], i * (CH * 16))
                    dve.tensor_copy(node[j][:], o.to_node[:, bass.ds(chunk(i, j), CH)]).then_inc(named[j], 1)

        @block.gpsimd
        def _(pool):
            with pool.Fori(0, NPAIR) as i:
                for j in range(2):
                    pool.wait_ge(loaded[j], i * 16 + 16)
                    pool.wait_ge(named[j], i + 1)
                    pool.sem_inc(started, 1)
                    for r in range(CH):
                        pool.indirect_dma_start(
                            out=net.node_r[:, :], out_offset=bass.IndirectOffsetOnAxis(ap=node[j][:, r:r + 1], axis=0),
                            in_=rows[j][:, r, :], in_offset=None,
                            bounds_check=NR - 1, oob_is_err=False).then_inc(sent[j], 16)
            for j in range(2):
                pool.wait_ge(sent[j], NPAIR * CH * 16)




class Norm:

    def __init__(self, net, c, name):
        nc = net.nc
        self.mean, self.var = tile(nc, c, name + "_mean", [P, G]), tile(nc, c, name + "_var", [P, G])
        self.square = tile(nc, c, name + "_square", [P, G, D])
        self.eps = tile(nc, c, name + "_eps", [P, 1])
        self.summed, self.rooted, self.ready = (net.sem(f"{name}_{n}") for n in ("summed", "rooted", "eps_ready"))

    STEPS = 6

    def start(self, dve):
        dve.memset(self.eps[:], EPS).then_inc(self.ready, 1)

    def vector(self, dve, st, x, n):
        st.did(dve.tensor_reduce(self.mean[:], x, AX.X, ALU.add))
        st.did(dve.tensor_scalar(self.mean[:], self.mean[:], -1.0 / D, None, ALU.mult))
        st.did(dve.tensor_tensor(x, x, spread(self.mean[:], 2, D), ALU.add))
        st.did(dve.tensor_tensor(self.square[:], x, x, ALU.mult))
        dve.tensor_reduce(self.var[:], self.square[:], AX.X, ALU.add).then_inc(self.summed, 1)
        dve.wait_ge(self.rooted, n + 1)
        st.did(dve.reciprocal(self.var[:], self.var[:]))
        st.did(dve.tensor_tensor(x, x, spread(self.var[:], 2, D), ALU.mult))

    def scalar(self, act, n):
        act.wait_ge(self.summed, n + 1)
        act.activation(self.var[:], self.var[:], ACT.Sqrt, bias=self.eps[:, 0:1], scale=1.0 / D).then_inc(self.rooted, 1)


def node_chunk(i, j):
    return bass.ds(i * (2 * G) + j * G, G)


def x1_phase(net, x):
    nc = net.nc
    with net.phase() as c:
        row = [tile(nc, c, f"x1_row{j}", [P, G, XW]) for j in range(2)]
        nr = [tile(nc, c, f"x1_nr{j}", [P, G, D]) for j in range(2)]
        norm = Norm(net, c, "x1")
        own, blank = net.sem("x1_own"), net.sem("x1_blank")
        sem2 = lambda n: [net.sem(f"x1_{n}{j}") for j in range(2)]
        loaded, summed, used, made, stored = (sem2(n) for n in ("loaded", "summed", "used", "made", "stored"))
        rows, sums, to = RealRows(x), node_view(net.node_r, D), node_view(net.x1_rows, XW)
        block = c.enter_context(nc.Block())

        @block.sync
        def _(sp):
            sp.wait_ge(blank, 2)
            for a, b, full in PARTS:
                with sp.Fori(a, b) as i:
                    for j in range(2):
                        sp.wait_ge(used[j], i)
                        sp.dma_start(nr[j][:], sums[:, node_chunk(i, j), :]).then_inc(summed[j], 16)
                        sp.wait_ge(stored[j], i * 16)
                        rows.move(sp, loaded[j], row[j][:, :, 0:D], node_chunk(i, j), full, False)

        @block.vector
        def _(dve):
            st = Steps(dve, own)
            norm.start(dve)
            for j in range(2):
                dve.memset(row[j][:], 0.0).then_inc(blank, 1)
            dve.wait_ge(blank, 2)
            for a, b, full in PARTS:
                with dve.Fori(a, b) as i:
                    st.enter(i - a, 2 * (3 + Norm.STEPS))
                    for j in range(2):
                        at, xr = node_chunk(i, j), row[j][:, :, 0:D]
                        dve.wait_ge(loaded[j], moved(i, full))
                        dve.wait_ge(summed[j], i * 16 + 16)
                        st.did(dve.tensor_tensor(xr, xr, spread(net.own_k[:, at], 2, D), ALU.mult))
                        st.did(dve.tensor_tensor(xr, xr, nr[j][:], ALU.add))
                        dve.sem_inc(used[j], 1)
                        norm.vector(dve, st, xr, i * 2 + j)
                        st.did(dve.tensor_copy(row[j][:, :, D], net.inv_deg[:, at]))
                        dve.sem_inc(made[j], 1)
                    st.leave(b - a)

        @block.scalar
        def _(act):
            act.wait_ge(norm.ready, 1)
            for a, b, full in PARTS:
                with act.Fori(a, b) as i:
                    for j in range(2):
                        norm.scalar(act, i * 2 + j)
                        act.wait_ge(made[j], i + 1)
                        act.dma_start(to[:, node_chunk(i, j), :], row[j][:]).then_inc(stored[j], 16)
            for j in range(2):
                act.wait_ge(stored[j], PAIRS * 16)


def gcn_edges_phase(net, o, mask, edge_attr):
    nc = net.nc
    with net.phase() as c:
        rec = [tile(nc, c, f"ge_rec{j}", [P, CH, 4], I32) for j in range(2)]
        node = [tile(nc, c, f"ge_node{j}", [P, CH], I32) for j in range(2)]
        xg = [tile(nc, c, f"ge_xg{j}", [P, CH, XW]) for j in range(2)]
        eg = [tile(nc, c, f"ge_eg{j}", [P, CH, ED]) for j in range(2)]
        msg = [tile(nc, c, f"ge_msg{j}", [P, AW, CH]) for j in range(2)]
        sums = [tile(nc, c, f"ge_sums{j}", [P, AW, CH]) for j in range(2)]
        rows = [tile(nc, c, f"ge_rows{j}", [P, CH, AW]) for j in range(2)]
        factor = tile(nc, c, "ge_factor", [P, CH])
        own, started, blank = net.sem("ge_own"), net.sem("ge_started"), net.sem("ge_blank")
        sem2 = lambda n: [net.sem(f"ge_{n}{j}") for j in range(2)]
        staged, gathered, used, edges_in, summed, rowed, sent = (
            sem2(n) for n in ("staged", "gathered", "used", "edges_in", "summed", "rowed", "sent"))
        fix = Fix(net, c, "ge", AW)
        block = c.enter_context(nc.Block())
        records = edge_view(o.records[1:EP + 1, :])

        @block.sync
        def _(sp):
            with sp.Fori(0, NPAIR) as i:
                for j in range(2):
                    sp.wait_ge(used[j], i)
                    sp.wait_ge(edges_in[j], i)
                    sp.dma_start(rec[j][:], records[:, bass.ds(chunk(i, j), CH), :]).then_inc(staged[j], 16)

        @block.gpsimd
        def _(pool):
            def gather(i, j):
                pool.wait_ge(staged[j], i * 16 + 16)
                pool.sem_inc(started, 1)
                for r in range(CH):
                    pool.indirect_dma_start(
                        out=xg[j][:, r, :], out_offset=None, in_=net.x1_rows[:, :],
                        in_offset=bass.IndirectOffsetOnAxis(ap=rec[j][:, r, 1:2], axis=0)).then_inc(gathered[j], 16)
                    pool.indirect_dma_start(
                        out=eg[j][:, r, :], out_offset=None, in_=edge_attr,
                        in_offset=bass.IndirectOffsetOnAxis(ap=rec[j][:, r, 3:4], axis=0),
                        bounds_check=E - 1, oob_is_err=False).then_inc(gathered[j], 16)

            def scatter(i, j):
                pool.wait_ge(rowed[j], i + 1)
                pool.sem_inc(started, 1)
                for r in range(CH):
                    pool.indirect_dma_start(
                        out=net.agg[:, :], out_offset=bass.IndirectOffsetOnAxis(ap=node[j][:, r:r + 1], axis=0),
                        in_=rows[j][:, r, :], in_offset=None,
                        bounds_check=NR - 1, oob_is_err=False).then_inc(sent[j], 16)

            pool.wait_ge(blank, 2)
            gather(0, 0)
            with pool.Fori(0, NPAIR - 1) as i:
                gather(i, 1)
                scatter(i, 0)
                gather(i + 1, 0)
                scatter(i, 1)
            gather(NPAIR - 1, 1)
            scatter(NPAIR - 1, 0)
            scatter(NPAIR - 1, 1)
            for j in range(2):
                pool.wait_ge(sent[j], NPAIR * CH * 16)
            fix.gpsimd(pool, 0, net.agg[:, :], o.fix_node[:], NR - 1)

        @block.vector
        def _(dve):
            st = Steps(dve, own)
            fix.blank(dve)
            for j in range(2):
                dve.memset(eg[j][:], 0.0).then_inc(blank, 1)
            st.did(dve.memset(sums[1][:, :, CH - 1:CH], 0.0))
            with dve.Fori(0, NPAIR) as i:
                st.enter(i, 2 * (3 + scan_steps(AW)))
                for j in range(2):
                    dve.wait_ge(gathered[j], i * (2 * CH * 16) + 2 * CH * 16)
                    st.did(dve.tensor_tensor(factor[:], rec[j][:, :, 2].bitcast(F32), xg[j][:, :, D], ALU.mult))
                    st.did(dve.tensor_tensor(msg[j][:, 0:D, :].rearrange("p f t -> p t f"), xg[j][:, :, 0:D],
                                             spread(factor[:], 2, D), ALU.mult))
                    dve.sem_inc(used[j], 1)
                    dve.wait_ge(edges_in[j], i + 1)
                    dve.wait_ge(rowed[j], i)
                    scan_chunk(dve, st, o, mask, msg[j], sums[j], sums[1 - j], i, j)
                    dve.wait_ge(sent[j], i * (CH * 16))
                    st.did(dve.tensor_copy(node[j][:], o.to_node[:, bass.ds(chunk(i, j), CH)]))
                    dve.sem_inc(summed[j], 1)
                st.leave(NPAIR)
            fix.vector(dve, 0)

        @block.scalar
        def _(act):
            def edges(i, j):
                act.wait_ge(gathered[j], i * (2 * CH * 16) + 2 * CH * 16)
                act.wait_ge(summed[j], i)
                act.activation(msg[j][:, D:AW, :].rearrange("p f t -> p t f"), eg[j][:], ACT.Copy).then_inc(edges_in[j], 1)

            with act.Fori(0, NPAIR) as i:
                for j in range(2):
                    edges(i, j)
                    act.wait_ge(summed[j], i + 1)
                    act.activation(rows[j][:], sums[j][:].rearrange("p f t -> p t f"), ACT.Copy).then_inc(rowed[j], 1)

        @block.tensor
        def _(pe):
            pe.wait_ge(summed[1], NPAIR)
            fix.tensor(pe, 0, o, sums[1][:, :, CH - 1])


def x2_phase(net, weight, bias):
    nc = net.nc
    with net.phase() as c:
        x1 = [tile(nc, c, f"x2_x1{j}", [P, G, XW]) for j in range(2)]
        ag = [tile(nc, c, f"x2_ag{j}", [P, G, D]) for j in range(2)]
        turned = [tile(nc, c, f"x2_turned{j}", [P, G // 2 * P]) for j in range(2)]
        y = [tile(nc, c, f"x2_y{j}", [P, G, D]) for j in range(2)]
        w = tile(nc, c, "x2_w", [P, 2 * D])
        bi = tile(nc, c, "x2_bias", [P, D])
        tb = [bank(nc, c, f"x2_tb{j}", [P, G // 2 * P]) for j in range(2)]
        mb = [bank(nc, c, f"x2_mb{j}", [P, G, D]) for j in range(2)]
        norm = Norm(net, c, "x2")
        own, weights, cleared = net.sem("x2_own"), net.sem("x2_weights"), net.sem("x2_cleared")
        sem2 = lambda n: [net.sem(f"x2_{n}{j}") for j in range(2)]
        loaded, tb_ready, turned_ready, mb_ready, used, made, stored = (
            sem2(n) for n in ("loaded", "tb_ready", "turned_ready", "mb_ready", "used", "made", "stored"))
        rows, sums, to = node_view(net.x1_rows, XW), node_view(net.agg, AW), node_view(net.x2, D)
        block = c.enter_context(nc.Block())

        @block.sync
        def _(sp):
            sp.wait_ge(cleared, 1)
            for h in range(2):
                sp.dma_start(w[h * D:(h + 1) * D, h * D:(h + 1) * D], weight).then_inc(weights, 16)
            sp.dma_start(bi[:], bias.partition_broadcast(P)).then_inc(weights, 16)
            with sp.Fori(0, PAIRS) as i:
                for j in range(2):
                    sp.wait_ge(used[j], i)
                    sp.dma_start(x1[j][:], rows[:, node_chunk(i, j), :]).then_inc(loaded[j], 16)
                    sp.dma_start(ag[j][:], sums[:, node_chunk(i, j), 0:D]).then_inc(loaded[j], 16)

        @block.tensor
        def _(pe):
            pe.wait_ge(weights, 3 * 16)

            def turn(i, j):
                pe.wait_ge(loaded[j], i * 32 + 32)
                pe.wait_ge(turned_ready[j], i)
                for q in range(G // 2):
                    last = pe.transpose(tb[j][:, q * P:(q + 1) * P], ag[j][:, 2 * q:2 * q + 2, :].rearrange("p g f -> p (g f)"), net.ident[:])
                last.then_inc(tb_ready[j], 1)

            def multiply(i, j):
                pe.wait_ge(turned_ready[j], i + 1)
                pe.wait_ge(used[j], i)
                for q in range(G // 2):
                    last = pe.matmul(mb[j][:, 2 * q:2 * q + 2, :], turned[j][:, q * P:(q + 1) * P], w[:],
                                     start=True, stop=True)
                last.then_inc(mb_ready[j], 1)

            with pe.Fori(0, PAIRS) as i:
                for j in range(2):
                    turn(i, j)
                for j in range(2):
                    multiply(i, j)

        @block.scalar
        def _(act):
            act.wait_ge(norm.ready, 1)
            with act.Fori(0, PAIRS) as i:
                for j in range(2):
                    act.wait_ge(tb_ready[j], i + 1)
                    act.wait_ge(mb_ready[j], i)
                    act.activation(turned[j][:], tb[j][:], ACT.Copy).then_inc(turned_ready[j], 1)
                for j in range(2):
                    norm.scalar(act, i * 2 + j)
                    act.wait_ge(made[j], i + 1)
                    act.dma_start(to[:, node_chunk(i, j), :], y[j][:]).then_inc(stored[j], 16)
            for j in range(2):
                act.wait_ge(stored[j], PAIRS * 16)

        @block.vector
        def _(dve):
            st = Steps(dve, own)
            norm.start(dve)
            dve.memset(w[:], 0.0).then_inc(cleared, 1)
            dve.wait_ge(weights, 3 * 16)
            with dve.Fori(0, PAIRS) as i:
                st.enter(i, 2 * (3 + Norm.STEPS))
                for j in range(2):
                    dve.wait_ge(mb_ready[j], i + 1)
                    dve.wait_ge(stored[j], i * 16)
                    st.did(dve.tensor_tensor(y[j][:], mb[j][:], spread(net.inv_deg[:, node_chunk(i, j)], 2, D), ALU.mult))
                    st.did(dve.tensor_tensor(y[j][:], y[j][:], x1[j][:, :, 0:D], ALU.add))
                    dve.sem_inc(used[j], 1)
                    st.did(dve.tensor_tensor(y[j][:], y[j][:], spread(bi[:], 1, G), ALU.add))
                    norm.vector(dve, st, y[j][:], i * 2 + j)
                    dve.sem_inc(made[j], 1)
                st.leave(PAIRS)




BIG = 1e38
QG = 4


def scores_phase(net, o, at_edges, attn_w, attn_b):
    nc = net.nc
    W3 = 3 * D
    with net.phase() as c:
        rec = [tile(nc, c, f"sc_rec{j}", [P, CH, 4], I32) for j in range(2)]
        xg = [tile(nc, c, f"sc_xg{j}", [P, CH, 2 * D]) for j in range(2)]
        turned = [tile(nc, c, f"sc_turned{j}", [P, QG * P]) for j in range(2)]
        qkv = [tile(nc, c, f"sc_qkv{j}", [P, QG, W3]) for j in range(2)]
        qk = tile(nc, c, "sc_qk", [P, QG * HEADS, HD])
        w = tile(nc, c, "sc_w", [P, W3])
        bi = tile(nc, c, "sc_bias", [P, W3])
        tb = [bank(nc, c, f"sc_tb{j}", [P, QG * P]) for j in range(2)]
        mb = [bank(nc, c, f"sc_mb{j}", [P, 2, 512]) for j in range(2)]
        own, started, weights, packed = (net.sem("sc_" + n) for n in ("own", "started", "weights", "packed"))
        sem2 = lambda n: [net.sem(f"sc_{n}{j}") for j in range(2)]
        staged, gathered, all_turned, tb_ready, turned_ready, mb_ready, mb_used, v_kept = (
            sem2(n) for n in ("staged", "gathered", "all_turned", "tb_ready", "turned_ready", "mb_ready",
                              "mb_used", "v_kept"))
        block = c.enter_context(nc.Block())
        records = edge_view(o.records[1:EP + 1, :])
        NG = CH // QG
        halfgroups = NG

        @block.sync
        def _(sp):
            for h in range(2):
                sp.dma_start(w[h * D:(h + 1) * D, :], attn_w).then_inc(weights, 16)
            sp.dma_start(bi[:], attn_b.partition_broadcast(P)).then_inc(weights, 16)
            with sp.Fori(0, NPAIR) as i:
                for j in range(2):
                    sp.wait_ge(gathered[j], i * (2 * CH * 16))
                    sp.dma_start(rec[j][:], records[:, bass.ds(chunk(i, j), CH), :]).then_inc(staged[j], 16)

        @block.gpsimd
        def _(pool):
            with pool.Fori(0, NPAIR) as i:
                for j in range(2):
                    pool.wait_ge(staged[j], i * 16 + 16)
                    pool.wait_ge(all_turned[j], i)
                    pool.sem_inc(started, 1)
                    for r in range(CH):
                        for h in range(2):
                            pool.indirect_dma_start(
                                out=xg[j][:, r, h * D:(h + 1) * D], out_offset=None, in_=net.x2[:, :],
                                in_offset=bass.IndirectOffsetOnAxis(ap=rec[j][:, r, h:h + 1], axis=0)).then_inc(gathered[j], 16)

        @block.tensor
        def _(pe):
            pe.wait_ge(packed, 1)

            def turn(i, k):
                j, b = k // NG, k % 2
                if k % NG == 0:
                    pe.wait_ge(gathered[j], i * (2 * CH * 16) + 2 * CH * 16)
                pe.wait_ge(turned_ready[b], i * halfgroups + k // 2)
                for q in range(QG):
                    last = pe.transpose(tb[b][:, q * P:(q + 1) * P], xg[j][:, (k % NG) * QG + q, :], net.ident[:])
                last.then_inc(tb_ready[b], 1)
                if k % NG == NG - 1:
                    pe.wait_ge(turned_ready[b], i * halfgroups + k // 2 + 1)
                    pe.sem_inc(all_turned[j], 1)

            def multiply(i, k):
                b = k % 2
                pe.wait_ge(turned_ready[b], i * halfgroups + k // 2 + 1)
                pe.wait_ge(mb_used[b], i * halfgroups + k // 2)
                for q in range(QG):
                    last = pe.matmul(mb[b][:, q // 2, (q % 2) * W3:(q % 2 + 1) * W3], turned[b][:, q * P:(q + 1) * P],
                                     w[:], start=True, stop=True)
                last.then_inc(mb_ready[b], 1)

            with pe.Fori(0, NPAIR) as i:
                turn(i, 0)
                for k in range(1, 2 * NG):
                    turn(i, k)
                    multiply(i, k - 1)
                multiply(i, 2 * NG - 1)

        @block.scalar
        def _(act):
            with act.Fori(0, NPAIR) as i:
                for k in range(2 * NG + 1):
                    if k < 2 * NG:
                        b = k % 2
                        act.wait_ge(tb_ready[b], i * halfgroups + k // 2 + 1)
                        act.wait_ge(mb_ready[b], i * halfgroups + k // 2)
                        act.activation(turned[b][:], tb[b][:], ACT.Copy).then_inc(turned_ready[b], 1)
                    if k:
                        b, t0 = (k - 1) % 2, i * (2 * CH) + (k - 1) * QG
                        act.wait_ge(mb_used[b], i * halfgroups + (k - 1) // 2 + 1)
                        act.activation(at_edges.v[:, bass.ds(t0, QG), :].rearrange("p t (h d) -> p (t h) d", h=HEADS),
                                       qkv[b][:].rearrange("p t (h x) -> p (t h) x", h=HEADS)[:, :, 2 * HD:3 * HD],
                                       ACT.Copy).then_inc(v_kept[b], 1)

        @block.vector
        def _(dve):
            st = Steps(dve, own)
            dve.wait_ge(weights, 3 * 16)
            heads = w[:].rearrange("p (h x) -> p h x", h=HEADS)
            st.did(dve.memset(heads[0:D, :, HD:3 * HD], 0.0))
            dve.memset(heads[D:2 * D, :, 0:HD], 0.0).then_inc(packed, 1)
            with dve.Fori(0, NPAIR) as i:
                st.enter(i, 2 * NG * 2)
                for k in range(2 * NG):
                    b, t0 = k % 2, i * (2 * CH) + k * QG
                    dve.wait_ge(mb_ready[b], i * halfgroups + k // 2 + 1)
                    dve.wait_ge(v_kept[b], i * halfgroups + k // 2)
                    for q in range(2):
                        ins = dve.tensor_tensor(qkv[b][:, 2 * q:2 * q + 2, :],
                                                mb[b][:, q, 0:2 * W3].rearrange("p (t x) -> p t x", t=2),
                                                spread(bi[:], 1, 2), ALU.add)
                    ins.then_inc(mb_used[b], 1)
                    dve.wait_ge(mb_used[b], i * halfgroups + k // 2 + 1)
                    x = qkv[b][:].rearrange("p t (h x) -> p (t h) x", h=HEADS)
                    st.did(dve.tensor_tensor(qk[:], x[:, :, 0:HD], x[:, :, HD:2 * HD], ALU.mult))
                    st.did(dve.tensor_reduce(at_edges.score[:, :, bass.ds(t0, QG)].rearrange("p h t -> p t h"),
                                             qk[:].rearrange("p (t h) d -> p t h d", t=QG), AX.X, ALU.add))
                st.leave(NPAIR)
            for b in range(2):
                dve.wait_ge(v_kept[b], NPAIR * halfgroups)


class AtEdges:

    def __init__(self, net, c):
        self.v = tile(net.nc, c, "ae_v", [P, T, D])
        self.score = tile(net.nc, c, "ae_score", [P, HEADS, T])


def softmax_phase(net, o, at_edges):
    nc = net.nc
    with net.phase() as c:
        most = tile(nc, c, "sm_most", [P, HEADS, T])
        fwd, bwd, keep_f, keep_b, lead, tail = (
            tile(nc, c, "sm_" + n, [P, T]) for n in ("fwd", "bwd", "keep_f", "keep_b", "lead", "tail"))
        ends = tile(nc, c, "sm_ends", [P, 2, HEADS])
        total = tile(nc, c, "sm_total", [P, 2, HEADS])
        key_diag = [tile(nc, c, f"sm_kdiag{e}", [P, P]) for e in range(2)]
        diag = [tile(nc, c, f"sm_diag{e}", [P, P]) for e in range(2)]
        same = [[tile(nc, c, f"sm_same{a}{b}", [P, P]) for b in range(2)] for a in range(2)]
        tmp = tile(nc, c, "sm_tmp", [P, 2, P])
        rb = [bank(nc, c, f"sm_rb{e}", [P, P]) for e in range(2)]
        own, diags, rows, scaled, done = (net.sem("sm_" + n) for n in ("own", "diags", "rows", "scaled", "done"))
        block = c.enter_context(nc.Block())
        ends_of = (slice(0, 1), slice(T - 1, T))

        @block.vector
        def _(dve):
            st = Steps(dve, own)
            st.did(dve.tensor_scalar(keep_f[:], o.cont[:], -1.0, BIG, ALU.add, ALU.mult))
            st.did(dve.memset(keep_b[:, T - 1:T], -BIG))
            st.did(dve.tensor_copy(keep_b[:, 0:T - 1], keep_f[:, 1:T]))
            for e, m in enumerate((lead, tail)):
                st.did(dve.tensor_scalar(m[:], o.key[:], o.key[:, ends_of[e]], None, ALU.is_equal))
                st.did(dve.tensor_scalar(m[:], m[:], -1.0, BIG, ALU.add, ALU.mult))
            for h in range(HEADS):
                s = at_edges.score[:, h, :]
                st.did(dve.tensor_tensor_scan(out=fwd[:], data0=keep_f[:], data1=s, initial=-BIG, op0=ALU.add, op1=ALU.max))
                st.did(dve.tensor_tensor_scan(out=bwd[:, ::-1], data0=keep_b[:, ::-1], data1=s[:, ::-1],
                                              initial=-BIG, op0=ALU.add, op1=ALU.max))
                dve.tensor_copy(ends[:, 0, h:h + 1], bwd[:, 0:1])
                dve.tensor_copy(ends[:, 1, h:h + 1], fwd[:, T - 1:T])
                st.did(dve.tensor_tensor(most[:, h, :], fwd[:], bwd[:], ALU.max))
            for e in range(2):
                dve.tensor_scalar(key_diag[e][:], net.ident[:], o.key[:, ends_of[e]], None, ALU.mult).then_inc(diags, 1)
            dve.wait_ge(rows, 1)
            for a in range(2):
                for b in range(2):
                    st.did(dve.tensor_scalar(same[a][b][:], rb[b][:], o.key[:, ends_of[a]], None, ALU.is_equal))
                    st.did(dve.tensor_scalar(same[a][b][:], same[a][b][:], -1.0, BIG, ALU.add, ALU.mult))
            for h in range(HEADS):
                for e in range(2):
                    dve.tensor_scalar(diag[e][:], net.ident[:], ends[:, e, h:h + 1], None, ALU.mult).then_inc(diags, 1)
                dve.wait_ge(rows, h + 2)
                for a in range(2):
                    for b in range(2):
                        ins = dve.tensor_tensor(tmp[:, b, :], same[a][b][:], rb[b][:], ALU.add)
                    st.did(ins)
                    st.did(dve.tensor_reduce(total[:, a, h:h + 1], tmp[:], AX.XY, ALU.max))
            for h in range(HEADS):
                m = most[:, h, :]
                st.did(dve.scalar_tensor_tensor(out=m, in0=lead[:], scalar=total[:, 0, h:h + 1], in1=m, op0=ALU.add, op1=ALU.max))
                st.did(dve.scalar_tensor_tensor(out=m, in0=tail[:], scalar=total[:, 1, h:h + 1], in1=m, op0=ALU.add, op1=ALU.max))
                dve.tensor_tensor(at_edges.score[:, h, :], at_edges.score[:, h, :], m, ALU.subtract).then_inc(scaled, 1)

        @block.tensor
        def _(pe):
            for n, two in enumerate([key_diag] + [diag] * HEADS):
                pe.wait_ge(diags, 2 * n + 2)
                for e in range(2):
                    last = pe.matmul(rb[e][:], net.ones[:], two[e][:], start=True, stop=True)
                last.then_inc(rows, 1)

        @block.scalar
        def _(act):
            for h in range(HEADS):
                act.wait_ge(scaled, h + 1)
                act.activation(at_edges.score[:, h, :], at_edges.score[:, h, :], ACT.Exp, scale=float(D) ** -0.5).then_inc(done, 1)


def attend_phase(net, o, mask, at_edges):
    nc = net.nc
    with net.phase() as c:
        node = [tile(nc, c, f"at_node{j}", [P, CH], I32) for j in range(2)]
        msg = tile(nc, c, "at_msg", [P, QW, CH])
        sums = [tile(nc, c, f"at_sums{j}", [P, QW, CH]) for j in range(2)]
        rows = [tile(nc, c, f"at_rows{j}", [P, CH, QW]) for j in range(2)]
        own, started = net.sem("at_own"), net.sem("at_started")
        sem2 = lambda n: [net.sem(f"at_{n}{j}") for j in range(2)]
        summed, rowed, sent = (sem2(n) for n in ("summed", "rowed", "sent"))
        fix = Fix(net, c, "at", QW)
        block = c.enter_context(nc.Block())

        @block.vector
        def _(dve):
            st = Steps(dve, own)
            fix.blank(dve)
            st.did(dve.memset(sums[1][:, :, CH - 1:CH], 0.0))
            with dve.Fori(0, NPAIR) as i:
                st.enter(i, 2 * (2 + scan_steps(QW)))
                for j in range(2):
                    at = bass.ds(chunk(i, j), CH)
                    e = at_edges.score[:, :, at]
                    dve.tensor_tensor(msg[:, 0:D, :].rearrange("p (h d) t -> p h t d", h=HEADS),
                                      at_edges.v[:, at, :].rearrange("p t (h d) -> p h t d", h=HEADS),
                                      spread(e, 3, HD), ALU.mult)
                    st.did(dve.tensor_copy(msg[:, D:QW, :], e))
                    dve.wait_ge(rowed[j], i)
                    scan_chunk(dve, st, o, mask, msg, sums[j], sums[1 - j], i, j)
                    dve.wait_ge(sent[j], i * (CH * 16))
                    st.did(dve.tensor_copy(node[j][:], o.to_node[:, at]))
                    dve.sem_inc(summed[j], 1)
                st.leave(NPAIR)
            fix.vector(dve, 0)

        @block.scalar
        def _(act):
            with act.Fori(0, NPAIR) as i:
                for j in range(2):
                    act.wait_ge(summed[j], i + 1)
                    act.activation(rows[j][:], sums[j][:].rearrange("p f t -> p t f"), ACT.Copy).then_inc(rowed[j], 1)

        @block.gpsimd
        def _(pool):
            with pool.Fori(0, NPAIR) as i:
                for j in range(2):
                    pool.wait_ge(rowed[j], i + 1)
                    pool.sem_inc(started, 1)
                    for r in range(CH):
                        pool.indirect_dma_start(
                            out=net.att[:, :], out_offset=bass.IndirectOffsetOnAxis(ap=node[j][:, r:r + 1], axis=0),
                            in_=rows[j][:, r, :], in_offset=None,
                            bounds_check=NR - 1, oob_is_err=False).then_inc(sent[j], 16)
            for j in range(2):
                pool.wait_ge(sent[j], NPAIR * CH * 16)
            fix.gpsimd(pool, 0, net.att[:, :], o.fix_node[:], NR - 1)

        @block.tensor
        def _(pe):
            pe.wait_ge(summed[1], NPAIR)
            fix.tensor(pe, 0, o, sums[1][:, :, CH - 1])



def last_phase(net, w, out):
    nc = net.nc
    CIN = D + ED
    with net.phase() as c:
        t2 = lambda n, shape: [tile(nc, c, f"la_{n}{j}", shape) for j in range(2)]
        x2, at, es, y, u, comb = (t2("x2", [P, G, D]), t2("at", [P, G, QW]), t2("es", [P, G, ED]),
                                  t2("y", [P, G, D]), t2("u", [P, G, D]), t2("comb", [P, G, P]))
        yT, hT, cT, h1, h2 = (t2("yT", [P, 4 * P]), t2("hT", [P, 4, 4 * P]), t2("cT", [P, 2, 4 * P]),
                              t2("h1", [P, 2, 4 * P]), t2("h2", [P, 2, 4 * P]))
        den = tile(nc, c, "la_den", [P, G, HEADS])
        vec = {n: tile(nc, c, "la_" + n, [P, D]) for n in ("g1", "be1", "g2", "be2", "b2", "mb3")}
        w1 = tile(nc, c, "la_w1", [P, FFN])
        w2 = tile(nc, c, "la_w2", [P, 2, D])
        fb1 = tile(nc, c, "la_fb1", [P, 2])
        mw1, mu, u0 = tile(nc, c, "la_mw1", [CIN, HID]), tile(nc, c, "la_mu", [UD, HID]), tile(nc, c, "la_graph0", [UD, 1])
        mw2, mw3 = tile(nc, c, "la_mw2", [HID, HID]), tile(nc, c, "la_mw3", [HID, D])
        mb1, mb2, mc1 = (tile(nc, c, "la_" + n, [HID, 1]) for n in ("mb1", "mb2", "mc1"))
        tb = [bank(nc, c, f"la_tb{k}", [P, 4 * P]) for k in range(2)]
        ring = [bank(nc, c, f"la_ring{k}", [P, 4 * P]) for k in range(4)]
        ob = [bank(nc, c, f"la_ob{k}", [P, G, D]) for k in range(2)]
        norm = Norm(net, c, "la")
        own, weights, ubias, ring_ready, ring_used, tb_ready, tb_used, blank = (
            net.sem("la_" + n) for n in ("own", "weights", "ubias", "ring_ready", "ring_used", "tb_ready", "tb_used", "blank"))
        sem2 = lambda n: [net.sem(f"la_{n}{j}") for j in range(2)]
        loaded, inputs_used, y_ready, ffn_ready, comb_ready, model_ready, made, stored = (
            sem2(n) for n in ("loaded", "inputs_used", "y_ready", "ffn_ready", "comb_ready", "model_ready", "made", "stored"))
        block = c.enter_context(nc.Block())
        x2_rows, at_rows, agg_rows, outs = node_view(net.x2, D), node_view(net.att, QW), node_view(net.agg, AW), RealRows(out)
        column = lambda ap: ap.rearrange("(k p) -> p k", p=P)
        LOADS = []

        @block.sync
        def _(sp):
            def load(to, of):
                LOADS.append(16)
                sp.dma_start(to, of).then_inc(weights, 16)

            for h in range(2):
                load(w1[h * D:(h + 1) * D, :], w["L2_gnn_w1"])
            load(w2[:], w["L2_gnn_w2"].rearrange("(k p) n -> p k n", p=P))
            load(mw1[:], w["L3_gnn_W1"][0:CIN, :])
            load(mu[:], w["L3_gnn_W1"][CIN:CIN + UD, :])
            load(mw2[:], w["L3_gnn_W2"])
            load(mw3[:], w["L3_gnn_W3"])
            with nc.allow_non_contiguous_dma(reason="columns of biases"):
                load(fb1[:], column(w["L2_gnn_b1"]))
                load(u0[:], w["L3_gnn_u"][0, :].rearrange("(p k) -> p k", k=1))
                load(mb1[:], column(w["L3_gnn_b1"]))
                load(mb2[:], column(w["L3_gnn_b2"]))
            for n, name in (("g1", "L2_gnn_ln1_g"), ("be1", "L2_gnn_ln1_b"), ("g2", "L2_gnn_ln2_g"),
                            ("be2", "L2_gnn_ln2_b"), ("b2", "L2_gnn_b2"), ("mb3", "L3_gnn_b3")):
                load(vec[n][:], w[name].partition_broadcast(P))
            with sp.Fori(0, PAIRS) as i:
                for j in range(2):
                    sp.wait_ge(inputs_used[j], i)
                    sp.dma_start(x2[j][:], x2_rows[:, node_chunk(i, j), :]).then_inc(loaded[j], 16)
                    sp.dma_start(at[j][:], at_rows[:, node_chunk(i, j), :]).then_inc(loaded[j], 16)
                    sp.dma_start(es[j][:], agg_rows[:, node_chunk(i, j), D:AW]).then_inc(loaded[j], 16)

        @block.tensor
        def _(pe):
            pe.wait_ge(weights, sum(LOADS))
            pe.matmul(ring[0][:, 0:1], mu[:], u0[:], start=True, stop=True).then_inc(ubias, 1)
            pe.wait_ge(ubias, 2)
            pe.sem_inc(ring_used, 4)

            def bank_of(i, n):
                pe.wait_ge(ring_used, i * 16 + n + 1)
                return ring[n % 4]

            def ffn(i, j):
                pe.wait_ge(y_ready[j], i + 1)
                pe.wait_ge(tb_used, i * 6 + j)
                for q in range(4):
                    last = pe.transpose(tb[0][:, q * P:(q + 1) * P], y[j][:, 2 * q:2 * q + 2, :].rearrange("p g f -> p (g f)"), net.ident[:])
                last.then_inc(tb_ready, 1)
                pe.wait_ge(tb_used, i * 6 + j + 1)
                for n in range(4):
                    h, m = n // 2, n % 2
                    pe.matmul(bank_of(i, j * 4 + n)[:], w1[h * D:(h + 1) * D, m * P:(m + 1) * P],
                              yT[j][h * D:(h + 1) * D, :], start=True, stop=True).then_inc(ring_ready, 1)
                pe.wait_ge(ring_used, i * 16 + j * 4 + 4 + 4)
                pe.wait_ge(made[j], i)
                for g in range(G):
                    h, q = g % 2, g // 2
                    for m in range(2):
                        last = pe.matmul(ob[j][:, g, :], hT[j][:, 2 * h + m, q * P:(q + 1) * P], w2[:, m, :],
                                         start=(m == 0), stop=(m == 1))
                last.then_inc(ffn_ready[j], 1)

            def model(i, j):
                pe.wait_ge(comb_ready[j], i + 1)
                pe.wait_ge(tb_used, i * 6 + 2 + 2 * j)
                for g in range(G):
                    last = pe.transpose(tb[g // 4][0:CIN, (g % 4) * P:(g % 4 + 1) * P], comb[j][:, g, 0:CIN], net.ident[:])
                    if g % 4 == 3:
                        last.then_inc(tb_ready, 1)
                pe.wait_ge(tb_used, i * 6 + 2 + 2 * j + 2)
                for k in range(2):
                    pe.matmul(bank_of(i, 8 + j * 4 + k)[:], mw1[:], cT[j][0:CIN, k, :], start=True, stop=True).then_inc(ring_ready, 1)
                for k in range(2):
                    pe.wait_ge(ring_used, i * 16 + 8 + j * 4 + k + 1 + 4)
                    pe.matmul(bank_of(i, 8 + j * 4 + 2 + k)[:], mw2[:], h1[j][:, k, :], start=True, stop=True).then_inc(ring_ready, 1)
                pe.wait_ge(ring_used, i * 16 + 8 + j * 4 + 4 + 4)
                for g in range(G):
                    last = pe.matmul(ob[j][:, g, :], h2[j][:, g // 4, (g % 4) * P:(g % 4 + 1) * P], mw3[:], start=True, stop=True)
                last.then_inc(model_ready[j], 1)

            with pe.Fori(0, PAIRS) as i:
                for j in range(2):
                    ffn(i, j)
                for j in range(2):
                    model(i, j)

        @block.scalar
        def _(act):
            act.wait_ge(norm.ready, 1)
            act.wait_ge(ubias, 1)
            act.activation(mc1[:], ring[0][:, 0:1], ACT.Identity, bias=mb1[:, 0:1]).then_inc(ubias, 1)

            def leave(i, n, to, bias):
                act.wait_ge(ring_ready, i * 16 + n + 1)
                act.activation(to, ring[n % 4][:], ACT.Relu, bias=bias).then_inc(ring_used, 1)

            def turn(full):
                def body(i):
                    for j in range(2):
                        norm.scalar(act, i * 8 + j)
                        act.wait_ge(tb_ready, i * 6 + j + 1)
                        act.activation(yT[j][:], tb[0][:], ACT.Copy).then_inc(tb_used, 1)
                        for n in range(4):
                            leave(i, j * 4 + n, hT[j][:, n, :], fb1[:, n % 2:n % 2 + 1])
                    for j in range(2):
                        norm.scalar(act, i * 8 + 2 + 2 * j)
                        norm.scalar(act, i * 8 + 2 + 2 * j + 1)
                        for k in range(2):
                            act.wait_ge(tb_ready, i * 6 + 2 + 2 * j + k + 1)
                            act.activation(cT[j][0:CIN, k, :], tb[k][0:CIN, :], ACT.Copy).then_inc(tb_used, 1)
                        for k in range(2):
                            leave(i, 8 + j * 4 + k, h1[j][:, k, :], mc1[:, 0:1])
                        for k in range(2):
                            leave(i, 8 + j * 4 + 2 + k, h2[j][:, k, :], mb2[:, 0:1])
                    for j in range(2):
                        norm.scalar(act, i * 8 + 6 + j)
                        act.wait_ge(made[j], i + 1)
                        outs.move(act, stored[j], y[j], node_chunk(i, j), full, True)
                return body

            for a, b, full in PARTS:
                body = turn(full)
                with act.Fori(a, b) as i:
                    body(i)
            for j in range(2):
                act.wait_ge(stored[j], moved(PAIRS - 1, False))

        @block.vector
        def _(dve):
            st = Steps(dve, own)
            norm.start(dve)
            dve.wait_ge(weights, sum(LOADS))

            def affine(x, scale, shift):
                st.did(dve.tensor_tensor(x, x, spread(vec[scale][:], 1, G), ALU.mult))
                st.did(dve.tensor_tensor(x, x, spread(vec[shift][:], 1, G), ALU.add))

            def attention(i, j, wait_stored):
                dve.wait_ge(loaded[j], i * 48 + 48)
                wait_stored(j)
                st.did(dve.tensor_scalar(den[:], at[j][:, :, D:QW], 1e-30, None, ALU.max))
                st.did(dve.reciprocal(den[:], den[:]))
                st.did(dve.tensor_tensor(y[j][:].rearrange("p g (h d) -> p g h d", h=HEADS),
                                         at[j][:, :, 0:D].rearrange("p g (h d) -> p g h d", h=HEADS),
                                         spread(den[:], 3, HD), ALU.mult))
                st.did(dve.tensor_tensor(y[j][:], y[j][:], x2[j][:], ALU.add))
                norm.vector(dve, st, y[j][:], i * 8 + j)
                affine(y[j][:], "g1", "be1")
                dve.sem_inc(y_ready[j], 1)

            def after_ffn(i, j):
                dve.wait_ge(ffn_ready[j], i + 1)
                st.did(dve.tensor_tensor(u[j][:], ob[j][:], y[j][:], ALU.add))
                st.did(dve.tensor_tensor(u[j][:], u[j][:], spread(vec["b2"][:], 1, G), ALU.add))
                norm.vector(dve, st, u[j][:], i * 8 + 2 + 2 * j)
                affine(u[j][:], "g2", "be2")
                x4 = comb[j][:, :, 0:D]
                st.did(dve.tensor_tensor(x4, u[j][:], x2[j][:], ALU.add))
                norm.vector(dve, st, x4, i * 8 + 2 + 2 * j + 1)
                st.did(dve.tensor_tensor(comb[j][:, :, D:CIN], es[j][:], spread(net.inv_count[:, node_chunk(i, j)], 2, ED), ALU.mult))
                dve.sem_inc(inputs_used[j], 1)
                dve.sem_inc(comb_ready[j], 1)

            def after_model(i, j):
                dve.wait_ge(model_ready[j], i + 1)
                st.did(dve.tensor_tensor(y[j][:], ob[j][:], comb[j][:, :, 0:D], ALU.add))
                st.did(dve.tensor_tensor(y[j][:], y[j][:], spread(vec["mb3"][:], 1, G), ALU.add))
                norm.vector(dve, st, y[j][:], i * 8 + 6 + j)
                dve.sem_inc(made[j], 1)

            for a, b, full in PARTS:
                with dve.Fori(a, b) as i:
                    st.enter(i - a, 2 * (4 + 2 + 4 * Norm.STEPS + 2 + 2 + 2 + 2))
                    for j in range(2):
                        attention(i, j, lambda j: dve.wait_ge(stored[j], moved(i, full, 0)))
                    for j in range(2):
                        after_ffn(i, j)
                    for j in range(2):
                        after_model(i, j)
                    st.leave(b - a)


def tables(net):
    net.records = net.dram("records", [EP, 4], I32)
    net.half_sorted = net.dram("half_sorted", [EP, 4], I32)
    net.orders = [net.dram(n, [EP + 2, 4], I32) for n in ("dst_records", "src_records")]
    net.by_dst, net.by_src = net.dram("by_dst", [NR, 2]), net.dram("by_src", [NR, 2])
    net.pairs = net.dram("pairs", [NR, 2])
    net.x_rows = net.dram("x_rows", [NR, XW])
    net.x1_rows = net.dram("x1_rows", [NR, XW])
    net.x2 = net.dram("x2", [NR, D])
    net.x_edges = net.dram("x_edges", [EP, D])
    net.slots = [net.dram(f"slots{k}", [TR, D]) for k in range(2)]
    net.slot_index = net.dram("slot_index", [P, T], I32)
    net.node_r = net.dram("node_r", [NR, D])
    net.agg = net.dram("agg", [NR, AW])
    net.att = net.dram("att", [NR, QW])


class Coefficients:

    def __init__(self, net, c):
        self.weight, self.src_part, self.dst_part, self.alpha = (
            tile(net.nc, c, "co_" + n, [P, T]) for n in ("weight", "src_part", "dst_part", "alpha"))
        self.mask = tile(net.nc, c, "co_mask", [P, 2 * NPAIR, MW * CH], BF16)


def gnn_kernel(nc, w, out, kinds=None):
    with ExitStack() as c:
        net = Net(nc, c)
        net.kinds = kinds or {}
        tables(net)
        constants(net, c)
        net.inv_deg, net.inv_count = tile(nc, c, "inv_deg", [P, NPP]), tile(nc, c, "inv_count", [P, NPP])
        by_source = Order(net, c, "os", net.orders[1], 0)

        with ExitStack() as c1:
            net.own_k = tile(nc, c1, "own_k", [P, NPP])
            by_dest = Order(net, c1, "od", net.orders[0], 1)
            with ExitStack() as c2:
                net.zeros = tile(nc, c2, "zeros", [P, ZW])
                setup_phase(net, w["src"], w["dst"], w["edge_weight"])
                zero = zero_parts(net)
                for n, (name, table, key) in enumerate((("sd", net.orders[0], 1), ("ss", net.orders[1], 0))):
                    sort_pass(net, name + "l", net.records, net.half_sorted, key, False, zero[2 * n::4])
                    sort_pass(net, name + "h", net.half_sorted, table, key, True, zero[2 * n + 1::4])
                order_phase(net, by_source, net.by_src, "count")
                order_phase(net, by_dest, net.by_dst, "slot")
            with ExitStack() as c2:
                net.inv_out, net.inv_in, net.own_part, net.slot1 = (
                    tile(nc, c2, n, [P, NPP]) for n in ("inv_out", "inv_in", "own_part", "slot1"))
                node_scalars_phase(net)
                x_rows_phase(net, w["x"])
            with ExitStack() as c2:
                co = Coefficients(net, c2)
                mask_phase(net, by_dest, co.mask)
                appnp_first_phase(net, by_dest, co)
                appnp_steps_phase(net, by_dest, co)
            to_nodes_phase(net, by_dest)
            x1_phase(net, w["x"])

        mask = tile(nc, c, "src_mask", [P, 2 * NPAIR, MW * CH], BF16)
        mask_phase(net, by_source, mask)
        gcn_edges_phase(net, by_source, mask, w["edge_attr_48"])
        x2_phase(net, w["L1_gnn_weight"], w["L1_gnn_bias"])

        with ExitStack() as c3:
            at_edges = AtEdges(net, c3)
            scores_phase(net, by_source, at_edges, w["L2_gnn_attn_w"], w["L2_gnn_attn_b"])
            softmax_phase(net, by_source, at_edges)
            attend_phase(net, by_source, mask, at_edges)

        last_phase(net, w, out)


INS = ["x", "src", "dst", "edge_attr_48", "edge_weight", "L1_gnn_weight", "L1_gnn_bias",
       "L2_gnn_attn_w", "L2_gnn_attn_b", "L2_gnn_w1", "L2_gnn_b1", "L2_gnn_w2", "L2_gnn_b2",
       "L2_gnn_ln1_g", "L2_gnn_ln1_b", "L2_gnn_ln2_g", "L2_gnn_ln2_b",
       "L3_gnn_u", "L3_gnn_W1", "L3_gnn_b1", "L3_gnn_W2", "L3_gnn_b2", "L3_gnn_W3", "L3_gnn_b3"]


def kernel(**inputs):
    import numpy as np
    import concourse.bacc as bacc
    from concourse.bass_utils import run_bass_kernel_spmd

    nc = bacc.Bacc("TRN2", target_bir_lowering=False, num_devices=1)
    arrays, w = {}, {}
    for name in INS:
        a = np.ascontiguousarray(inputs[name])
        arrays[f"in_{name}_dram"] = a
        w[name] = nc.dram_tensor(f"in_{name}_dram", a.shape, mybir.dt.from_np(a.dtype), kind="ExternalInput").ap()
    out = nc.dram_tensor("out_0_dram", (N, D), F32, kind="ExternalOutput").ap()
    gnn_kernel(nc, w, out)
    r = run_bass_kernel_spmd(nc, [arrays], core_ids=[0])
    return r.results[0]["out_0_dram"]
```

```python
import concourse.bass as bass
from concourse import mybir
from concourse.alu_op_type import AluOpType as ALU
from contextlib import ExitStack, contextmanager

F32, I32, F16, BF16 = mybir.dt.float32, mybir.dt.int32, mybir.dt.float16, mybir.dt.bfloat16
ACT = mybir.ActivationFunctionType
AX = mybir.AxisListType

P = 128
D = 64
ED = 48
N, E = 100000, 50000
HEADS, HD = 8, 8
FFN, HID, UD = 256, 128, 32
K_STEPS = 10
EPS = 1e-5
CH = 28
T = -(-E // (P * 2 * CH)) * 2 * CH
NPAIR = T // (2 * CH)
EP = P * T
G = 8
NPP = -(-N // (P * 2 * G)) * 2 * G
NR = P * NPP
NLAST = N - (P - 1) * NPP
PAIRS_FULL = NLAST // (2 * G)
PAIRS = NPP // (2 * G)
SKIP = 1 << 20
ZROW = EP
TR = EP + P
LOBITS = 9
NB_LO, NB_HI = 1 << LOBITS, (N >> LOBITS) + 1
XW = D + 4
AW = D + ED
QW = D + HEADS
RING = 7
DH, DL = 16, 32
DC = P // DH
ZW = NPP * 8


class Steps:

    def __init__(self, eng, sem):
        self.eng, self.sem, self.base, self.n = eng, sem, 0, 0

    def enter(self, i, per):
        self.outer, self.start, self.per, self.n = (self.base, self.n), self.n, per, 0
        self.base = self.base + self.start + i * per

    def leave(self, turns):
        assert self.n == self.per, f"{self.n} steps in a turn, not {self.per}"
        self.base, self.n = self.outer[0], self.outer[1] + turns * self.per

    def mark(self, ins):
        ins.then_inc(self.sem, 1)
        self.n += 1
        return self.n

    def did(self, ins):
        self.mark(ins)
        self.wait()

    def wait(self):
        self.upto(self.n)

    def upto(self, n):
        self.eng.wait_ge(self.sem, self.base + n)


def spread(ap, axis, count):
    v = ap.unsqueeze(axis)
    shape = list(v.shape)
    shape[axis] = count
    return v.to_broadcast(shape)


def halves(eng, sem, tile_of, dram_of, store):
    for a, b in ((0, P - P // 8), (P - P // 8, P - 1)):
        if store:
            eng.dma_start(dram_of(a, b), tile_of(a, b)).then_inc(sem, 16)
        else:
            eng.dma_start(tile_of(a, b), dram_of(a, b)).then_inc(sem, 16)


class Net:

    def __init__(self, nc, ctx):
        self.nc, self.ctx = nc, ctx

    own = None

    def sem(self, name):
        if self.own is None:
            return self.ctx.enter_context(self.nc.semaphore(name))
        self.own.append(self.nc.alloc_semaphore(name=name))
        return self.own[-1]

    @contextmanager
    def phase(self):
        self.own = []
        with ExitStack() as c:
            yield c
        self.nc.clear_and_free_semaphores(self.own)
        self.nc.all_engine_barrier()
        self.own = None

    def dram(self, name, shape, dt=F32):
        return self.nc.dram_tensor(name, shape, dt, kind=self.kinds.get(name, "Internal")).ap()

    kinds = {}


def tile(nc, ctx, name, shape, dt=F32):
    return ctx.enter_context(nc.sbuf_tensor(name, shape, dt))


def bank(nc, ctx, name, shape, dt=F32):
    return ctx.enter_context(nc.psum_tensor(name, shape, dt))



def constants(net, c):
    nc = net.nc
    net.ident = tile(nc, c, "ident", [P, P])
    net.upper = tile(nc, c, "upper", [P, P])
    net.ones = tile(nc, c, "ones", [P, P])
    net.part = tile(nc, c, "part", [P, 1])
    net.minus = tile(nc, c, "minus", [1, 4], I32)
    net.iota16 = tile(nc, c, "iota16", [P, NB_LO], F16)
    net.zero16, net.ones16, net.upper16, net.lower16 = (
        tile(nc, c, n, [P, P], F16) for n in ("zero16", "ones16", "upper16", "lower16"))
    net.zero_tile, net.zeroed = net.sem("zero_tile"), net.sem("zeroed")


def setup_phase(net, src, dst, edge_weight):
    nc = net.nc
    with net.phase() as c:
        s_in = tile(nc, c, "su_src", [P, T], I32)
        d_in = tile(nc, c, "su_dst", [P, T], I32)
        w_in = tile(nc, c, "su_w", [P, T])
        e_no = tile(nc, c, "su_no", [P, T], I32)
        rec = tile(nc, c, "su_rec", [P, T, 4], I32)
        iota_lo = tile(nc, c, "su_iota", [P, NB_LO])
        padded, loaded, made, const, stored, drawn = (
            net.sem("su_" + n) for n in ("padded", "loaded", "made", "const", "stored", "drawn"))
        block = c.enter_context(nc.Block())

        @block.gpsimd
        def _(pool):
            pool.iota(e_no[:], pattern=[[1, T]], base=0, channel_multiplier=T).then_inc(const, 1)
            pool.iota(iota_lo[:], pattern=[[1, NB_LO]], base=0, channel_multiplier=0,
                      allow_small_or_imprecise_dtypes=True).then_inc(const, 1)
            pool.iota(net.part[:], pattern=[[0, 1]], base=0, channel_multiplier=1,
                      allow_small_or_imprecise_dtypes=True).then_inc(const, 1)
            pool.memset(net.ones[:], 1.0).then_inc(const, 1)
            pool.wait_ge(const, 4)
            pool.affine_select(out=net.ident[:], in_=net.ones[:], compare_op=ALU.is_equal, fill=0.0,
                               base=0, pattern=[[-1, P]], channel_multiplier=1).then_inc(const, 1)
            pool.affine_select(out=net.upper[:], in_=net.ones[:], compare_op=ALU.is_gt, fill=0.0,
                               base=0, pattern=[[1, P]], channel_multiplier=-1).then_inc(const, 1)

        @block.vector
        def _(dve):
            dve.memset(s_in[:], N)
            dve.memset(d_in[:], N)
            dve.memset(w_in[:], 0.0).then_inc(padded, 1)
            dve.memset(net.minus[:], -1)
            dve.memset(net.zeros[:], 0.0).then_inc(net.zero_tile, 1)
            dve.memset(net.zero16[:], 0.0)
            dve.memset(net.ones16[:], 1.0)
            dve.wait_ge(const, 6)
            dve.tensor_copy(net.iota16[:], iota_lo[:])
            dve.tensor_copy(net.upper16[:], net.upper[:])
            dve.tensor_scalar(net.lower16[:], net.upper[:], -1.0, 1.0, ALU.mult, ALU.add)
            dve.tensor_copy(rec[:, :, 3], e_no[:])
            dve.wait_ge(loaded, 9 * 16)
            dve.tensor_copy(rec[:, :, 0], s_in[:])
            dve.tensor_copy(rec[:, :, 1], d_in[:])
            dve.tensor_copy(rec[:, :, 2].bitcast(F32), w_in[:]).then_inc(made, 1)

        @block.sync
        def _(sp):
            sp.wait_ge(padded, 1)
            whole = (P - 1) * T
            for ap, to in ((src, s_in), (dst, d_in), (edge_weight, w_in)):
                rows = ap[0:whole].rearrange("(p t) -> p t", t=T)
                halves(sp, loaded, lambda a, b: to[a:b, :], lambda a, b: rows[a:b, :], False)
                sp.dma_start(to[P - 1:P, 0:E - whole],
                             ap[whole:E].rearrange("(p t) -> p t", p=1)).then_inc(loaded, 16)
            sp.wait_ge(made, 1)
            sp.dma_start(net.records[:, :].rearrange("(p t) c -> p t c", p=P), rec[:]).then_inc(stored, 16)
            sp.wait_ge(stored, 16)

        @block.scalar
        def _(act):
            act.wait_ge(net.zero_tile, 1)
            for table in net.orders:
                for row in (0, EP + 1):
                    act.dma_start(table[row:row + 1, :], net.minus[0:1, :]).then_inc(drawn, 16)
            act.wait_ge(drawn, 4 * 16)



def zero_parts(net):
    parts = []
    for table, w in ((net.by_dst, 2), (net.by_src, 2), (net.node_r, D), (net.agg, AW), (net.att, QW)):
        flat = table[:, :].rearrange("(p g) c -> p (g c)", p=P)
        for a in range(0, NPP * w, ZW):
            b = min(a + ZW, NPP * w)
            parts.append((flat[:, a:b], b - a))
    for k in range(2):
        parts.append((net.slots[k][EP:TR, :].rearrange("(p z) c -> p (z c)", p=P), D))
    net.zeroed_all = 16 * len(parts)
    return parts


def sort_pass(net, name, source, dest, key, high, zero):
    nc = net.nc
    nb = NB_HI if high else NB_LO
    with net.phase() as c:
        rec = tile(nc, c, name + "rec", [P, T, 4], I32)
        digit = tile(nc, c, name + "digit", [P, T], I32)
        digitf = tile(nc, c, name + "digitf", [P, T + 2])
        part = [tile(nc, c, name + f"part{k}", [P, T], I32) for k in range(2)]
        partf = [tile(nc, c, name + f"partf{k}", [P, T], F16) for k in range(2)]
        hot_up, hot_low = tile(nc, c, name + "hot_up", [P, T, DH], F16), tile(nc, c, name + "hot_low", [P, T, DL], F16)
        upto, before = tile(nc, c, name + "upto", [DH, DL]), tile(nc, c, name + "before", [DH, DL])
        rows_before = tile(nc, c, name + "rows_before", [DH, DH])
        base, base2 = tile(nc, c, name + "base", [DH, DH, DL]), tile(nc, c, name + "base2", [DH, DH, DL])
        same, fold = tile(nc, c, name + "same", [P, DC]), tile(nc, c, name + "fold", [P, DH])
        own_part, by_row = tile(nc, c, name + "own_part", [P, DC, DL]), tile(nc, c, name + "by_row", [P, DL])
        cross = bank(nc, c, name + "cross", [P, DC, DL])
        counts = bank(nc, c, name + "counts", [DH, DL])
        hot = [tile(nc, c, name + f"hot{r}", [P, nb], F16) for r in range(RING)]
        junk = [tile(nc, c, name + f"junk{r}", [P, nb]) for r in range(2)]
        rank = [tile(nc, c, name + f"rank{j}", [P, CH]) for j in range(2)]
        ranki = [tile(nc, c, name + f"ranki{j}", [P, CH], I32) for j in range(2)]
        low = [tile(nc, c, name + f"low{j}", [P, CH], I32) for j in range(2)]
        row = [tile(nc, c, name + f"row{j}", [P, CH], I32) for j in range(2)]
        stage = [tile(nc, c, name + f"stage{j}", [P, CH, 4], I32) for j in range(2)]
        acc = [bank(nc, c, name + f"acc{b}", [P, 512]) for b in range(2)]
        loaded, own, parts_ready, crossed, folding, counted, base_ready, hot_ready, ranked, read, started = (
            net.sem(name + n) for n in ("loaded", "own", "parts_ready", "crossed", "folding", "counted",
                                        "base_ready", "hot_ready", "ranked", "read", "started"))
        rows_ready = [net.sem(name + f"rows{j}") for j in range(2)]
        staged = [net.sem(name + f"staged{j}") for j in range(2)]
        sent = [net.sem(name + f"sent{j}") for j in range(2)]
        block = c.enter_context(nc.Block())
        records = source.rearrange("(p t) c -> p t c", p=P)
        COUNTED = 7

        @block.scalar
        def _(act):
            act.wait_ge(loaded, 16)
            for table, width in zero:
                act.dma_start(table, net.zeros[:, 0:width]).then_inc(net.zeroed, 16)

        @block.sync
        def _(sp):
            sp.dma_start(rec[:], records).then_inc(loaded, 16)
            with sp.Fori(0, NPAIR) as i:
                for j in range(2):
                    sp.wait_ge(sent[j], i * (16 * CH))
                    sp.dma_start(stage[j][:], records[:, bass.ds(i * (2 * CH) + j * CH, CH), :]).then_inc(staged[j], 16)

        @block.vector
        def _(dve):
            st = Steps(dve, own)
            for t in (RING - 2, RING - 1):
                dve.memset(hot[t][:], 0.0)
            dve.memset(digitf[:, T:T + 2], 0.0)
            dve.wait_ge(loaded, 16)
            op, n = (ALU.arith_shift_right, LOBITS) if high else (ALU.bitwise_and, NB_LO - 1)
            st.did(dve.tensor_scalar(digit[:], rec[:, :, key], n, None, op))
            st.did(dve.tensor_copy(digitf[:, 0:T], digit[:]))
            dve.tensor_scalar(part[0][:], digit[:], 5, None, ALU.arith_shift_right)
            st.did(dve.tensor_scalar(part[1][:], digit[:], DL - 1, None, ALU.bitwise_and))
            for k in range(2):
                st.did(dve.tensor_copy(partf[k][:], part[k][:]))
            for k, (hots, width) in enumerate(((hot_up, DH), (hot_low, DL))):
                dve.tensor_tensor(hots[:], spread(partf[k][:], 2, width), spread(net.iota16[:, 0:width], 1, T),
                                  ALU.is_equal).then_inc(parts_ready, 1)
            blocks = net.ident[:].rearrange("p (c h) -> p c h", h=DH)
            dve.tensor_reduce(same[:], blocks, AX.X, ALU.add)
            st.did(dve.tensor_reduce(fold[:], blocks.rearrange("p c h -> p h c"), AX.X, ALU.add))
            dve.wait_ge(crossed, T // DC)
            st.did(dve.tensor_tensor(own_part[:], cross[:], spread(same[:], 2, DL), ALU.mult))
            dve.tensor_reduce(by_row[:], own_part[:].rearrange("p c l -> p l c"), AX.X, ALU.add).then_inc(folding, 1)
            dve.wait_ge(counted, 1)
            st.did(dve.tensor_tensor_scan(out=upto[:], data0=net.ones[0:DH, 0:DL], data1=counts[:], initial=0.0,
                                          op0=ALU.mult, op1=ALU.add))
            st.did(dve.tensor_tensor(before[:], upto[:], counts[:], ALU.subtract))
            st.did(dve.tensor_scalar(rows_before[:], net.upper[0:DH, 0:DH], upto[:, DL - 1:DL], None, ALU.mult))
            st.did(dve.tensor_tensor(base[:], spread(before[:], 1, DH), spread(net.ident[0:DH, 0:DH], 2, DL), ALU.mult))
            st.did(dve.tensor_tensor(base2[:], base[:], spread(rows_before[:], 2, DL), ALU.add))
            dve.sem_inc(base_ready, 1)

            def one_hot(r, t):
                dve.tensor_scalar(hot[r][:], net.iota16[:, 0:nb], digitf[:, bass.ds(t, 1)], None,
                                  ALU.is_equal).then_inc(hot_ready, 1)

            one_hot(0, 0)
            one_hot(1, 1)
            with dve.Fori(0, NPAIR) as i:
                st.enter(i, 2 * (1 if high else 3))
                for j in range(2):
                    dve.wait_ge(sent[j], i * (16 * CH))
                    for u in range(j * CH, (j + 1) * CH):
                        one_hot((u + 2) % RING, i * (2 * CH) + (u + 2))
                        dve.wait_ge(ranked, i * (2 * CH) + (u + 1))
                        dve.scalar_tensor_tensor(out=junk[u % 2][:], in0=hot[u % RING][:], scalar=1.0,
                                                 in1=acc[u % 2][:, 0:nb], op0=ALU.mult, op1=ALU.mult,
                                                 accum_out=rank[j][:, u % CH:u % CH + 1]).then_inc(read, 1)
                    dve.wait_ge(read, i * (2 * CH) + (j + 1) * CH + 2)
                    if high:
                        st.did(dve.tensor_scalar(rank[j][:], rank[j][:], 1.0, None, ALU.add))
                        dve.tensor_copy(row[j][:], rank[j][:]).then_inc(rows_ready[j], 1)
                    else:
                        st.did(dve.tensor_copy(ranki[j][:], rank[j][:]))
                        st.did(dve.tensor_scalar(low[j][:], ranki[j][:], P - 1, None, ALU.bitwise_and))
                        st.did(dve.tensor_scalar(ranki[j][:], ranki[j][:], 7, None, ALU.arith_shift_right))
                        dve.scalar_tensor_tensor(out=row[j][:], in0=low[j][:], scalar=float(T), in1=ranki[j][:],
                                                 op0=ALU.mult, op1=ALU.add).then_inc(rows_ready[j], 1)
                st.leave(NPAIR)

        @block.tensor
        def _(pe):
            pe.wait_ge(parts_ready, 2)

            def cross_product(n, first):
                cols = bass.ds(n * DC, DC)
                pe.matmul(cross[:], hot_up[:, cols, :].rearrange("p c h -> p (c h)"), hot_low[:, cols, :],
                          start=first, stop=False, skip_group_check=True).then_inc(crossed, 1)

            for n in range(COUNTED):
                cross_product(n, n == 0)
            with pe.Fori(1, T // (DC * COUNTED)) as i:
                for n in range(COUNTED):
                    cross_product(i * COUNTED + n, False)
            pe.wait_ge(folding, 1)
            pe.matmul(counts[:], fold[:], by_row[:], start=True, stop=True).then_inc(counted, 1)
            pe.wait_ge(base_ready, 1)
            for b in range(2):
                pe.matmul(acc[b][:, 0:nb], net.ones[0:DH, :], base2[:].rearrange("p h l -> p (h l)")[:, 0:nb], start=True, stop=False, skip_group_check=True)
            pe.sem_inc(read, 2)
            with pe.Fori(0, NPAIR) as i:
                for u in range(2 * CH):
                    a = acc[u % 2][:, 0:nb]
                    pe.wait_ge(hot_ready, i * (2 * CH) + u + 1)
                    pe.wait_ge(read, i * (2 * CH) + u + 1)
                    pe.matmul(a, net.lower16[:], hot[(u - 2) % RING][:], start=False, stop=False, skip_group_check=True)
                    pe.matmul(a, net.ones16[:], hot[(u - 1) % RING][:], start=False, stop=False, skip_group_check=True)
                    pe.matmul(a, net.upper16[:], hot[u % RING][:], start=False, stop=True, skip_group_check=True).then_inc(ranked, 1)

        @block.gpsimd
        def _(pool):
            with pool.Fori(0, NPAIR) as i:
                for j in range(2):
                    pool.wait_ge(rows_ready[j], i + 1)
                    pool.wait_ge(staged[j], i * 16 + 16)
                    pool.sem_inc(started, 1)
                    for r in range(CH):
                        pool.indirect_dma_start(
                            out=dest, out_offset=bass.IndirectOffsetOnAxis(ap=row[j][:, r:r + 1], axis=0),
                            in_=stage[j][:, r, :], in_offset=None).then_inc(sent[j], 16)
            for j in range(2):
                pool.wait_ge(sent[j], NPAIR * CH * 16)



class Order:

    def __init__(self, net, c, name, records, key):
        nc = net.nc
        self.name, self.records, self.key_col = name, records, key
        self.cont = tile(nc, c, name + "_cont", [P, T])
        self.key = tile(nc, c, name + "_key", [P, T])
        self.scan = tile(nc, c, name + "_scan", [P, T])
        self.to_node = tile(nc, c, name + "_to_node", [P, T], I32)
        self.carry = tile(nc, c, name + "_carry", [P, P])
        self.fix_node = tile(nc, c, name + "_fix_node", [P, 1], I32)
        self.fix_slot = tile(nc, c, name + "_fix_slot", [P, 1], I32)


def order_phase(net, o, table, second):
    nc = net.nc
    name = o.name
    with net.phase() as c:
        rec, prev, nxt = (tile(nc, c, name + n, [P, T, 4], I32) for n in ("rec", "prev", "nxt"))
        key = o.key
        pkey, nkey, t1, last, lead, deg, num = (
            tile(nc, c, name + n, [P, T]) for n in ("pkey", "nkey", "t1", "last", "lead", "deg", "num"))
        diag = tile(nc, c, name + "diag", [P, P])
        fixf, ends, cnt, s1 = (tile(nc, c, name + n, [P, 1]) for n in ("fixf", "ends", "cnt", "s1"))
        tail = tile(nc, c, name + "tail", [P, 2])
        carried = tile(nc, c, name + "carried", [P, 2])
        slot = tile(nc, c, name + "slot", [P, T])
        stage = [tile(nc, c, name + f"stage{j}", [P, CH, 2]) for j in range(2)]
        row = [tile(nc, c, name + f"row{j}", [P, CH], I32) for j in range(2)]
        kb = bank(nc, c, name + "kb", [P, P])
        cb = bank(nc, c, name + "cb", [P, 2])
        loaded, own, diag_ready, key_rows, tail_ready, carry_ready, iotas, started = (
            net.sem(name + n) for n in ("loaded", "own", "diag_ready", "key_rows", "tail_ready",
                                        "carry_ready", "iotas", "started"))
        staged = [net.sem(name + f"staged{j}") for j in range(2)]
        sent = [net.sem(name + f"sent{j}") for j in range(2)]
        block = c.enter_context(nc.Block())

        @block.sync
        def _(sp):
            for k, to in enumerate((prev, rec, nxt)):
                sp.dma_start(to[:], o.records[k:k + EP, :].rearrange("(p t) c -> p t c", p=P)).then_inc(loaded, 16)

        @block.vector
        def _(dve):
            st = Steps(dve, own)
            dve.wait_ge(loaded, 3 * 16)
            dve.tensor_copy(pkey[:], prev[:, :, o.key_col])
            dve.tensor_copy(nkey[:], nxt[:, :, o.key_col])
            st.did(dve.tensor_copy(key[:], rec[:, :, o.key_col]))
            dve.tensor_tensor(o.cont[:], key[:], pkey[:], ALU.is_equal)
            dve.tensor_tensor(last[:], key[:], nkey[:], ALU.not_equal)
            st.did(dve.tensor_scalar(lead[:], key[:], key[:, 0:1], None, ALU.is_equal))
            st.did(dve.tensor_copy(o.scan[:], o.cont[:]))
            st.did(dve.memset(o.scan[:].rearrange("p (c t) -> p c t", t=CH)[:, :, 0:1], 0.0))
            st.did(dve.tensor_scalar(t1[:], key[:], float(SKIP), None, ALU.subtract))
            st.did(dve.tensor_tensor(t1[:], t1[:], last[:], ALU.mult))
            st.did(dve.tensor_scalar(o.to_node[:], t1[:], float(SKIP), None, ALU.add))
            st.did(dve.tensor_scalar(diag[:], net.ident[:], key[:, 0:1], None, ALU.mult))
            dve.sem_inc(diag_ready, 1)
            dve.wait_ge(key_rows, 1)
            st.did(dve.tensor_scalar(diag[:], kb[:], key[:, T - 1:T], None, ALU.is_equal))
            st.did(dve.tensor_tensor(o.carry[:], diag[:], net.upper[:], ALU.mult))
            st.did(dve.tensor_reduce(cnt[:], lead[:], AX.X, ALU.add))
            st.did(dve.tensor_tensor(ends[:], key[:, 0:1], nkey[:, T - 1:T], ALU.not_equal))
            st.did(dve.tensor_tensor(ends[:], ends[:], o.cont[:, 0:1], ALU.mult))
            st.did(dve.tensor_scalar(fixf[:], key[:, 0:1], float(SKIP), None, ALU.subtract))
            st.did(dve.tensor_tensor(fixf[:], fixf[:], ends[:], ALU.mult))
            dve.tensor_scalar(o.fix_node[:], fixf[:], float(SKIP), None, ALU.add)
            st.did(dve.tensor_scalar(s1[:], net.part[:], float(T), float(-1 - SKIP), ALU.mult, ALU.add))
            st.did(dve.tensor_tensor(s1[:], s1[:], cnt[:], ALU.add))
            st.did(dve.tensor_tensor(s1[:], s1[:], ends[:], ALU.mult))
            st.did(dve.tensor_scalar(o.fix_slot[:], s1[:], float(SKIP), None, ALU.add))
            weight = rec[:, :, 2].bitcast(F32)
            st.did(dve.tensor_tensor_scan(out=deg[:], data0=o.cont[:], data1=weight, initial=0.0,
                                          op0=ALU.mult, op1=ALU.add))
            if second == "count":
                st.did(dve.memset(t1[:], 1.0))
                st.did(dve.tensor_tensor_scan(out=num[:], data0=o.cont[:], data1=t1[:], initial=0.0,
                                              op0=ALU.mult, op1=ALU.add))
                st.did(dve.tensor_copy(tail[:, 1:2], num[:, T - 1:T]))
            else:
                st.did(dve.memset(tail[:, 1:2], 0.0))
                dve.wait_ge(iotas, 1)
            st.did(dve.tensor_copy(tail[:, 0:1], deg[:, T - 1:T]))
            dve.sem_inc(tail_ready, 1)
            st.did(dve.tensor_scalar(lead[:], lead[:], o.cont[:, 0:1], None, ALU.mult))
            dve.wait_ge(carry_ready, 1)
            st.did(dve.tensor_copy(carried[:], cb[:]))
            st.did(dve.tensor_scalar(t1[:], lead[:], carried[:, 0:1], None, ALU.mult))
            st.did(dve.tensor_tensor(deg[:], deg[:], t1[:], ALU.add))
            if second == "count":
                st.did(dve.tensor_scalar(t1[:], lead[:], carried[:, 1:2], None, ALU.mult))
                st.did(dve.tensor_tensor(num[:], num[:], t1[:], ALU.add))
            both = (deg, num if second == "count" else slot)
            with dve.Fori(0, NPAIR) as i:
                for j in range(2):
                    at = bass.ds(i * (2 * CH) + j * CH, CH)
                    dve.wait_ge(sent[j], i * (16 * CH))
                    dve.tensor_copy(stage[j][:, :, 0], both[0][:, at])
                    dve.tensor_copy(stage[j][:, :, 1], both[1][:, at])
                    dve.tensor_copy(row[j][:], o.to_node[:, at]).then_inc(staged[j], 1)

        @block.tensor
        def _(pe):
            pe.wait_ge(diag_ready, 1)
            pe.matmul(kb[:], net.ones[:], diag[:], start=True, stop=True).then_inc(key_rows, 1)
            pe.wait_ge(tail_ready, 1)
            pe.matmul(cb[:], o.carry[:], tail[:], start=True, stop=True).then_inc(carry_ready, 1)

        @block.gpsimd
        def _(pool):
            pool.iota(slot[:], pattern=[[1, T]], base=1, channel_multiplier=T,
                      allow_small_or_imprecise_dtypes=True).then_inc(iotas, 1)
            pool.wait_ge(net.zeroed, net.zeroed_all)
            with pool.Fori(0, NPAIR) as i:
                for j in range(2):
                    pool.wait_ge(staged[j], i + 1)
                    pool.sem_inc(started, 1)
                    for r in range(CH):
                        pool.indirect_dma_start(
                            out=table, out_offset=bass.IndirectOffsetOnAxis(ap=row[j][:, r:r + 1], axis=0),
                            in_=stage[j][:, r, :], in_offset=None,
                            bounds_check=NR - 1, oob_is_err=False).then_inc(sent[j], 16)
            for j in range(2):
                pool.wait_ge(sent[j], NPAIR * CH * 16)



def node_scalars_phase(net):
    nc = net.nc
    with net.phase() as c:
        bd = tile(nc, c, "ns_bd", [P, NPP, 2])
        bs = tile(nc, c, "ns_bs", [P, NPP, 2])
        deg = [tile(nc, c, f"ns_deg{n}", [P, NPP]) for n in range(3)]
        pos = [tile(nc, c, f"ns_pos{n}", [P, NPP]) for n in range(3)]
        root = [tile(nc, c, f"ns_root{n}", [P, NPP]) for n in range(3)]
        pair = tile(nc, c, "ns_pair", [P, NPP, 2])
        half = tile(nc, c, "ns_half", [P, NPP])
        loaded, own, degrees, rooted, paired, written = (
            net.sem("ns_" + n) for n in ("loaded", "own", "degrees", "rooted", "paired", "written"))
        block = c.enter_context(nc.Block())

        @block.sync
        def _(sp):
            sp.dma_start(bd[:], net.by_dst[:, :].rearrange("(p g) c -> p g c", p=P)).then_inc(loaded, 16)
            sp.dma_start(bs[:], net.by_src[:, :].rearrange("(p g) c -> p g c", p=P)).then_inc(loaded, 16)
            sp.wait_ge(paired, 1)
            sp.dma_start(net.pairs[:, :].rearrange("(p g) c -> p g c", p=P), pair[:]).then_inc(written, 16)
            sp.wait_ge(written, 16)

        @block.scalar
        def _(act):
            act.wait_ge(degrees, 1)
            for n in range(3):
                act.activation(root[n][:], deg[n][:], ACT.Sqrt).then_inc(rooted, 1)

        @block.vector
        def _(dve):
            st = Steps(dve, own)
            dve.wait_ge(loaded, 2 * 16)
            dve.tensor_scalar(deg[0][:], bs[:, :, 0], 1.0, None, ALU.add)
            dve.tensor_scalar(deg[1][:], bd[:, :, 0], 1.0, None, ALU.add)
            st.did(dve.tensor_copy(deg[2][:], bs[:, :, 1]))
            dve.tensor_copy(net.slot1[:], bd[:, :, 1])
            for n in range(3):
                st.did(dve.tensor_scalar(pos[n][:], deg[n][:], 0.0, None, ALU.is_gt))
            st.did(dve.tensor_scalar(deg[0][:], deg[0][:], 1e-30, None, ALU.max))
            st.did(dve.tensor_scalar(deg[1][:], deg[1][:], 1e-30, None, ALU.max))
            dve.tensor_scalar(deg[2][:], deg[2][:], 1.0, None, ALU.max).then_inc(degrees, 1)
            dve.wait_ge(rooted, 3)
            dve.reciprocal(net.inv_count[:], deg[2][:])
            for n, to in enumerate((net.inv_out, net.inv_in, net.inv_deg)):
                st.did(dve.reciprocal(root[n][:], root[n][:]))
                st.did(dve.tensor_tensor(half[:], root[n][:], root[n][:], ALU.mult))
                st.did(dve.tensor_tensor(half[:], half[:], deg[n][:], ALU.mult))
                st.did(dve.tensor_scalar(half[:], half[:], -0.5, 1.5, ALU.mult, ALU.add))
                st.did(dve.tensor_tensor(root[n][:], root[n][:], half[:], ALU.mult))
                st.did(dve.tensor_tensor(to[:], root[n][:], pos[n][:], ALU.mult))
            st.did(dve.scalar_tensor_tensor(out=net.own_part[:], in0=net.inv_out[:], scalar=0.9, in1=net.inv_in[:],
                                            op0=ALU.mult, op1=ALU.mult))
            dve.tensor_copy(pair[:, :, 0], net.inv_in[:])
            dve.tensor_copy(pair[:, :, 1], net.own_part[:]).then_inc(paired, 1)
            st.did(dve.memset(net.own_k[:], 1.0))
            for _ in range(K_STEPS):
                st.did(dve.tensor_tensor(net.own_k[:], net.own_k[:], net.own_part[:], ALU.mult))
                st.did(dve.tensor_scalar(net.own_k[:], net.own_k[:], 0.1, None, ALU.add))
            st.did(dve.tensor_scalar(net.own_k[:], net.own_k[:], 1.0, None, ALU.add))


def node_view(table, width):
    return table[:, :].rearrange("(p g) c -> p g c", p=P)


class RealRows:

    def __init__(self, ap):
        whole = (P - 1) * NPP
        self.first = ap[0:whole, :].rearrange("(p g) c -> p g c", g=NPP)
        self.last = ap[whole:N, :].rearrange("(p g) c -> p g c", p=1)

    def move(self, eng, sem, tile_ap, at, full, store):
        halves(eng, sem, lambda a, b: tile_ap[a:b], lambda a, b: self.first[a:b, at, :], store)
        if full:
            if store:
                eng.dma_start(self.last[:, at, :], tile_ap[P - 1:P]).then_inc(sem, 16)
            else:
                eng.dma_start(tile_ap[P - 1:P], self.last[:, at, :]).then_inc(sem, 16)


PARTS = ((0, PAIRS_FULL, True), (PAIRS_FULL, PAIRS, False))


def moved(i, full, turns=1):
    return (i + turns) * 48 if full else (i + turns) * 32 + PAIRS_FULL * 16


def x_rows_phase(net, x):
    nc = net.nc
    with net.phase() as c:
        row = [tile(nc, c, f"xr_row{j}", [P, G, XW]) for j in range(2)]
        blank = net.sem("xr_blank")
        loaded = [net.sem(f"xr_loaded{j}") for j in range(2)]
        made = [net.sem(f"xr_made{j}") for j in range(2)]
        stored = [net.sem(f"xr_stored{j}") for j in range(2)]
        rows, to = RealRows(x), node_view(net.x_rows, XW)
        block = c.enter_context(nc.Block())

        @block.sync
        def _(sp):
            sp.wait_ge(blank, 2)
            for a, b, full in PARTS:
                with sp.Fori(a, b) as i:
                    for j in range(2):
                        sp.wait_ge(stored[j], i * 16)
                        rows.move(sp, loaded[j], row[j][:, :, 0:D], bass.ds(i * (2 * G) + j * G, G), full, False)

        @block.vector
        def _(dve):
            for j in range(2):
                dve.memset(row[j][:], 0.0).then_inc(blank, 1)
            dve.wait_ge(blank, 2)
            for a, b, full in PARTS:
                with dve.Fori(a, b) as i:
                    for j in range(2):
                        at = bass.ds(i * (2 * G) + j * G, G)
                        dve.wait_ge(stored[j], i * 16)
                        dve.tensor_copy(row[j][:, :, D], net.inv_out[:, at])
                        dve.tensor_copy(row[j][:, :, D + 1], net.own_part[:, at])
                        dve.tensor_copy(row[j][:, :, D + 2], net.slot1[:, at]).then_inc(made[j], 1)

        @block.scalar
        def _(act):
            for a, b, full in PARTS:
                with act.Fori(a, b) as i:
                    for j in range(2):
                        act.wait_ge(loaded[j], moved(i, full))
                        act.wait_ge(made[j], i + 1)
                        act.dma_start(to[:, bass.ds(i * (2 * G) + j * G, G), :], row[j][:]).then_inc(stored[j], 16)
            for j in range(2):
                act.wait_ge(stored[j], PAIRS * 16)



def edge_view(table):
    return table.rearrange("(p t) c -> p t c", p=P)


def chunk(i, j):
    return i * (2 * CH) + j * CH


MW = 32


def mask_phase(net, o, mask):
    nc = net.nc
    with net.phase() as c:
        block = c.enter_context(nc.Block())

        @block.vector
        def _(dve):
            with dve.Fori(0, NPAIR) as i:
                for j in range(2):
                    dve.tensor_copy(mask[:, bass.ds(i * 2 + j, 1), :].rearrange("p o (f t) -> p (o f) t", t=CH),
                                    spread(o.scan[:, bass.ds(chunk(i, j), CH)], 1, MW))


class Fix:

    def __init__(self, net, c, name, width):
        self.row = tile(net.nc, c, name + "_fixrow", [P, width])
        self.bank = bank(net.nc, c, name + "_fixbank", [P, width])
        self.product, self.got, self.added, self.put, self.turns, self.blanked = (
            net.sem(f"{name}_fix_{n}") for n in ("product", "got", "added", "put", "turns", "blanked"))

    def tensor(self, pe, n, o, tail):
        pe.wait_ge(self.added, n)
        pe.matmul(self.bank[:], o.carry[:], tail, start=True, stop=True).then_inc(self.product, 1)

    def blank(self, dve):
        dve.memset(self.row[:], 0.0).then_inc(self.blanked, 1)

    def gpsimd(self, pool, n, table, index, last_row):
        pool.wait_ge(self.blanked, 1)
        pool.sem_inc(self.turns, 1)
        pool.indirect_dma_start(out=self.row[:], out_offset=None, in_=table,
                                in_offset=bass.IndirectOffsetOnAxis(ap=index, axis=0),
                                bounds_check=last_row, oob_is_err=False).then_inc(self.got, 16)
        pool.wait_ge(self.added, n + 1)
        pool.sem_inc(self.turns, 1)
        pool.indirect_dma_start(out=table, out_offset=bass.IndirectOffsetOnAxis(ap=index, axis=0),
                                in_=self.row[:], in_offset=None,
                                bounds_check=last_row, oob_is_err=False).then_inc(self.put, 16)
        pool.wait_ge(self.put, n * 16 + 16)

    def vector(self, dve, n):
        dve.wait_ge(self.product, n + 1)
        dve.wait_ge(self.got, n * 16 + 16)
        dve.tensor_tensor(self.row[:], self.row[:], self.bank[:], ALU.add).then_inc(self.added, 1)


def scan_chunk(dve, st, o, mask, msg, sums, prev, i, j):
    w, flat = msg.shape[1], "p f t -> p (f t)"
    st.did(dve.scalar_tensor_tensor(out=msg[:, :, 0], in0=prev[:, :, CH - 1], scalar=o.cont[:, bass.ds(chunk(i, j), 1)],
                                    in1=msg[:, :, 0], op0=ALU.mult, op1=ALU.add))
    for a in range(0, w, MW):
        b = min(a + MW, w)
        ins = dve.tensor_tensor_scan(out=sums[:, a:b, :].rearrange(flat), data1=msg[:, a:b, :].rearrange(flat),
                                     data0=mask[:, bass.ds(i * 2 + j, 1), 0:(b - a) * CH].rearrange("p o n -> p (o n)"),
                                     initial=0.0, op0=ALU.mult, op1=ALU.add)
        (st.did if b == w else st.mark)(ins)


def scan_steps(w):
    return 1 + -(-w // MW)



def appnp_first_phase(net, o, co):
    nc = net.nc
    with net.phase() as c:
        rec = [tile(nc, c, f"a0_rec{j}", [P, CH, 4], I32) for j in range(2)]
        xg = [tile(nc, c, f"a0_xg{j}", [P, CH, XW]) for j in range(2)]
        pg = [tile(nc, c, f"a0_pg{j}", [P, CH, 2]) for j in range(2)]
        msg = [tile(nc, c, f"a0_msg{j}", [P, D, CH]) for j in range(2)]
        sums = [tile(nc, c, f"a0_sums{j}", [P, D, CH]) for j in range(2)]
        rows = [tile(nc, c, f"a0_rows{j}", [P, CH, D]) for j in range(2)]
        slot = tile(nc, c, "a0_slot", [P, T])
        has = tile(nc, c, "a0_has", [P, T])
        zrow = tile(nc, c, "a0_zrow", [P, 1])
        index = tile(nc, c, "a0_index", [P, T], I32)
        own, started, indexed, kept = (net.sem("a0_" + n) for n in ("own", "started", "indexed", "kept"))
        sem2 = lambda n: [net.sem(f"a0_{n}{j}") for j in range(2)]
        staged, gathered, used, summed, rowed, x_out, r_out = (
            sem2(n) for n in ("staged", "gathered", "used", "summed", "rowed", "x_out", "r_out"))
        fix = Fix(net, c, "a0", D)
        block = c.enter_context(nc.Block())
        records = edge_view(o.records[1:EP + 1, :])

        @block.sync
        def _(sp):
            with sp.Fori(0, NPAIR) as i:
                for j in range(2):
                    sp.wait_ge(used[j], i)
                    sp.dma_start(rec[j][:], records[:, bass.ds(chunk(i, j), CH), :]).then_inc(staged[j], 16)
            sp.wait_ge(indexed, 1)
            sp.dma_start(net.slot_index[:, :], index[:]).then_inc(kept, 16)
            sp.wait_ge(kept, 16)

        @block.gpsimd
        def _(pool):
            with pool.Fori(0, NPAIR) as i:
                for j in range(2):
                    pool.wait_ge(staged[j], i * 16 + 16)
                    pool.wait_ge(x_out[j], i * 16)
                    pool.sem_inc(started, 1)
                    for r in range(CH):
                        pool.indirect_dma_start(
                            out=xg[j][:, r, :], out_offset=None, in_=net.x_rows[:, :],
                            in_offset=bass.IndirectOffsetOnAxis(ap=rec[j][:, r, 0:1], axis=0)).then_inc(gathered[j], 16)
                        pool.indirect_dma_start(
                            out=pg[j][:, r, :], out_offset=None, in_=net.pairs[:, :],
                            in_offset=bass.IndirectOffsetOnAxis(ap=rec[j][:, r, 1:2], axis=0)).then_inc(gathered[j], 16)
            for j in range(2):
                pool.wait_ge(r_out[j], NPAIR * 16)
            fix.gpsimd(pool, 0, net.slots[1][:, :], o.fix_slot[:], TR - 1)

        @block.vector
        def _(dve):
            st = Steps(dve, own)
            fix.blank(dve)
            st.did(dve.memset(sums[1][:, :, CH - 1:CH], 0.0))
            st.did(dve.tensor_scalar(zrow[:], net.part[:], float(ZROW), None, ALU.add))
            with dve.Fori(0, NPAIR) as i:
                st.enter(i, 2 * (6 + scan_steps(D)))
                for j in range(2):
                    at = bass.ds(chunk(i, j), CH)
                    dve.wait_ge(gathered[j], i * (2 * CH * 16) + 2 * CH * 16)
                    st.did(dve.scalar_tensor_tensor(out=co.weight[:, at], in0=rec[j][:, :, 2].bitcast(F32), scalar=0.9,
                                                    in1=xg[j][:, :, D], op0=ALU.mult, op1=ALU.mult))
                    st.did(dve.tensor_tensor(co.weight[:, at], co.weight[:, at], pg[j][:, :, 0], ALU.mult))
                    st.did(dve.tensor_copy(co.src_part[:, at], xg[j][:, :, D + 1]))
                    st.did(dve.tensor_copy(co.dst_part[:, at], pg[j][:, :, 1]))
                    st.did(dve.tensor_copy(slot[:, at], xg[j][:, :, D + 2]))
                    st.did(dve.tensor_tensor(msg[j][:].rearrange("p f t -> p t f"), xg[j][:, :, 0:D],
                                             spread(co.weight[:, at], 2, D), ALU.mult))
                    dve.sem_inc(used[j], 1)
                    dve.wait_ge(rowed[j], i)
                    scan_chunk(dve, st, o, co.mask, msg[j], sums[j], sums[1 - j], i, j)
                    dve.sem_inc(summed[j], 1)
                st.leave(NPAIR)
            st.did(dve.tensor_scalar(has[:], slot[:], 0.0, None, ALU.is_gt))
            st.did(dve.tensor_scalar(slot[:], slot[:], zrow[:, 0:1], -1.0, ALU.subtract, ALU.add))
            st.did(dve.tensor_tensor(slot[:], slot[:], has[:], ALU.mult))
            dve.tensor_scalar(index[:], slot[:], zrow[:, 0:1], None, ALU.add).then_inc(indexed, 1)
            st.did(dve.tensor_scalar(co.alpha[:], co.src_part[:], 0.1, None, ALU.add))
            fix.vector(dve, 0)

        @block.scalar
        def _(act):
            with act.Fori(0, NPAIR) as i:
                for j in range(2):
                    at = bass.ds(chunk(i, j), CH)
                    act.wait_ge(gathered[j], i * (2 * CH * 16) + 2 * CH * 16)
                    act.dma_start(edge_view(net.x_edges)[:, at, :], xg[j][:, :, 0:D]).then_inc(x_out[j], 16)
                    act.wait_ge(summed[j], i + 1)
                    act.wait_ge(r_out[j], i * 16)
                    act.activation(rows[j][:], sums[j][:].rearrange("p f t -> p t f"), ACT.Copy).then_inc(rowed[j], 1)
                    act.wait_ge(rowed[j], i + 1)
                    act.dma_start(edge_view(net.slots[1][0:EP, :])[:, at, :], rows[j][:]).then_inc(r_out[j], 16)
            for j in range(2):
                act.wait_ge(x_out[j], NPAIR * 16)

        @block.tensor
        def _(pe):
            pe.wait_ge(summed[1], NPAIR)
            fix.tensor(pe, 0, o, sums[1][:, :, CH - 1])


def appnp_steps_phase(net, o, co):
    nc = net.nc
    with net.phase() as c:
        index = [tile(nc, c, f"as_index{j}", [P, CH], I32) for j in range(2)]
        rg = [tile(nc, c, f"as_rg{j}", [P, CH, D]) for j in range(2)]
        xe = [tile(nc, c, f"as_xe{j}", [P, CH, D]) for j in range(2)]
        rr = [tile(nc, c, f"as_rr{j}", [P, CH, D]) for j in range(2)]
        msg = [tile(nc, c, f"as_msg{j}", [P, D, CH]) for j in range(2)]
        sums = [tile(nc, c, f"as_sums{j}", [P, D, CH]) for j in range(2)]
        of_x = tile(nc, c, "as_of_x", [P, T])
        own, started, stepped, turns, begun = (
            net.sem("as_" + n) for n in ("own", "started", "stepped", "turns", "begun"))
        sem2 = lambda n: [net.sem(f"as_{n}{j}") for j in range(2)]
        staged, gathered, streamed, used, summed, r_out = (
            sem2(n) for n in ("staged", "gathered", "streamed", "used", "summed", "r_out"))
        fix = Fix(net, c, "as", D)
        block = c.enter_context(nc.Block())
        STEPS = K_STEPS - 1
        PER = NPAIR * 2 * (5 + scan_steps(D)) + 5

        def steps(eng, step):
            with eng.Fori(0, STEPS // 2) as m:
                for odd in range(2):
                    step(m * 2 + odd, 1 - odd)
            step(STEPS - 1, 1)

        @block.sync
        def _(sp):
            def step(s, rt):
                sp.wait_ge(stepped, s)
                sp.sem_inc(turns, 1)
                with sp.Fori(0, NPAIR) as i:
                    n = s * NPAIR + i
                    for j in range(2):
                        at = bass.ds(chunk(i, j), CH)
                        sp.wait_ge(gathered[j], n * (CH * 16))
                        sp.dma_start(index[j][:], net.slot_index[:, at]).then_inc(staged[j], 16)
                        sp.wait_ge(used[j], n)
                        sp.sem_inc(turns, 1)
                        sp.wait_ge(r_out[j], n * 16)
                        sp.dma_start(xe[j][:], edge_view(net.x_edges)[:, at, :]).then_inc(streamed[j], 16)
                        sp.dma_start(rr[j][:], edge_view(net.slots[rt][0:EP, :])[:, at, :]).then_inc(streamed[j], 16)
            steps(sp, step)

        @block.gpsimd
        def _(pool):
            def step(s, rt):
                with pool.Fori(0, NPAIR) as i:
                    n = s * NPAIR + i
                    for j in range(2):
                        pool.wait_ge(staged[j], n * 16 + 16)
                        pool.wait_ge(used[j], n)
                        pool.sem_inc(started, 1)
                        for r in range(CH):
                            pool.indirect_dma_start(
                                out=rg[j][:, r, :], out_offset=None, in_=net.slots[rt][:, :],
                                in_offset=bass.IndirectOffsetOnAxis(ap=index[j][:, r:r + 1], axis=0)).then_inc(gathered[j], 16)
                for j in range(2):
                    pool.wait_ge(r_out[j], (s + 1) * (NPAIR * 16))
                fix.gpsimd(pool, s, net.slots[1 - rt][:, :], o.fix_slot[:], TR - 1)
                pool.sem_inc(stepped, 1)
            steps(pool, step)

        @block.vector
        def _(dve):
            st = Steps(dve, own)
            fix.blank(dve)

            def step(s, rt):
                own_before = st.base
                st.base = own_before + s * PER
                st.n = 0
                dve.wait_ge(fix.product, s)
                st.did(dve.memset(sums[1][:, :, CH - 1:CH], 0.0))
                st.did(dve.tensor_tensor(of_x[:], co.alpha[:], co.weight[:], ALU.mult))
                dve.sem_inc(begun, 1)
                with dve.Fori(0, NPAIR) as i:
                    n = s * NPAIR + i
                    st.enter(i, 2 * (5 + scan_steps(D)))
                    for j in range(2):
                        at = bass.ds(chunk(i, j), CH)
                        dve.wait_ge(streamed[j], n * 32 + 32)
                        st.did(dve.tensor_tensor(xe[j][:], xe[j][:], spread(of_x[:, at], 2, D), ALU.mult))
                        dve.wait_ge(gathered[j], n * (CH * 16) + CH * 16)
                        st.did(dve.tensor_tensor(rg[j][:], rg[j][:], spread(co.weight[:, at], 2, D), ALU.mult))
                        st.did(dve.tensor_tensor(msg[j][:].rearrange("p f t -> p t f"), rg[j][:], xe[j][:], ALU.add))
                        dve.sem_inc(used[j], 1)
                        scan_chunk(dve, st, o, co.mask, msg[j], sums[j], sums[1 - j], i, j)
                        st.did(dve.tensor_tensor(rr[j][:], rr[j][:], spread(co.dst_part[:, at], 2, D), ALU.mult))
                        st.did(dve.tensor_tensor(rr[j][:], rr[j][:], sums[j][:].rearrange("p f t -> p t f"), ALU.add))
                        dve.sem_inc(summed[j], 1)
                    st.leave(NPAIR)
                st.did(dve.tensor_tensor(co.alpha[:], co.alpha[:], co.src_part[:], ALU.mult))
                st.did(dve.tensor_scalar(co.alpha[:], co.alpha[:], 0.1, None, ALU.add))
                fix.vector(dve, s)
                st.did(dve.nop())
                assert st.n == PER, st.n
                st.base = own_before
            steps(dve, step)

        @block.scalar
        def _(act):
            def step(s, rt):
                with act.Fori(0, NPAIR) as i:
                    n = s * NPAIR + i
                    for j in range(2):
                        act.wait_ge(summed[j], n + 1)
                        act.dma_start(edge_view(net.slots[1 - rt][0:EP, :])[:, bass.ds(chunk(i, j), CH), :],
                                      rr[j][:]).then_inc(r_out[j], 16)
            steps(act, step)

        @block.tensor
        def _(pe):
            def step(s, rt):
                pe.wait_ge(summed[1], (s + 1) * NPAIR)
                fix.tensor(pe, s, o, sums[1][:, :, CH - 1])
            steps(pe, step)


def to_nodes_phase(net, o):
    nc = net.nc
    with net.phase() as c:
        rows = [tile(nc, c, f"tn_rows{j}", [P, CH, D]) for j in range(2)]
        node = [tile(nc, c, f"tn_node{j}", [P, CH], I32) for j in range(2)]
        started = net.sem("tn_started")
        sem2 = lambda n: [net.sem(f"tn_{n}{j}") for j in range(2)]
        loaded, named, sent = (sem2(n) for n in ("loaded", "named", "sent"))
        block = c.enter_context(nc.Block())

        @block.sync
        def _(sp):
            with sp.Fori(0, NPAIR) as i:
                for j in range(2):
                    sp.wait_ge(sent[j], i * (CH * 16))
                    sp.dma_start(rows[j][:], edge_view(net.slots[0][0:EP, :])[:, bass.ds(chunk(i, j), CH), :]).then_inc(loaded[j], 16)

        @block.vector
        def _(dve):
            with dve.Fori(0, NPAIR) as i:
                for j in range(2):
                    dve.wait_ge(sent[j], i * (CH * 16))
                    dve.tensor_copy(node[j][:], o.to_node[:, bass.ds(chunk(i, j), CH)]).then_inc(named[j], 1)

        @block.gpsimd
        def _(pool):
            with pool.Fori(0, NPAIR) as i:
                for j in range(2):
                    pool.wait_ge(loaded[j], i * 16 + 16)
                    pool.wait_ge(named[j], i + 1)
                    pool.sem_inc(started, 1)
                    for r in range(CH):
                        pool.indirect_dma_start(
                            out=net.node_r[:, :], out_offset=bass.IndirectOffsetOnAxis(ap=node[j][:, r:r + 1], axis=0),
                            in_=rows[j][:, r, :], in_offset=None,
                            bounds_check=NR - 1, oob_is_err=False).then_inc(sent[j], 16)
            for j in range(2):
                pool.wait_ge(sent[j], NPAIR * CH * 16)




class Norm:

    def __init__(self, net, c, name):
        nc = net.nc
        self.mean, self.var = tile(nc, c, name + "_mean", [P, G]), tile(nc, c, name + "_var", [P, G])
        self.square = tile(nc, c, name + "_square", [P, G, D])
        self.eps = tile(nc, c, name + "_eps", [P, 1])
        self.summed, self.rooted, self.ready = (net.sem(f"{name}_{n}") for n in ("summed", "rooted", "eps_ready"))

    STEPS = 6

    def start(self, dve):
        dve.memset(self.eps[:], EPS).then_inc(self.ready, 1)

    def vector(self, dve, st, x, n):
        st.did(dve.tensor_reduce(self.mean[:], x, AX.X, ALU.add))
        st.did(dve.tensor_scalar(self.mean[:], self.mean[:], -1.0 / D, None, ALU.mult))
        st.did(dve.tensor_tensor(x, x, spread(self.mean[:], 2, D), ALU.add))
        st.did(dve.tensor_tensor(self.square[:], x, x, ALU.mult))
        dve.tensor_reduce(self.var[:], self.square[:], AX.X, ALU.add).then_inc(self.summed, 1)
        dve.wait_ge(self.rooted, n + 1)
        st.did(dve.reciprocal(self.var[:], self.var[:]))
        st.did(dve.tensor_tensor(x, x, spread(self.var[:], 2, D), ALU.mult))

    def scalar(self, act, n):
        act.wait_ge(self.summed, n + 1)
        act.activation(self.var[:], self.var[:], ACT.Sqrt, bias=self.eps[:, 0:1], scale=1.0 / D).then_inc(self.rooted, 1)


def node_chunk(i, j):
    return bass.ds(i * (2 * G) + j * G, G)


def x1_phase(net, x):
    nc = net.nc
    with net.phase() as c:
        row = [tile(nc, c, f"x1_row{j}", [P, G, XW]) for j in range(2)]
        nr = [tile(nc, c, f"x1_nr{j}", [P, G, D]) for j in range(2)]
        norm = Norm(net, c, "x1")
        own, blank = net.sem("x1_own"), net.sem("x1_blank")
        sem2 = lambda n: [net.sem(f"x1_{n}{j}") for j in range(2)]
        loaded, summed, used, made, stored = (sem2(n) for n in ("loaded", "summed", "used", "made", "stored"))
        rows, sums, to = RealRows(x), node_view(net.node_r, D), node_view(net.x1_rows, XW)
        block = c.enter_context(nc.Block())

        @block.sync
        def _(sp):
            sp.wait_ge(blank, 2)
            for a, b, full in PARTS:
                with sp.Fori(a, b) as i:
                    for j in range(2):
                        sp.wait_ge(used[j], i)
                        sp.dma_start(nr[j][:], sums[:, node_chunk(i, j), :]).then_inc(summed[j], 16)
                        sp.wait_ge(stored[j], i * 16)
                        rows.move(sp, loaded[j], row[j][:, :, 0:D], node_chunk(i, j), full, False)

        @block.vector
        def _(dve):
            st = Steps(dve, own)
            norm.start(dve)
            for j in range(2):
                dve.memset(row[j][:], 0.0).then_inc(blank, 1)
            dve.wait_ge(blank, 2)
            for a, b, full in PARTS:
                with dve.Fori(a, b) as i:
                    st.enter(i - a, 2 * (3 + Norm.STEPS))
                    for j in range(2):
                        at, xr = node_chunk(i, j), row[j][:, :, 0:D]
                        dve.wait_ge(loaded[j], moved(i, full))
                        dve.wait_ge(summed[j], i * 16 + 16)
                        st.did(dve.tensor_tensor(xr, xr, spread(net.own_k[:, at], 2, D), ALU.mult))
                        st.did(dve.tensor_tensor(xr, xr, nr[j][:], ALU.add))
                        dve.sem_inc(used[j], 1)
                        norm.vector(dve, st, xr, i * 2 + j)
                        st.did(dve.tensor_copy(row[j][:, :, D], net.inv_deg[:, at]))
                        dve.sem_inc(made[j], 1)
                    st.leave(b - a)

        @block.scalar
        def _(act):
            act.wait_ge(norm.ready, 1)
            for a, b, full in PARTS:
                with act.Fori(a, b) as i:
                    for j in range(2):
                        norm.scalar(act, i * 2 + j)
                        act.wait_ge(made[j], i + 1)
                        act.dma_start(to[:, node_chunk(i, j), :], row[j][:]).then_inc(stored[j], 16)
            for j in range(2):
                act.wait_ge(stored[j], PAIRS * 16)


def gcn_edges_phase(net, o, mask, edge_attr):
    nc = net.nc
    with net.phase() as c:
        rec = [tile(nc, c, f"ge_rec{j}", [P, CH, 4], I32) for j in range(2)]
        node = [tile(nc, c, f"ge_node{j}", [P, CH], I32) for j in range(2)]
        xg = [tile(nc, c, f"ge_xg{j}", [P, CH, XW]) for j in range(2)]
        eg = [tile(nc, c, f"ge_eg{j}", [P, CH, ED]) for j in range(2)]
        msg = [tile(nc, c, f"ge_msg{j}", [P, AW, CH]) for j in range(2)]
        sums = [tile(nc, c, f"ge_sums{j}", [P, AW, CH]) for j in range(2)]
        rows = [tile(nc, c, f"ge_rows{j}", [P, CH, AW]) for j in range(2)]
        factor = tile(nc, c, "ge_factor", [P, CH])
        own, started, blank = net.sem("ge_own"), net.sem("ge_started"), net.sem("ge_blank")
        sem2 = lambda n: [net.sem(f"ge_{n}{j}") for j in range(2)]
        staged, gathered, used, edges_in, summed, rowed, sent = (
            sem2(n) for n in ("staged", "gathered", "used", "edges_in", "summed", "rowed", "sent"))
        fix = Fix(net, c, "ge", AW)
        block = c.enter_context(nc.Block())
        records = edge_view(o.records[1:EP + 1, :])

        @block.sync
        def _(sp):
            with sp.Fori(0, NPAIR) as i:
                for j in range(2):
                    sp.wait_ge(used[j], i)
                    sp.wait_ge(edges_in[j], i)
                    sp.dma_start(rec[j][:], records[:, bass.ds(chunk(i, j), CH), :]).then_inc(staged[j], 16)

        @block.gpsimd
        def _(pool):
            def gather(i, j):
                pool.wait_ge(staged[j], i * 16 + 16)
                pool.sem_inc(started, 1)
                for r in range(CH):
                    pool.indirect_dma_start(
                        out=xg[j][:, r, :], out_offset=None, in_=net.x1_rows[:, :],
                        in_offset=bass.IndirectOffsetOnAxis(ap=rec[j][:, r, 1:2], axis=0)).then_inc(gathered[j], 16)
                    pool.indirect_dma_start(
                        out=eg[j][:, r, :], out_offset=None, in_=edge_attr,
                        in_offset=bass.IndirectOffsetOnAxis(ap=rec[j][:, r, 3:4], axis=0),
                        bounds_check=E - 1, oob_is_err=False).then_inc(gathered[j], 16)

            def scatter(i, j):
                pool.wait_ge(rowed[j], i + 1)
                pool.sem_inc(started, 1)
                for r in range(CH):
                    pool.indirect_dma_start(
                        out=net.agg[:, :], out_offset=bass.IndirectOffsetOnAxis(ap=node[j][:, r:r + 1], axis=0),
                        in_=rows[j][:, r, :], in_offset=None,
                        bounds_check=NR - 1, oob_is_err=False).then_inc(sent[j], 16)

            pool.wait_ge(blank, 2)
            gather(0, 0)
            with pool.Fori(0, NPAIR - 1) as i:
                gather(i, 1)
                scatter(i, 0)
                gather(i + 1, 0)
                scatter(i, 1)
            gather(NPAIR - 1, 1)
            scatter(NPAIR - 1, 0)
            scatter(NPAIR - 1, 1)
            for j in range(2):
                pool.wait_ge(sent[j], NPAIR * CH * 16)
            fix.gpsimd(pool, 0, net.agg[:, :], o.fix_node[:], NR - 1)

        @block.vector
        def _(dve):
            st = Steps(dve, own)
            fix.blank(dve)
            for j in range(2):
                dve.memset(eg[j][:], 0.0).then_inc(blank, 1)
            st.did(dve.memset(sums[1][:, :, CH - 1:CH], 0.0))
            with dve.Fori(0, NPAIR) as i:
                st.enter(i, 2 * (3 + scan_steps(AW)))
                for j in range(2):
                    dve.wait_ge(gathered[j], i * (2 * CH * 16) + 2 * CH * 16)
                    st.did(dve.tensor_tensor(factor[:], rec[j][:, :, 2].bitcast(F32), xg[j][:, :, D], ALU.mult))
                    st.did(dve.tensor_tensor(msg[j][:, 0:D, :].rearrange("p f t -> p t f"), xg[j][:, :, 0:D],
                                             spread(factor[:], 2, D), ALU.mult))
                    dve.sem_inc(used[j], 1)
                    dve.wait_ge(edges_in[j], i + 1)
                    dve.wait_ge(rowed[j], i)
                    scan_chunk(dve, st, o, mask, msg[j], sums[j], sums[1 - j], i, j)
                    dve.wait_ge(sent[j], i * (CH * 16))
                    st.did(dve.tensor_copy(node[j][:], o.to_node[:, bass.ds(chunk(i, j), CH)]))
                    dve.sem_inc(summed[j], 1)
                st.leave(NPAIR)
            fix.vector(dve, 0)

        @block.scalar
        def _(act):
            def edges(i, j):
                act.wait_ge(gathered[j], i * (2 * CH * 16) + 2 * CH * 16)
                act.wait_ge(summed[j], i)
                act.activation(msg[j][:, D:AW, :].rearrange("p f t -> p t f"), eg[j][:], ACT.Copy).then_inc(edges_in[j], 1)

            with act.Fori(0, NPAIR) as i:
                for j in range(2):
                    edges(i, j)
                    act.wait_ge(summed[j], i + 1)
                    act.activation(rows[j][:], sums[j][:].rearrange("p f t -> p t f"), ACT.Copy).then_inc(rowed[j], 1)

        @block.tensor
        def _(pe):
            pe.wait_ge(summed[1], NPAIR)
            fix.tensor(pe, 0, o, sums[1][:, :, CH - 1])


def x2_phase(net, weight, bias):
    nc = net.nc
    with net.phase() as c:
        x1 = [tile(nc, c, f"x2_x1{j}", [P, G, XW]) for j in range(2)]
        ag = [tile(nc, c, f"x2_ag{j}", [P, G, D]) for j in range(2)]
        turned = [tile(nc, c, f"x2_turned{j}", [P, G // 2 * P]) for j in range(2)]
        y = [tile(nc, c, f"x2_y{j}", [P, G, D]) for j in range(2)]
        w = tile(nc, c, "x2_w", [P, 2 * D])
        bi = tile(nc, c, "x2_bias", [P, D])
        tb = [bank(nc, c, f"x2_tb{j}", [P, G // 2 * P]) for j in range(2)]
        mb = [bank(nc, c, f"x2_mb{j}", [P, G, D]) for j in range(2)]
        norm = Norm(net, c, "x2")
        own, weights, cleared = net.sem("x2_own"), net.sem("x2_weights"), net.sem("x2_cleared")
        sem2 = lambda n: [net.sem(f"x2_{n}{j}") for j in range(2)]
        loaded, tb_ready, turned_ready, mb_ready, used, made, stored = (
            sem2(n) for n in ("loaded", "tb_ready", "turned_ready", "mb_ready", "used", "made", "stored"))
        rows, sums, to = node_view(net.x1_rows, XW), node_view(net.agg, AW), node_view(net.x2, D)
        block = c.enter_context(nc.Block())

        @block.sync
        def _(sp):
            sp.wait_ge(cleared, 1)
            for h in range(2):
                sp.dma_start(w[h * D:(h + 1) * D, h * D:(h + 1) * D], weight).then_inc(weights, 16)
            sp.dma_start(bi[:], bias.partition_broadcast(P)).then_inc(weights, 16)
            with sp.Fori(0, PAIRS) as i:
                for j in range(2):
                    sp.wait_ge(used[j], i)
                    sp.dma_start(x1[j][:], rows[:, node_chunk(i, j), :]).then_inc(loaded[j], 16)
                    sp.dma_start(ag[j][:], sums[:, node_chunk(i, j), 0:D]).then_inc(loaded[j], 16)

        @block.tensor
        def _(pe):
            pe.wait_ge(weights, 3 * 16)

            def turn(i, j):
                pe.wait_ge(loaded[j], i * 32 + 32)
                pe.wait_ge(turned_ready[j], i)
                for q in range(G // 2):
                    last = pe.transpose(tb[j][:, q * P:(q + 1) * P], ag[j][:, 2 * q:2 * q + 2, :].rearrange("p g f -> p (g f)"), net.ident[:])
                last.then_inc(tb_ready[j], 1)

            def multiply(i, j):
                pe.wait_ge(turned_ready[j], i + 1)
                pe.wait_ge(used[j], i)
                for q in range(G // 2):
                    last = pe.matmul(mb[j][:, 2 * q:2 * q + 2, :], turned[j][:, q * P:(q + 1) * P], w[:],
                                     start=True, stop=True)
                last.then_inc(mb_ready[j], 1)

            with pe.Fori(0, PAIRS) as i:
                for j in range(2):
                    turn(i, j)
                for j in range(2):
                    multiply(i, j)

        @block.scalar
        def _(act):
            act.wait_ge(norm.ready, 1)
            with act.Fori(0, PAIRS) as i:
                for j in range(2):
                    act.wait_ge(tb_ready[j], i + 1)
                    act.wait_ge(mb_ready[j], i)
                    act.activation(turned[j][:], tb[j][:], ACT.Copy).then_inc(turned_ready[j], 1)
                for j in range(2):
                    norm.scalar(act, i * 2 + j)
                    act.wait_ge(made[j], i + 1)
                    act.dma_start(to[:, node_chunk(i, j), :], y[j][:]).then_inc(stored[j], 16)
            for j in range(2):
                act.wait_ge(stored[j], PAIRS * 16)

        @block.vector
        def _(dve):
            st = Steps(dve, own)
            norm.start(dve)
            dve.memset(w[:], 0.0).then_inc(cleared, 1)
            dve.wait_ge(weights, 3 * 16)
            with dve.Fori(0, PAIRS) as i:
                st.enter(i, 2 * (3 + Norm.STEPS))
                for j in range(2):
                    dve.wait_ge(mb_ready[j], i + 1)
                    dve.wait_ge(stored[j], i * 16)
                    st.did(dve.tensor_tensor(y[j][:], mb[j][:], spread(net.inv_deg[:, node_chunk(i, j)], 2, D), ALU.mult))
                    st.did(dve.tensor_tensor(y[j][:], y[j][:], x1[j][:, :, 0:D], ALU.add))
                    dve.sem_inc(used[j], 1)
                    st.did(dve.tensor_tensor(y[j][:], y[j][:], spread(bi[:], 1, G), ALU.add))
                    norm.vector(dve, st, y[j][:], i * 2 + j)
                    dve.sem_inc(made[j], 1)
                st.leave(PAIRS)




BIG = 1e38
QG = 4


def scores_phase(net, o, at_edges, attn_w, attn_b):
    nc = net.nc
    W3 = 3 * D
    with net.phase() as c:
        rec = [tile(nc, c, f"sc_rec{j}", [P, CH, 4], I32) for j in range(2)]
        xg = [tile(nc, c, f"sc_xg{j}", [P, CH, 2 * D]) for j in range(2)]
        turned = [tile(nc, c, f"sc_turned{j}", [P, QG * P]) for j in range(2)]
        qkv = [tile(nc, c, f"sc_qkv{j}", [P, QG, W3]) for j in range(2)]
        qk = tile(nc, c, "sc_qk", [P, QG * HEADS, HD])
        w = tile(nc, c, "sc_w", [P, W3])
        bi = tile(nc, c, "sc_bias", [P, W3])
        tb = [bank(nc, c, f"sc_tb{j}", [P, QG * P]) for j in range(2)]
        mb = [bank(nc, c, f"sc_mb{j}", [P, 2, 512]) for j in range(2)]
        own, started, weights, packed = (net.sem("sc_" + n) for n in ("own", "started", "weights", "packed"))
        sem2 = lambda n: [net.sem(f"sc_{n}{j}") for j in range(2)]
        staged, gathered, all_turned, tb_ready, turned_ready, mb_ready, mb_used, v_kept = (
            sem2(n) for n in ("staged", "gathered", "all_turned", "tb_ready", "turned_ready", "mb_ready",
                              "mb_used", "v_kept"))
        block = c.enter_context(nc.Block())
        records = edge_view(o.records[1:EP + 1, :])
        NG = CH // QG
        halfgroups = NG

        @block.sync
        def _(sp):
            for h in range(2):
                sp.dma_start(w[h * D:(h + 1) * D, :], attn_w).then_inc(weights, 16)
            sp.dma_start(bi[:], attn_b.partition_broadcast(P)).then_inc(weights, 16)
            with sp.Fori(0, NPAIR) as i:
                for j in range(2):
                    sp.wait_ge(gathered[j], i * (2 * CH * 16))
                    sp.dma_start(rec[j][:], records[:, bass.ds(chunk(i, j), CH), :]).then_inc(staged[j], 16)

        @block.gpsimd
        def _(pool):
            with pool.Fori(0, NPAIR) as i:
                for j in range(2):
                    pool.wait_ge(staged[j], i * 16 + 16)
                    pool.wait_ge(all_turned[j], i)
                    pool.sem_inc(started, 1)
                    for r in range(CH):
                        for h in range(2):
                            pool.indirect_dma_start(
                                out=xg[j][:, r, h * D:(h + 1) * D], out_offset=None, in_=net.x2[:, :],
                                in_offset=bass.IndirectOffsetOnAxis(ap=rec[j][:, r, h:h + 1], axis=0)).then_inc(gathered[j], 16)

        @block.tensor
        def _(pe):
            pe.wait_ge(packed, 1)

            def turn(i, k):
                j, b = k // NG, k % 2
                if k % NG == 0:
                    pe.wait_ge(gathered[j], i * (2 * CH * 16) + 2 * CH * 16)
                pe.wait_ge(turned_ready[b], i * halfgroups + k // 2)
                for q in range(QG):
                    last = pe.transpose(tb[b][:, q * P:(q + 1) * P], xg[j][:, (k % NG) * QG + q, :], net.ident[:])
                last.then_inc(tb_ready[b], 1)
                if k % NG == NG - 1:
                    pe.wait_ge(turned_ready[b], i * halfgroups + k // 2 + 1)
                    pe.sem_inc(all_turned[j], 1)

            def multiply(i, k):
                b = k % 2
                pe.wait_ge(turned_ready[b], i * halfgroups + k // 2 + 1)
                pe.wait_ge(mb_used[b], i * halfgroups + k // 2)
                for q in range(QG):
                    last = pe.matmul(mb[b][:, q // 2, (q % 2) * W3:(q % 2 + 1) * W3], turned[b][:, q * P:(q + 1) * P],
                                     w[:], start=True, stop=True)
                last.then_inc(mb_ready[b], 1)

            with pe.Fori(0, NPAIR) as i:
                turn(i, 0)
                for k in range(1, 2 * NG):
                    turn(i, k)
                    multiply(i, k - 1)
                multiply(i, 2 * NG - 1)

        @block.scalar
        def _(act):
            with act.Fori(0, NPAIR) as i:
                for k in range(2 * NG + 1):
                    if k < 2 * NG:
                        b = k % 2
                        act.wait_ge(tb_ready[b], i * halfgroups + k // 2 + 1)
                        act.wait_ge(mb_ready[b], i * halfgroups + k // 2)
                        act.activation(turned[b][:], tb[b][:], ACT.Copy).then_inc(turned_ready[b], 1)
                    if k:
                        b, t0 = (k - 1) % 2, i * (2 * CH) + (k - 1) * QG
                        act.wait_ge(mb_used[b], i * halfgroups + (k - 1) // 2 + 1)
                        act.activation(at_edges.v[:, bass.ds(t0, QG), :].rearrange("p t (h d) -> p (t h) d", h=HEADS),
                                       qkv[b][:].rearrange("p t (h x) -> p (t h) x", h=HEADS)[:, :, 2 * HD:3 * HD],
                                       ACT.Copy).then_inc(v_kept[b], 1)

        @block.vector
        def _(dve):
            st = Steps(dve, own)
            dve.wait_ge(weights, 3 * 16)
            heads = w[:].rearrange("p (h x) -> p h x", h=HEADS)
            st.did(dve.memset(heads[0:D, :, HD:3 * HD], 0.0))
            dve.memset(heads[D:2 * D, :, 0:HD], 0.0).then_inc(packed, 1)
            with dve.Fori(0, NPAIR) as i:
                st.enter(i, 2 * NG * 2)
                for k in range(2 * NG):
                    b, t0 = k % 2, i * (2 * CH) + k * QG
                    dve.wait_ge(mb_ready[b], i * halfgroups + k // 2 + 1)
                    dve.wait_ge(v_kept[b], i * halfgroups + k // 2)
                    for q in range(2):
                        ins = dve.tensor_tensor(qkv[b][:, 2 * q:2 * q + 2, :],
                                                mb[b][:, q, 0:2 * W3].rearrange("p (t x) -> p t x", t=2),
                                                spread(bi[:], 1, 2), ALU.add)
                    ins.then_inc(mb_used[b], 1)
                    dve.wait_ge(mb_used[b], i * halfgroups + k // 2 + 1)
                    x = qkv[b][:].rearrange("p t (h x) -> p (t h) x", h=HEADS)
                    st.did(dve.tensor_tensor(qk[:], x[:, :, 0:HD], x[:, :, HD:2 * HD], ALU.mult))
                    st.did(dve.tensor_reduce(at_edges.score[:, :, bass.ds(t0, QG)].rearrange("p h t -> p t h"),
                                             qk[:].rearrange("p (t h) d -> p t h d", t=QG), AX.X, ALU.add))
                st.leave(NPAIR)
            for b in range(2):
                dve.wait_ge(v_kept[b], NPAIR * halfgroups)


class AtEdges:

    def __init__(self, net, c):
        self.v = tile(net.nc, c, "ae_v", [P, T, D])
        self.score = tile(net.nc, c, "ae_score", [P, HEADS, T])


def softmax_phase(net, o, at_edges):
    nc = net.nc
    with net.phase() as c:
        most = tile(nc, c, "sm_most", [P, HEADS, T])
        fwd, bwd, keep_f, keep_b, lead, tail = (
            tile(nc, c, "sm_" + n, [P, T]) for n in ("fwd", "bwd", "keep_f", "keep_b", "lead", "tail"))
        ends = tile(nc, c, "sm_ends", [P, 2, HEADS])
        total = tile(nc, c, "sm_total", [P, 2, HEADS])
        key_diag = [tile(nc, c, f"sm_kdiag{e}", [P, P]) for e in range(2)]
        diag = [tile(nc, c, f"sm_diag{e}", [P, P]) for e in range(2)]
        same = [[tile(nc, c, f"sm_same{a}{b}", [P, P]) for b in range(2)] for a in range(2)]
        tmp = tile(nc, c, "sm_tmp", [P, 2, P])
        rb = [bank(nc, c, f"sm_rb{e}", [P, P]) for e in range(2)]
        own, diags, rows, scaled, done = (net.sem("sm_" + n) for n in ("own", "diags", "rows", "scaled", "done"))
        block = c.enter_context(nc.Block())
        ends_of = (slice(0, 1), slice(T - 1, T))

        @block.vector
        def _(dve):
            st = Steps(dve, own)
            st.did(dve.tensor_scalar(keep_f[:], o.cont[:], -1.0, BIG, ALU.add, ALU.mult))
            st.did(dve.memset(keep_b[:, T - 1:T], -BIG))
            st.did(dve.tensor_copy(keep_b[:, 0:T - 1], keep_f[:, 1:T]))
            for e, m in enumerate((lead, tail)):
                st.did(dve.tensor_scalar(m[:], o.key[:], o.key[:, ends_of[e]], None, ALU.is_equal))
                st.did(dve.tensor_scalar(m[:], m[:], -1.0, BIG, ALU.add, ALU.mult))
            for h in range(HEADS):
                s = at_edges.score[:, h, :]
                st.did(dve.tensor_tensor_scan(out=fwd[:], data0=keep_f[:], data1=s, initial=-BIG, op0=ALU.add, op1=ALU.max))
                st.did(dve.tensor_tensor_scan(out=bwd[:, ::-1], data0=keep_b[:, ::-1], data1=s[:, ::-1],
                                              initial=-BIG, op0=ALU.add, op1=ALU.max))
                dve.tensor_copy(ends[:, 0, h:h + 1], bwd[:, 0:1])
                dve.tensor_copy(ends[:, 1, h:h + 1], fwd[:, T - 1:T])
                st.did(dve.tensor_tensor(most[:, h, :], fwd[:], bwd[:], ALU.max))
            for e in range(2):
                dve.tensor_scalar(key_diag[e][:], net.ident[:], o.key[:, ends_of[e]], None, ALU.mult).then_inc(diags, 1)
            dve.wait_ge(rows, 1)
            for a in range(2):
                for b in range(2):
                    st.did(dve.tensor_scalar(same[a][b][:], rb[b][:], o.key[:, ends_of[a]], None, ALU.is_equal))
                    st.did(dve.tensor_scalar(same[a][b][:], same[a][b][:], -1.0, BIG, ALU.add, ALU.mult))
            for h in range(HEADS):
                for e in range(2):
                    dve.tensor_scalar(diag[e][:], net.ident[:], ends[:, e, h:h + 1], None, ALU.mult).then_inc(diags, 1)
                dve.wait_ge(rows, h + 2)
                for a in range(2):
                    for b in range(2):
                        ins = dve.tensor_tensor(tmp[:, b, :], same[a][b][:], rb[b][:], ALU.add)
                    st.did(ins)
                    st.did(dve.tensor_reduce(total[:, a, h:h + 1], tmp[:], AX.XY, ALU.max))
            for h in range(HEADS):
                m = most[:, h, :]
                st.did(dve.scalar_tensor_tensor(out=m, in0=lead[:], scalar=total[:, 0, h:h + 1], in1=m, op0=ALU.add, op1=ALU.max))
                st.did(dve.scalar_tensor_tensor(out=m, in0=tail[:], scalar=total[:, 1, h:h + 1], in1=m, op0=ALU.add, op1=ALU.max))
                dve.tensor_tensor(at_edges.score[:, h, :], at_edges.score[:, h, :], m, ALU.subtract).then_inc(scaled, 1)

        @block.tensor
        def _(pe):
            for n, two in enumerate([key_diag] + [diag] * HEADS):
                pe.wait_ge(diags, 2 * n + 2)
                for e in range(2):
                    last = pe.matmul(rb[e][:], net.ones[:], two[e][:], start=True, stop=True)
                last.then_inc(rows, 1)

        @block.scalar
        def _(act):
            for h in range(HEADS):
                act.wait_ge(scaled, h + 1)
                act.activation(at_edges.score[:, h, :], at_edges.score[:, h, :], ACT.Exp, scale=float(D) ** -0.5).then_inc(done, 1)


def attend_phase(net, o, mask, at_edges):
    nc = net.nc
    with net.phase() as c:
        node = [tile(nc, c, f"at_node{j}", [P, CH], I32) for j in range(2)]
        msg = tile(nc, c, "at_msg", [P, QW, CH])
        sums = [tile(nc, c, f"at_sums{j}", [P, QW, CH]) for j in range(2)]
        rows = [tile(nc, c, f"at_rows{j}", [P, CH, QW]) for j in range(2)]
        own, started = net.sem("at_own"), net.sem("at_started")
        sem2 = lambda n: [net.sem(f"at_{n}{j}") for j in range(2)]
        summed, rowed, sent = (sem2(n) for n in ("summed", "rowed", "sent"))
        fix = Fix(net, c, "at", QW)
        block = c.enter_context(nc.Block())

        @block.vector
        def _(dve):
            st = Steps(dve, own)
            fix.blank(dve)
            st.did(dve.memset(sums[1][:, :, CH - 1:CH], 0.0))
            with dve.Fori(0, NPAIR) as i:
                st.enter(i, 2 * (2 + scan_steps(QW)))
                for j in range(2):
                    at = bass.ds(chunk(i, j), CH)
                    e = at_edges.score[:, :, at]
                    dve.tensor_tensor(msg[:, 0:D, :].rearrange("p (h d) t -> p h t d", h=HEADS),
                                      at_edges.v[:, at, :].rearrange("p t (h d) -> p h t d", h=HEADS),
                                      spread(e, 3, HD), ALU.mult)
                    st.did(dve.tensor_copy(msg[:, D:QW, :], e))
                    dve.wait_ge(rowed[j], i)
                    scan_chunk(dve, st, o, mask, msg, sums[j], sums[1 - j], i, j)
                    dve.wait_ge(sent[j], i * (CH * 16))
                    st.did(dve.tensor_copy(node[j][:], o.to_node[:, at]))
                    dve.sem_inc(summed[j], 1)
                st.leave(NPAIR)
            fix.vector(dve, 0)

        @block.scalar
        def _(act):
            with act.Fori(0, NPAIR) as i:
                for j in range(2):
                    act.wait_ge(summed[j], i + 1)
                    act.activation(rows[j][:], sums[j][:].rearrange("p f t -> p t f"), ACT.Copy).then_inc(rowed[j], 1)

        @block.gpsimd
        def _(pool):
            with pool.Fori(0, NPAIR) as i:
                for j in range(2):
                    pool.wait_ge(rowed[j], i + 1)
                    pool.sem_inc(started, 1)
                    for r in range(CH):
                        pool.indirect_dma_start(
                            out=net.att[:, :], out_offset=bass.IndirectOffsetOnAxis(ap=node[j][:, r:r + 1], axis=0),
                            in_=rows[j][:, r, :], in_offset=None,
                            bounds_check=NR - 1, oob_is_err=False).then_inc(sent[j], 16)
            for j in range(2):
                pool.wait_ge(sent[j], NPAIR * CH * 16)
            fix.gpsimd(pool, 0, net.att[:, :], o.fix_node[:], NR - 1)

        @block.tensor
        def _(pe):
            pe.wait_ge(summed[1], NPAIR)
            fix.tensor(pe, 0, o, sums[1][:, :, CH - 1])



class ChunkOf4:

    def __init__(self, i, k):
        self.number, self.slot, self.turn = i * 4 + k, k % 4, i + k // 4
        self.first = isinstance(i, int) and self.turn == 0
        self.nodes = bass.ds(self.number * G, G)

    def before(self, n):
        return not isinstance(self.number, int) or self.number >= n


CHUNKS = NPP // G
CHUNKS_FULL = PAIRS_FULL * 2
CIN = D + ED


def last_phase(net, w, out):
    nc = net.nc
    assert CHUNKS_FULL % 4 == 2 and CHUNKS % 4 == 2
    with net.phase() as c:
        t4 = lambda n, shape: [tile(nc, c, f"la_{n}{k}", shape) for k in range(4)]
        x2, at, es, y, comb, o = (t4("x2", [P, G, D]), t4("at", [P, G, QW]), t4("es", [P, G, ED]),
                                  t4("y", [P, G, D]), t4("comb", [P, G, CIN]), t4("o", [P, G, D]))
        yT, hT, cT = tile(nc, c, "la_yT", [P, 4 * P]), tile(nc, c, "la_hT", [P, 4, 4 * P]), tile(nc, c, "la_cT", [CIN, 2, 4 * P])
        h1, h2 = tile(nc, c, "la_h1", [HID, 2, 4 * P]), tile(nc, c, "la_h2", [HID, 2, 4 * P])
        u = tile(nc, c, "la_u", [P, G, D])
        vec = {n: tile(nc, c, "la_" + n, [P, D]) for n in ("g2", "be2", "mb3")}
        w1 = tile(nc, c, "la_w1", [P, FFN])
        w2 = tile(nc, c, "la_w2", [P, 2, D])
        g1, be1, b2 = (tile(nc, c, "la_" + n, [P, 1]) for n in ("g1", "be1", "b2"))
        shift = tile(nc, c, "la_shift", [P, 1])
        fb1, hidden_bias = tile(nc, c, "la_fb1", [P, 2]), tile(nc, c, "la_hidden_bias", [P, 2])
        mw1, mu, u0 = tile(nc, c, "la_mw1", [CIN, HID]), tile(nc, c, "la_mu", [UD, HID]), tile(nc, c, "la_graph0", [UD, 1])
        mw2, mw3 = tile(nc, c, "la_mw2", [HID, HID]), tile(nc, c, "la_mw3", [HID, D])
        mb1, mb2, mc1 = (tile(nc, c, "la_" + n, [HID, 1]) for n in ("mb1", "mb2", "mc1"))
        eps = tile(nc, c, "la_eps", [P, 1])
        norms = {n: (tile(nc, c, f"la_sum{n}", [P, G]), tile(nc, c, f"la_var{n}", [P, G]), tile(nc, c, f"la_square{n}", [P, G, D]))
                 for n in ("first", "ffn", "model")}
        tb = [bank(nc, c, f"la_tb{k}", [P, 4 * P]) for k in range(2)]
        fbank = [bank(nc, c, f"la_fbank{k}", [P, 4 * P]) for k in range(2)]
        mbank = [bank(nc, c, f"la_mbank{k}", [P, 4 * P]) for k in range(2)]
        ffn_out, model_out = bank(nc, c, "la_ffn_out", [P, G, D]), bank(nc, c, "la_model_out", [P, G, D])
        (own, pool_own, weights, eps_ready, early, early_out, den_ready, z_ready, y_ready, y_turned, yT_ready,
         f_ready, f_used, ffn_ready, ffn_used, x2_used, comb_ready, comb_turned, cT_ready, m_ready, m_used, model_ready,
         model_used, made) = (net.sem("la_" + n) for n in (
             "own", "pool_own", "weights", "eps_ready", "early", "early_out", "den_ready", "z_ready", "y_ready",
             "y_turned", "yT_ready", "f_ready", "f_used", "ffn_ready", "ffn_used", "x2_used", "comb_ready",
             "comb_turned", "cT_ready", "m_ready", "m_used", "model_ready", "model_used", "made"))
        centred, squared = ({n: net.sem(f"la_{what}_{n}") for n in ("first", "model")} for what in ("centred", "squared"))
        summed, rooted = ({n: net.sem(f"la_{what}_{n}") for n in norms} for what in ("summed", "rooted"))
        loaded = [net.sem(f"la_loaded{k}") for k in range(4)]
        stored = [net.sem(f"la_stored{k}") for k in range(4)]
        block = c.enter_context(nc.Block())
        x2_rows, at_rows, agg_rows, outs = node_view(net.x2, D), node_view(net.att, QW), node_view(net.agg, AW), RealRows(out)
        LOADS = []

        def steps(eng, step, enter=lambda i, a: None, leave=lambda turns: None):
            for k in range(4):
                step(0, k, True)
            split, last = CHUNKS_FULL // 4 + 1, (CHUNKS + 2) // 4 - 2
            for a, b, full in ((1, split, True), (split, last, False)):
                with eng.Fori(a, b) as i:
                    enter(i, a)
                    for k in range(4):
                        step(i, k, full)
                    leave(b - a)
            for n in range(8):
                step(last + n // 4, n % 4, False)

        def exists(chunk):
            return not isinstance(chunk.number, int) or 0 <= chunk.number < CHUNKS

        def stores_done(chunk, full):
            if full:
                return chunk.turn * 48
            return chunk.turn * 32 + 16 * ((CHUNKS_FULL - chunk.slot + 3) // 4)

        @block.sync
        def _(sp):
            def load(to, of):
                LOADS.append(16)
                sp.dma_start(to, of).then_inc(weights, 16)

            column = lambda ap, k=1: ap.rearrange("(k p) -> p k", k=k)
            for h in range(2):
                half = slice(h * D, (h + 1) * D)
                load(w1[half, :], w["L2_gnn_w1"])
                with nc.allow_non_contiguous_dma(reason="columns of factors and biases"):
                    load(g1[half, :], column(w["L2_gnn_ln1_g"]))
                    load(be1[half, :], column(w["L2_gnn_ln1_b"]))
                    load(b2[half, :], column(w["L2_gnn_b2"]))
            load(w2[:], w["L2_gnn_w2"].rearrange("(k p) n -> p k n", p=P))
            load(mw1[:], w["L3_gnn_W1"][0:CIN, :])
            load(mu[:], w["L3_gnn_W1"][CIN:CIN + UD, :])
            load(mw2[:], w["L3_gnn_W2"])
            load(mw3[:], w["L3_gnn_W3"])
            with nc.allow_non_contiguous_dma(reason="columns of biases"):
                load(fb1[:], column(w["L2_gnn_b1"], 2))
                load(u0[:], column(w["L3_gnn_u"][0, :]))
                load(mb1[:], column(w["L3_gnn_b1"]))
                load(mb2[:], column(w["L3_gnn_b2"]))
            for n, name in (("g2", "L2_gnn_ln2_g"), ("be2", "L2_gnn_ln2_b"), ("mb3", "L3_gnn_b3")):
                load(vec[n][:], w[name].partition_broadcast(P))

            def inputs(a):
                if not exists(a):
                    return
                if not a.first:
                    sp.wait_ge(x2_used, a.number - 3)
                for to, of in ((x2, x2_rows[:, a.nodes, :]), (at, at_rows[:, a.nodes, :]), (es, agg_rows[:, a.nodes, D:AW])):
                    sp.dma_start(to[a.slot][:], of).then_inc(loaded[a.slot], 16)

            def store(a, full):
                if exists(a):
                    sp.wait_ge(made, a.number + 1)
                    outs.move(sp, stored[a.slot], o[a.slot], a.nodes, full, True)

            def step(i, k, full):
                inputs(ChunkOf4(i, k + 3))
                store(ChunkOf4(i, k - 2), full)

            for k in range(3):
                inputs(ChunkOf4(0, k))
            steps(sp, step)
            for k in range(4):
                uses = (CHUNKS - k + 3) // 4
                sp.wait_ge(stored[k], uses * 32 + 16 * ((CHUNKS_FULL - k + 3) // 4))

        @block.gpsimd
        def _(pool):
            st = Steps(pool, pool_own)
            pool.wait_ge(weights, sum(LOADS))

            def prepare(a):
                if not exists(a):
                    return
                k = a.slot
                pool.wait_ge(den_ready, a.number + 1)
                if not a.first:
                    pool.wait_ge(y_turned, a.number - 3)
                    pool.wait_ge(model_used, a.number - 3)
                st.did(pool.tensor_tensor(y[k][:].rearrange("p g (h d) -> p g h d", h=HEADS),
                                          at[k][:, :, 0:D].rearrange("p g (h d) -> p g h d", h=HEADS),
                                          spread(at[k][:, :, D:QW], 3, HD), ALU.mult))
                st.did(pool.tensor_tensor(y[k][:], y[k][:], x2[k][:], ALU.add))
                pool.tensor_tensor(x2[k][:], x2[k][:], spread(vec["be2"][:], 1, G), ALU.add)
                pool.tensor_tensor(comb[k][:, :, D:CIN], es[k][:], spread(net.inv_count[:, a.nodes], 2, ED), ALU.mult).then_inc(z_ready, 1)

            for k in range(2):
                prepare(ChunkOf4(0, k))
            steps(pool, lambda i, k, full: prepare(ChunkOf4(i, k + 2)), lambda i, a: st.enter(i - a, 4 * 2), st.leave)

        @block.tensor
        def _(pe):
            pe.wait_ge(weights, sum(LOADS))
            pe.matmul(fbank[0][:, 0:1], mu[:], u0[:], start=True, stop=True)
            for m in range(2):
                last = pe.matmul(fbank[0][:, m + 1:m + 2], w1[0:D, m * P:(m + 1) * P], b2[0:D, :], start=True, stop=True)
            last.then_inc(early, 1)
            pe.wait_ge(early_out, 1)

            def model_end(a):
                if not exists(a):
                    return
                pe.wait_ge(m_used, a.number * 4 + 4)
                if a.before(1):
                    pe.wait_ge(model_used, a.number)
                for g in range(G):
                    last = pe.matmul(model_out[:, g, :], h2[:, g // 4, (g % 4) * P:(g % 4 + 1) * P], mw3[:], start=True, stop=True)
                last.then_inc(model_ready, 1)

            def ffn_turn(a):
                if not exists(a):
                    return
                pe.wait_ge(y_ready, a.number + 1)
                if a.before(2):
                    pe.wait_ge(cT_ready, a.number * 2 - 2)
                for q in range(4):
                    last = pe.transpose(tb[0][:, q * P:(q + 1) * P], y[a.slot][:, 2 * q:2 * q + 2, :].rearrange("p g f -> p (g f)"), net.ident[:])
                last.then_inc(y_turned, 1)

            def ffn(a):
                if not exists(a):
                    return
                pe.wait_ge(yT_ready, a.number + 1)
                for n in range(4):
                    h, m = n // 2, n % 2
                    if n >= 2 or a.before(1):
                        pe.wait_ge(f_used, a.number * 4 + n - 1)
                    pe.matmul(fbank[n % 2][:], w1[h * D:(h + 1) * D, m * P:(m + 1) * P],
                              yT[h * D:(h + 1) * D, :], start=True, stop=True).then_inc(f_ready, 1)
                if a.before(1):
                    pe.wait_ge(ffn_used, a.number)
                for q in range(4):
                    pe.matmul(ffn_out[:, 2 * q:2 * q + 2, :], yT[:, q * P:(q + 1) * P], net.ident[:],
                              start=True, stop=False, skip_group_check=True)
                    if q == 0:
                        pe.wait_ge(f_used, a.number * 4 + 4)
                    for h in range(2):
                        for m in range(2):
                            last = pe.matmul(ffn_out[:, 2 * q + h, :], hT[:, 2 * h + m, q * P:(q + 1) * P], w2[:, m, :],
                                             start=False, stop=(m == 1), skip_group_check=True)
                last.then_inc(ffn_ready, 1)

            def model(a):
                if not exists(a):
                    return
                pe.wait_ge(comb_ready, a.number + 1)
                if a.before(1):
                    pe.wait_ge(cT_ready, a.number * 2)
                for g in range(G):
                    last = pe.transpose(tb[g // 4][0:CIN, (g % 4) * P:(g % 4 + 1) * P], comb[a.slot][:, g, :], net.ident[:])
                    if g % 4 == 3:
                        last.then_inc(comb_turned, 1)
                for k in range(2):
                    pe.wait_ge(cT_ready, a.number * 2 + k + 1)
                    if a.before(1):
                        pe.wait_ge(m_used, a.number * 4 + k - 1)
                    pe.matmul(mbank[k][:], mw1[:], cT[:, k, :], start=True, stop=True).then_inc(m_ready, 1)
                for k in range(2):
                    pe.wait_ge(m_used, a.number * 4 + k + 1)
                    pe.matmul(mbank[k][:], mw2[:], h1[:, k, :], start=True, stop=True).then_inc(m_ready, 1)

            def step(i, k, full):
                ffn_turn(ChunkOf4(i, k))
                model_end(ChunkOf4(i, k - 2))
                ffn(ChunkOf4(i, k))
                model(ChunkOf4(i, k - 1))

            steps(pe, step)

        @block.scalar
        def _(act):
            act.wait_ge(weights, sum(LOADS))
            act.wait_ge(early, 1)
            act.wait_ge(eps_ready, 2)
            act.activation(mc1[:], fbank[0][:, 0:1], ACT.Identity, bias=mb1[:, 0:1])
            for m in range(2):
                last = act.activation(hidden_bias[:, m:m + 1], fbank[0][:, m + 1:m + 2], ACT.Identity,
                                      bias=fb1[:, m:m + 1], scale=-1.0)
            last.then_inc(early_out, 1)
            act.wait_ge(early_out, 1)

            def root(which, a):
                act.wait_ge(summed[which], a)
                var = norms[which][1]
                act.activation(var[:], var[:], ACT.Sqrt, bias=eps[:, 0:1], scale=1.0 / D).then_inc(rooted[which], 1)

            def square(which, x, a):
                act.wait_ge(centred[which], a)
                act.activation(norms[which][2][:], x, ACT.Square).then_inc(squared[which], 1)

            def step(i, k, full):
                ffn_c, after, model_c, end, first = (ChunkOf4(i, k), ChunkOf4(i, k - 1), ChunkOf4(i, k - 1),
                                                     ChunkOf4(i, k - 2), ChunkOf4(i, k + 1))

                def hidden(n):
                    if exists(ffn_c):
                        act.wait_ge(f_ready, ffn_c.number * 4 + n + 1)
                        act.activation(hT[:, n, :], fbank[n % 2][:], ACT.Relu, bias=hidden_bias[:, n % 2:n % 2 + 1]).then_inc(f_used, 1)

                def model_unit(n, to, bias):
                    act.wait_ge(m_ready, model_c.number * 4 + n + 1)
                    act.activation(to[:, n % 2, :], mbank[n % 2][:], ACT.Relu, bias=bias[:, 0:1]).then_inc(m_used, 1)

                if exists(ffn_c):
                    act.wait_ge(y_turned, ffn_c.number + 1)
                    if ffn_c.before(1):
                        act.wait_ge(ffn_ready, ffn_c.number)
                    act.activation(yT[:], tb[0][:], ACT.Identity, bias=shift[:, 0:1], scale=g1[:, 0:1]).then_inc(yT_ready, 1)
                if exists(after):
                    root("ffn", after.number * 2 + 1)
                for n in range(3):
                    hidden(n)
                if exists(after):
                    root("ffn", after.number * 2 + 2)
                hidden(3)
                if exists(end):
                    square("model", o[end.slot][:], end.number + 1)
                if exists(first):
                    square("first", y[first.slot][:], first.number + 1)
                for k in range(2):
                    if exists(model_c):
                        act.wait_ge(comb_turned, model_c.number * 2 + k + 1)
                        act.activation(cT[:, k, :], tb[k][0:CIN, :], ACT.Copy).then_inc(cT_ready, 1)
                    if k == 0 and exists(end):
                        root("model", end.number + 1)
                    if k == 0 and exists(first):
                        root("first", first.number + 1)
                if exists(model_c):
                    for n in range(2):
                        model_unit(n, h1, mc1)
                    if model_c.before(1):
                        act.wait_ge(model_ready, model_c.number)
                    for n in range(2, 4):
                        model_unit(n, h2, mb2)

            square("first", y[0][:], 1)
            root("first", 1)
            steps(act, step)

        @block.vector
        def _(dve):
            st = Steps(dve, own)
            dve.wait_ge(weights, sum(LOADS))
            dve.memset(eps[:], EPS).then_inc(eps_ready, 1)
            dve.tensor_tensor(shift[:], be1[:], b2[:], ALU.add).then_inc(eps_ready, 1)

            def invert(a):
                if not exists(a):
                    return
                k = a.slot
                dve.wait_ge(loaded[k], a.turn * 48 + 48)
                st.did(dve.tensor_scalar(at[k][:, :, D:QW], at[k][:, :, D:QW], 1e-30, None, ALU.max))
                dve.reciprocal(at[k][:, :, D:QW], at[k][:, :, D:QW]).then_inc(den_ready, 1)

            def after_ffn(a):
                if not exists(a):
                    return
                total, var, square = norms["ffn"]

                def norm(of, to, n):
                    st.did(dve.tensor_reduce(total[:], of, AX.X, ALU.add))
                    st.did(dve.scalar_tensor_tensor(out=u[:], in0=spread(total[:], 2, D), scalar=-1.0 / D, in1=of,
                                                    op0=ALU.mult, op1=ALU.add))
                    if n == 1:
                        dve.sem_inc(ffn_used, 1)
                    st.did(dve.tensor_tensor(square[:], u[:], u[:], ALU.mult))
                    dve.tensor_reduce(var[:], square[:], AX.X, ALU.add).then_inc(summed["ffn"], 1)
                    dve.wait_ge(rooted["ffn"], a.number * 2 + n)
                    st.did(dve.reciprocal(var[:], var[:]))
                    st.did(dve.tensor_tensor(to, u[:], spread(var[:], 2, D), ALU.mult))

                dve.wait_ge(ffn_ready, a.number + 1)
                norm(ffn_out[:], u[:], 1)
                st.did(dve.tensor_tensor(u[:], u[:], spread(vec["g2"][:], 1, G), ALU.mult))
                st.did(dve.tensor_tensor(u[:], u[:], x2[a.slot][:], ALU.add))
                dve.sem_inc(x2_used, 1)
                norm(u[:], comb[a.slot][:, :, 0:D], 2)
                dve.sem_inc(comb_ready, 1)

            def norms_beside(end, first, full):
                total = {n: norms[n][0] for n in centred}
                both = []
                if exists(end):
                    k = end.slot
                    dve.wait_ge(model_ready, end.number + 1)
                    if not end.first:
                        dve.wait_ge(stored[k], stores_done(end, full))
                    st.did(dve.tensor_tensor(o[k][:], model_out[:], comb[k][:, :, 0:D], ALU.add))
                    dve.sem_inc(model_used, 1)
                    st.did(dve.tensor_tensor(o[k][:], o[k][:], spread(vec["mb3"][:], 1, G), ALU.add))
                    both.append(("model", o[k][:], end.number, made))
                if exists(first):
                    dve.wait_ge(z_ready, first.number + 1)
                    both.append(("first", y[first.slot][:], first.number, y_ready))
                marks = {}
                for n, x, _, _ in both:
                    marks[n] = st.mark(dve.tensor_reduce(total[n][:], x, AX.X, ALU.add))
                for n, x, _, _ in both:
                    st.upto(marks[n])
                    dve.scalar_tensor_tensor(out=x, in0=spread(total[n][:], 2, D), scalar=-1.0 / D, in1=x,
                                             op0=ALU.mult, op1=ALU.add).then_inc(centred[n], 1)
                for n, x, number, _ in both:
                    dve.wait_ge(squared[n], number + 1)
                    dve.tensor_reduce(norms[n][1][:], norms[n][2][:], AX.X, ALU.add).then_inc(summed[n], 1)
                for n, x, number, _ in both:
                    dve.wait_ge(rooted[n], number + 1)
                    marks[n] = st.mark(dve.reciprocal(norms[n][1][:], norms[n][1][:]))
                for n, x, number, ready in both:
                    st.upto(marks[n])
                    dve.tensor_tensor(x, x, spread(norms[n][1][:], 2, D), ALU.mult).then_inc(ready, 1)

            def step(i, k, full):
                invert(ChunkOf4(i, k + 2))
                after_ffn(ChunkOf4(i, k - 1))
                norms_beside(ChunkOf4(i, k - 2), ChunkOf4(i, k + 1), full)

            for k in range(2):
                invert(ChunkOf4(0, k))
            norms_beside(ChunkOf4(0, -1), ChunkOf4(0, 0), True)
            steps(dve, step, lambda i, a: st.enter(i - a, 4 * 19), st.leave)


def tables(net):
    net.records = net.dram("records", [EP, 4], I32)
    net.half_sorted = net.dram("half_sorted", [EP, 4], I32)
    net.orders = [net.dram(n, [EP + 2, 4], I32) for n in ("dst_records", "src_records")]
    net.by_dst, net.by_src = net.dram("by_dst", [NR, 2]), net.dram("by_src", [NR, 2])
    net.pairs = net.dram("pairs", [NR, 2])
    net.x_rows = net.dram("x_rows", [NR, XW])
    net.x1_rows = net.dram("x1_rows", [NR, XW])
    net.x2 = net.dram("x2", [NR, D])
    net.x_edges = net.dram("x_edges", [EP, D])
    net.slots = [net.dram(f"slots{k}", [TR, D]) for k in range(2)]
    net.slot_index = net.dram("slot_index", [P, T], I32)
    net.node_r = net.dram("node_r", [NR, D])
    net.agg = net.dram("agg", [NR, AW])
    net.att = net.dram("att", [NR, QW])


class Coefficients:

    def __init__(self, net, c):
        self.weight, self.src_part, self.dst_part, self.alpha = (
            tile(net.nc, c, "co_" + n, [P, T]) for n in ("weight", "src_part", "dst_part", "alpha"))
        self.mask = tile(net.nc, c, "co_mask", [P, 2 * NPAIR, MW * CH], BF16)


def gnn_kernel(nc, w, out, kinds=None):
    with ExitStack() as c:
        net = Net(nc, c)
        net.kinds = kinds or {}
        tables(net)
        constants(net, c)
        net.inv_deg, net.inv_count = tile(nc, c, "inv_deg", [P, NPP]), tile(nc, c, "inv_count", [P, NPP])
        by_source = Order(net, c, "os", net.orders[1], 0)

        with ExitStack() as c1:
            net.own_k = tile(nc, c1, "own_k", [P, NPP])
            by_dest = Order(net, c1, "od", net.orders[0], 1)
            with ExitStack() as c2:
                net.zeros = tile(nc, c2, "zeros", [P, ZW])
                setup_phase(net, w["src"], w["dst"], w["edge_weight"])
                zero = zero_parts(net)
                for n, (name, table, key) in enumerate((("sd", net.orders[0], 1), ("ss", net.orders[1], 0))):
                    sort_pass(net, name + "l", net.records, net.half_sorted, key, False, zero[2 * n::4])
                    sort_pass(net, name + "h", net.half_sorted, table, key, True, zero[2 * n + 1::4])
                order_phase(net, by_source, net.by_src, "count")
                order_phase(net, by_dest, net.by_dst, "slot")
            with ExitStack() as c2:
                net.inv_out, net.inv_in, net.own_part, net.slot1 = (
                    tile(nc, c2, n, [P, NPP]) for n in ("inv_out", "inv_in", "own_part", "slot1"))
                node_scalars_phase(net)
                x_rows_phase(net, w["x"])
            with ExitStack() as c2:
                co = Coefficients(net, c2)
                mask_phase(net, by_dest, co.mask)
                appnp_first_phase(net, by_dest, co)
                appnp_steps_phase(net, by_dest, co)
            to_nodes_phase(net, by_dest)
            x1_phase(net, w["x"])

        mask = tile(nc, c, "src_mask", [P, 2 * NPAIR, MW * CH], BF16)
        mask_phase(net, by_source, mask)
        gcn_edges_phase(net, by_source, mask, w["edge_attr_48"])
        x2_phase(net, w["L1_gnn_weight"], w["L1_gnn_bias"])

        with ExitStack() as c3:
            at_edges = AtEdges(net, c3)
            scores_phase(net, by_source, at_edges, w["L2_gnn_attn_w"], w["L2_gnn_attn_b"])
            softmax_phase(net, by_source, at_edges)
            attend_phase(net, by_source, mask, at_edges)

        last_phase(net, w, out)


INS = ["x", "src", "dst", "edge_attr_48", "edge_weight", "L1_gnn_weight", "L1_gnn_bias",
       "L2_gnn_attn_w", "L2_gnn_attn_b", "L2_gnn_w1", "L2_gnn_b1", "L2_gnn_w2", "L2_gnn_b2",
       "L2_gnn_ln1_g", "L2_gnn_ln1_b", "L2_gnn_ln2_g", "L2_gnn_ln2_b",
       "L3_gnn_u", "L3_gnn_W1", "L3_gnn_b1", "L3_gnn_W2", "L3_gnn_b2", "L3_gnn_W3", "L3_gnn_b3"]


def kernel(**inputs):
    import numpy as np
    import concourse.bacc as bacc
    from concourse.bass_utils import run_bass_kernel_spmd

    nc = bacc.Bacc("TRN2", target_bir_lowering=False, num_devices=1)
    arrays, w = {}, {}
    for name in INS:
        a = np.ascontiguousarray(inputs[name])
        arrays[f"in_{name}_dram"] = a
        w[name] = nc.dram_tensor(f"in_{name}_dram", a.shape, mybir.dt.from_np(a.dtype), kind="ExternalInput").ap()
    out = nc.dram_tensor("out_0_dram", (N, D), F32, kind="ExternalOutput").ap()
    gnn_kernel(nc, w, out)
    r = run_bass_kernel_spmd(nc, [arrays], core_ids=[0])
    return r.results[0]["out_0_dram"]
```
